# Optimizing a Trainium2 kernel written in Bass

```python
import numpy as np
import jax
import jax.numpy as jnp

def _softmax(x, axis=-1):
    return jax.nn.softmax(x, axis=axis)

def _gelu(x):
    return jax.nn.gelu(x, approximate=True)

def _silu(x):
    return jax.nn.silu(x)

def _sigmoid(x):
    return jax.nn.sigmoid(x)

def _layernorm(x, axis=-1, eps=1e-05):
    m = jnp.mean(x, axis=axis, keepdims=True)
    v = jnp.var(x, axis=axis, keepdims=True)
    return (x - m) / jnp.sqrt(v + eps)

def _scatter_add(tgt, idx, src, axis=0):
    return tgt.at[idx].add(src)

def _segment_sum(src, seg, n):
    return jax.ops.segment_sum(src, seg, n)
kernel_name = 'mk_vit_tower_postln_d2_tok_img1024_r4_5e80a2'

def setup_inputs(seed: int=0):
    np.random.seed(seed)
    _w = jnp.asarray

    def _rec_inputs():
        import jax
        import jax.numpy as jnp
        _rk = jax.random.key(seed)
        x = -0.00016672 + 0.999947 * jax.random.normal(jax.random.fold_in(_rk, 1), (64, 3, 96, 96), jnp.float32)
        return x
    x = _rec_inputs()

    def _L0_tok_setup():
        import jax, jax.numpy as jnp
        import numpy as np
        IMG = 96
        PATCH = 16
        C_IN = 3
        EMBED = 256
        NPH = IMG // PATCH
        NUM_PATCHES = NPH * NPH
        PATCH_DIM = PATCH * PATCH * C_IN
        key = jax.random.key(seed)
        k_x, k_w, k_b, k_cls, k_pos = jax.random.split(key, 5)
        x = jax.random.normal(k_x, (64, C_IN, IMG, IMG), dtype=jnp.float32)
        W = jax.random.normal(k_w, (EMBED, PATCH_DIM), dtype=jnp.float32) * (1.0 / np.sqrt(PATCH_DIM))
        b = jax.random.normal(k_b, (EMBED,), dtype=jnp.float32) * 0.01
        cls_token = jax.random.normal(k_cls, (1, 1, EMBED), dtype=jnp.float32) * 0.02
        pos_embed = jax.random.normal(k_pos, (1, NUM_PATCHES + 1, EMBED), dtype=jnp.float32) * 0.02
        return {'x': x, 'W': W, 'b': b, 'cls_token': cls_token, 'pos_embed': pos_embed}
    _L0_tok_all = _L0_tok_setup()
    _L0_tok_in = {k: v for k, v in _L0_tok_all.items() if k in ('W', 'b', 'cls_token', 'pos_embed')}
    del _L0_tok_all

    def _L0_attn_setup():
        import jax, jax.numpy as jnp
        import numpy as np
        EMBED_DIM = 256
        NUM_HEADS = 16
        HEAD_DIM = EMBED_DIM // NUM_HEADS
        WINDOW_SIZE = 32
        HALF_BAND = 2 * WINDOW_SIZE
        BAND = 2 * HALF_BAND + 1
        key = jax.random.key(seed)
        ks = jax.random.split(key, 9)
        B, T, E = (1, 256, EMBED_DIM)
        scale = 0.02
        return {'hidden_states': jax.random.normal(ks[0], (B, T, E), jnp.float32), 'Wq': jax.random.normal(ks[1], (E, E), jnp.float32) * scale, 'bq': jax.random.normal(ks[2], (E,), jnp.float32) * scale, 'Wk': jax.random.normal(ks[3], (E, E), jnp.float32) * scale, 'bk': jax.random.normal(ks[4], (E,), jnp.float32) * scale, 'Wv': jax.random.normal(ks[5], (E, E), jnp.float32) * scale, 'bv': jax.random.normal(ks[6], (E,), jnp.float32) * scale, 'Wo': jax.random.normal(ks[7], (E, E), jnp.float32) * scale, 'bo': jax.random.normal(ks[8], (E,), jnp.float32) * scale}
    _L0_attn_all = _L0_attn_setup()
    _L0_attn_in = {k: v for k, v in _L0_attn_all.items() if k in ('Wq', 'bq', 'Wk', 'bk', 'Wv', 'bv', 'Wo', 'bo')}
    del _L0_attn_all

    def _L0_ffn_setup():
        import jax, jax.numpy as jnp
        import numpy as np
        B, S, H, I, E_ROUTED, TOP_K = (8, 512, 256, 512, 8, 2)

        def _expert(x, Wg, Wu, Wd):
            return jax.nn.silu(x @ Wg.T) * (x @ Wu.T) @ Wd.T
        key = jax.random.key(seed)
        ks = jax.random.split(key, 9)
        s = 0.02
        return {'x': jax.random.normal(ks[0], (B, S, H), dtype=jnp.float32), 'Wg_s': jax.random.normal(ks[1], (I, H), dtype=jnp.float32) * s, 'Wu_s': jax.random.normal(ks[2], (I, H), dtype=jnp.float32) * s, 'Wd_s': jax.random.normal(ks[3], (H, I), dtype=jnp.float32) * s, 'Wg': jax.random.normal(ks[4], (E_ROUTED, I, H), dtype=jnp.float32) * s, 'Wu': jax.random.normal(ks[5], (E_ROUTED, I, H), dtype=jnp.float32) * s, 'Wd': jax.random.normal(ks[6], (E_ROUTED, H, I), dtype=jnp.float32) * s, 'Wr': jax.random.normal(ks[7], (E_ROUTED, H), dtype=jnp.float32) * s, 'rb': jnp.zeros((E_ROUTED,), dtype=jnp.float32)}
    _L0_ffn_all = _L0_ffn_setup()
    _L0_ffn_in = {k: v for k, v in _L0_ffn_all.items() if k in ('Wg_s', 'Wu_s', 'Wd_s', 'Wg', 'Wu', 'Wd', 'Wr', 'rb')}
    del _L0_ffn_all

    def _L1_attn_setup():
        import jax, jax.numpy as jnp
        import numpy as np
        import math
        D_MODEL, N_HEADS, D_K, D_C, D_HR = (256, 8, 128, 32, 32)
        B, S = (4, 512)
        key = jax.random.key(seed)
        ks = jax.random.split(key, 17)

        def lin(k, fan_in, fan_out):
            lim = 1.0 / math.sqrt(fan_in)
            kw, kb = jax.random.split(k)
            W = jax.random.uniform(kw, (fan_in, fan_out), jnp.float32, -lim, lim)
            b = jax.random.uniform(kb, (fan_out,), jnp.float32, -lim, lim)
            return (W, b)
        W_DQ, b_DQ = lin(ks[0], D_MODEL, D_C)
        W_UQ, b_UQ = lin(ks[1], D_C, N_HEADS * D_K)
        W_DKV, b_DKV = lin(ks[2], D_MODEL, D_C)
        W_UK, b_UK = lin(ks[3], D_C, N_HEADS * D_K)
        W_UV, b_UV = lin(ks[4], D_C, N_HEADS * D_K)
        W_QR, b_QR = lin(ks[5], D_C, N_HEADS * D_HR)
        W_KR, b_KR = lin(ks[6], D_MODEL, D_HR)
        W_O, b_O = lin(ks[7], N_HEADS * D_K, D_MODEL)
        h_t = jax.random.normal(ks[8], (B, S, D_MODEL), jnp.float32)
        return {'h_t': h_t, 'W_DQ': W_DQ, 'b_DQ': b_DQ, 'W_UQ': W_UQ, 'b_UQ': b_UQ, 'W_DKV': W_DKV, 'b_DKV': b_DKV, 'W_UK': W_UK, 'b_UK': b_UK, 'W_UV': W_UV, 'b_UV': b_UV, 'W_QR': W_QR, 'b_QR': b_QR, 'W_KR': W_KR, 'b_KR': b_KR, 'W_O': W_O, 'b_O': b_O}
    _L1_attn_all = _L1_attn_setup()
    _L1_attn_in = {k: v for k, v in _L1_attn_all.items() if k in ('W_DQ', 'b_DQ', 'W_UQ', 'b_UQ', 'W_DKV', 'b_DKV', 'W_UK', 'b_UK', 'W_UV', 'b_UV', 'W_QR', 'b_QR', 'W_KR', 'b_KR', 'W_O', 'b_O')}
    del _L1_attn_all

    def _L1_ffn_setup():
        import jax, jax.numpy as jnp
        import numpy as np
        from jax import lax
        D = 256
        H = 1024
        E = 8
        TOPK = 2
        key = jax.random.key(seed)
        ks = jax.random.split(key, 7)
        s = 0.02
        return {'x': jax.random.normal(ks[0], (2, 512, D), dtype=jnp.float32), 'W1': jax.random.normal(ks[1], (E, D, H), dtype=jnp.float32) * s, 'b1': jnp.zeros((E, H), dtype=jnp.float32), 'W2': jax.random.normal(ks[2], (E, H, D), dtype=jnp.float32) * s, 'b2': jnp.zeros((E, D), dtype=jnp.float32), 'Wr': jax.random.normal(ks[3], (D, E), dtype=jnp.float32) * s, 'br': jnp.zeros((E,), dtype=jnp.float32)}
    _L1_ffn_all = _L1_ffn_setup()
    _L1_ffn_in = {k: v for k, v in _L1_ffn_all.items() if k in ('W1', 'b1', 'W2', 'b2', 'Wr', 'br')}
    del _L1_ffn_all
    return {'x': x, 'L0_tok_W': _L0_tok_in['W'], 'L0_tok_b': _L0_tok_in['b'], 'L0_tok_cls_token': _L0_tok_in['cls_token'], 'L0_tok_pos_embed': _L0_tok_in['pos_embed'], 'L0_attn_Wq': _L0_attn_in['Wq'], 'L0_attn_bq': _L0_attn_in['bq'], 'L0_attn_Wk': _L0_attn_in['Wk'], 'L0_attn_bk': _L0_attn_in['bk'], 'L0_attn_Wv': _L0_attn_in['Wv'], 'L0_attn_bv': _L0_attn_in['bv'], 'L0_attn_Wo': _L0_attn_in['Wo'], 'L0_attn_bo': _L0_attn_in['bo'], 'L0_ffn_Wg_s': _L0_ffn_in['Wg_s'], 'L0_ffn_Wu_s': _L0_ffn_in['Wu_s'], 'L0_ffn_Wd_s': _L0_ffn_in['Wd_s'], 'L0_ffn_Wg': _L0_ffn_in['Wg'], 'L0_ffn_Wu': _L0_ffn_in['Wu'], 'L0_ffn_Wd': _L0_ffn_in['Wd'], 'L0_ffn_Wr': _L0_ffn_in['Wr'], 'L0_ffn_rb': _L0_ffn_in['rb'], 'L1_attn_W_DQ': _L1_attn_in['W_DQ'], 'L1_attn_b_DQ': _L1_attn_in['b_DQ'], 'L1_attn_W_UQ': _L1_attn_in['W_UQ'], 'L1_attn_b_UQ': _L1_attn_in['b_UQ'], 'L1_attn_W_DKV': _L1_attn_in['W_DKV'], 'L1_attn_b_DKV': _L1_attn_in['b_DKV'], 'L1_attn_W_UK': _L1_attn_in['W_UK'], 'L1_attn_b_UK': _L1_attn_in['b_UK'], 'L1_attn_W_UV': _L1_attn_in['W_UV'], 'L1_attn_b_UV': _L1_attn_in['b_UV'], 'L1_attn_W_QR': _L1_attn_in['W_QR'], 'L1_attn_b_QR': _L1_attn_in['b_QR'], 'L1_attn_W_KR': _L1_attn_in['W_KR'], 'L1_attn_b_KR': _L1_attn_in['b_KR'], 'L1_attn_W_O': _L1_attn_in['W_O'], 'L1_attn_b_O': _L1_attn_in['b_O'], 'L1_ffn_W1': _L1_ffn_in['W1'], 'L1_ffn_b1': _L1_ffn_in['b1'], 'L1_ffn_W2': _L1_ffn_in['W2'], 'L1_ffn_b2': _L1_ffn_in['b2'], 'L1_ffn_Wr': _L1_ffn_in['Wr'], 'L1_ffn_br': _L1_ffn_in['br']}

def reference(x, L0_tok_W, L0_tok_b, L0_tok_cls_token, L0_tok_pos_embed, L0_attn_Wq, L0_attn_bq, L0_attn_Wk, L0_attn_bk, L0_attn_Wv, L0_attn_bv, L0_attn_Wo, L0_attn_bo, L0_ffn_Wg_s, L0_ffn_Wu_s, L0_ffn_Wd_s, L0_ffn_Wg, L0_ffn_Wu, L0_ffn_Wd, L0_ffn_Wr, L0_ffn_rb, L1_attn_W_DQ, L1_attn_b_DQ, L1_attn_W_UQ, L1_attn_b_UQ, L1_attn_W_DKV, L1_attn_b_DKV, L1_attn_W_UK, L1_attn_b_UK, L1_attn_W_UV, L1_attn_b_UV, L1_attn_W_QR, L1_attn_b_QR, L1_attn_W_KR, L1_attn_b_KR, L1_attn_W_O, L1_attn_b_O, L1_ffn_W1, L1_ffn_b1, L1_ffn_W2, L1_ffn_b2, L1_ffn_Wr, L1_ffn_br):
    import jax
    import jax.numpy as jnp

    def _L0_tok_ref(x, W, b, cls_token, pos_embed):
        import jax, jax.numpy as jnp
        import numpy as np
        IMG = 96
        PATCH = 16
        C_IN = 3
        EMBED = 256
        NPH = IMG // PATCH
        NUM_PATCHES = NPH * NPH
        PATCH_DIM = PATCH * PATCH * C_IN
        B, C, H, Wd = x.shape
        nph, npw = (H // PATCH, Wd // PATCH)
        patches = x.reshape(B, C, nph, PATCH, npw, PATCH)
        patches = patches.transpose(0, 2, 4, 1, 3, 5)
        patches = patches.reshape(B, nph * npw, C * PATCH * PATCH)
        proj = jnp.einsum('bnd,ed->bne', patches, W) + b
        cls = jnp.broadcast_to(cls_token, (B, 1, cls_token.shape[-1]))
        out = jnp.concatenate([cls, proj], axis=1) + pos_embed
        return out

    def _L0_attn_ref(hidden_states, Wq, bq, Wk, bk, Wv, bv, Wo, bo):
        import jax, jax.numpy as jnp
        import numpy as np
        EMBED_DIM = 256
        NUM_HEADS = 16
        HEAD_DIM = EMBED_DIM // NUM_HEADS
        WINDOW_SIZE = 32
        HALF_BAND = 2 * WINDOW_SIZE
        BAND = 2 * HALF_BAND + 1
        B, T, E = hidden_states.shape
        H, D = (NUM_HEADS, HEAD_DIM)
        S = T
        q = hidden_states @ Wq.T + bq
        k = hidden_states @ Wk.T + bk
        v = hidden_states @ Wv.T + bv
        q = q.reshape(B, T, H, D).transpose(0, 2, 1, 3)
        k = k.reshape(B, S, H, D).transpose(0, 2, 1, 3)
        v = v.reshape(B, S, H, D).transpose(0, 2, 1, 3)
        offsets = jnp.arange(-HALF_BAND, HALF_BAND + 1)
        idx = jnp.arange(T)[:, None] + offsets[None, :]
        valid = (idx >= 0) & (idx < S)
        idxc = jnp.clip(idx, 0, S - 1)
        kb = k[:, :, idxc, :]
        vb = v[:, :, idxc, :]
        scaling = jnp.sqrt(jnp.asarray(D, jnp.float32))
        scores = jnp.einsum('bhtd,bhtwd->bhtw', q, kb) / scaling
        scores = jnp.where(valid[None, None], scores, -jnp.inf)
        probs = jax.nn.softmax(scores, axis=-1)
        ctx = jnp.einsum('bhtw,bhtwd->bhtd', probs, vb)
        ctx = ctx.transpose(0, 2, 1, 3).reshape(B, T, H * D)
        attn_output = ctx @ Wo.T + bo
        return attn_output

    def _L0_ffn_ref(x, Wg_s, Wu_s, Wd_s, Wg, Wu, Wd, Wr, rb):
        import jax, jax.numpy as jnp
        import numpy as np
        B, S, H, I, E_ROUTED, TOP_K = (8, 512, 256, 512, 8, 2)

        def _expert(x, Wg, Wu, Wd):
            return jax.nn.silu(x @ Wg.T) * (x @ Wu.T) @ Wd.T
        shared = _expert(x, Wg_s, Wu_s, Wd_s)
        logits = jnp.einsum('bsh,eh->bse', x, Wr) + rb
        probs = jax.nn.sigmoid(logits)
        scores, idx = jax.lax.top_k(probs, TOP_K)
        cw = (jax.nn.one_hot(idx, E_ROUTED, dtype=x.dtype) * scores[..., None]).sum(-2)
        out = shared
        for e in range(E_ROUTED):
            out = out + cw[..., e:e + 1] * _expert(x, Wg[e], Wu[e], Wd[e])
        return out

    def _L1_attn_ref(h_t, W_DQ, b_DQ, W_UQ, b_UQ, W_DKV, b_DKV, W_UK, b_UK, W_UV, b_UV, W_QR, b_QR, W_KR, b_KR, W_O, b_O):
        import jax, jax.numpy as jnp
        import numpy as np
        import math
        D_MODEL, N_HEADS, D_K, D_C, D_HR = (256, 8, 128, 32, 32)
        B, S = (4, 512)
        b, s, _ = h_t.shape
        c_q = h_t @ W_DQ + b_DQ
        c_kv = h_t @ W_DKV + b_DKV
        q_c = (c_q @ W_UQ + b_UQ).reshape(b, s, N_HEADS, D_K).transpose(0, 2, 1, 3)
        k_c = (c_kv @ W_UK + b_UK).reshape(b, s, N_HEADS, D_K).transpose(0, 2, 1, 3)
        v_c = (c_kv @ W_UV + b_UV).reshape(b, s, N_HEADS, D_K).transpose(0, 2, 1, 3)
        q_r = (c_q @ W_QR + b_QR).reshape(b, s, N_HEADS, D_HR).transpose(0, 2, 1, 3)
        k_r = (h_t @ W_KR + b_KR)[:, None, :, :]
        k_r = jnp.broadcast_to(k_r, (b, N_HEADS, s, D_HR))
        q = jnp.concatenate([q_c, q_r], axis=-1)
        k = jnp.concatenate([k_c, k_r], axis=-1)
        scale = 1.0 / math.sqrt(D_K + D_HR)
        scores = jnp.einsum('bhsd,bhtd->bhst', q, k) * scale
        attn = jax.nn.softmax(scores, axis=-1)
        o = jnp.einsum('bhst,bhtd->bhsd', attn, v_c)
        o = o.transpose(0, 2, 1, 3).reshape(b, s, N_HEADS * D_K)
        return o @ W_O + b_O

    def _L1_ffn_ref(x, W1, b1, W2, b2, Wr, br):
        import jax, jax.numpy as jnp
        import numpy as np
        from jax import lax
        D = 256
        H = 1024
        E = 8
        TOPK = 2
        B, S, _ = x.shape
        xf = x.reshape(-1, D)
        logits = xf @ Wr + br
        topv, _ = lax.top_k(logits, TOPK)
        thresh = topv[:, TOPK - 1:TOPK]
        masked = jnp.where(logits >= thresh, logits, -jnp.inf)
        weights = jax.nn.softmax(masked, axis=-1)
        h = jax.nn.gelu(jnp.einsum('td,edh->eth', xf, W1) + b1[:, None, :], approximate=False)
        expert_out = jnp.einsum('eth,ehd->etd', h, W2) + b2[:, None, :]
        out = jnp.einsum('etd,te->td', expert_out, weights)
        return out.reshape(B, S, D)
    h = _L0_tok_ref(x, L0_tok_W, L0_tok_b, L0_tok_cls_token, L0_tok_pos_embed)
    h = _layernorm(h + _L0_attn_ref(h, L0_attn_Wq, L0_attn_bq, L0_attn_Wk, L0_attn_bk, L0_attn_Wv, L0_attn_bv, L0_attn_Wo, L0_attn_bo), axis=-1)
    h = _layernorm(h + _L0_ffn_ref(h, L0_ffn_Wg_s, L0_ffn_Wu_s, L0_ffn_Wd_s, L0_ffn_Wg, L0_ffn_Wu, L0_ffn_Wd, L0_ffn_Wr, L0_ffn_rb), axis=-1)
    h = _layernorm(h + _L1_attn_ref(h, L1_attn_W_DQ, L1_attn_b_DQ, L1_attn_W_UQ, L1_attn_b_UQ, L1_attn_W_DKV, L1_attn_b_DKV, L1_attn_W_UK, L1_attn_b_UK, L1_attn_W_UV, L1_attn_b_UV, L1_attn_W_QR, L1_attn_b_QR, L1_attn_W_KR, L1_attn_b_KR, L1_attn_W_O, L1_attn_b_O), axis=-1)
    h = _layernorm(h + _L1_ffn_ref(h, L1_ffn_W1, L1_ffn_b1, L1_ffn_W2, L1_ffn_b2, L1_ffn_Wr, L1_ffn_br), axis=-1)
    return h

_drawn_inputs = setup_inputs


def setup_inputs(seed=0):
    import zlib

    import numpy as np

    out = dict(_drawn_inputs(seed))
    spreads = {'L0_ffn_rb': (0.0, 0.644),
     'L1_ffn_b1': (0.0, 0.313),
     'L1_ffn_b2': (0.0, 0.1),
     'L1_ffn_br': (0.0, 0.1)}
    factors = {'L0_tok_b': 3.675,
     'L0_attn_Wq': 8.0,
     'L0_attn_bq': 8.0,
     'L0_attn_Wk': 8.0,
     'L0_attn_bk': 8.0,
     'L0_ffn_Wr': 2.827,
     'L1_attn_W_DQ': 6.709,
     'L1_attn_b_DQ': 8.0,
     'L1_attn_W_UQ': 8.0,
     'L1_attn_b_UQ': 8.0,
     'L1_attn_b_DKV': 4.332,
     'L1_attn_W_UK': 7.452,
     'L1_attn_b_UK': 8.0,
     'L1_attn_W_QR': 8.0,
     'L1_attn_b_QR': 8.0,
     'L1_attn_W_KR': 8.0,
     'L1_attn_b_KR': 8.0}
    for name, (base, spread) in spreads.items():
        noise = np.random.default_rng([zlib.crc32(name.encode()), seed]).standard_normal(out[name].shape)
        drawn = base * np.exp(spread * noise) if base else spread * noise
        out[name] = jnp.asarray(drawn.astype(out[name].dtype))
    for name, factor in factors.items():
        out[name] = (out[name] * factor).astype(out[name].dtype)
    return out
```

```python
from contextlib import ExitStack

import concourse.bass as bass
from concourse import mybir

F32 = mybir.dt.float32
F16 = mybir.dt.float16
I32 = mybir.dt.int32
ALU = mybir.AluOpType
ACT = mybir.ActivationFunctionType
AX = mybir.AxisListType

IMAGES = 64
GRID = 6
PATCHES = GRID * GRID
SEQ = PATCHES + 1
TOKENS = IMAGES * SEQ
D = 256
DC = D // 128
PATCH_DIM = 768
PC = PATCH_DIM // 128
PAIRS = IMAGES // 2
SLOT = 64
PAIR = 2 * SEQ
TRIO = 3 * SEQ
EPS = 1e-5
WS = 64.0

DUMMY = 128
ROWS = TOKENS + DUMMY
TOK_TILES = -(-TOKENS // 128)
TE = 8


class Sems:

    def __init__(self, nc, prefix):
        self.nc, self.prefix, self.made = nc, prefix, {}

    def __call__(self, name):
        if name not in self.made:
            self.made[name] = self.nc.alloc_semaphore(f"{self.prefix}_{name}")
        return self.made[name]

    def clear(self):
        self.nc.clear_and_free_semaphores(list(self.made.values()))
        self.nc.all_engine_barrier()


def wait(eng, sem, count):
    if isinstance(count, int) and count <= 0:
        return
    eng.wait_ge(sem, count)


def wait_alone(eng, S, name, count):
    wait(eng, S(name), count)
    if not isinstance(count, int):
        eng.sem_inc(S("passed"), 1)


class Step:

    def __init__(self, h, u, unroll, total):
        self.h, self.u, self.unroll, self.total = h, u, unroll, total

    def active(self, skew):
        if not isinstance(self.h, int):
            return True
        return 0 <= self.unroll * self.h + self.u - skew < self.total

    def item(self, skew):
        s = self.u - skew
        return (self.h * self.unroll + s, s % 2, self.h * (self.unroll // 2) + s // 2, s % self.unroll)


def run_steps(eng, total, skews, body, unroll=4):
    first = -(-(skews + 2) // unroll)
    last = total // unroll
    for h in range(first):
        for u in range(unroll):
            body(Step(h, u, unroll, total))
    with eng.Fori(first, last) as h:
        for u in range(unroll):
            body(Step(h, u, unroll, total))
    for t in range(last * unroll, total + skews):
        body(Step(t // unroll, t % unroll, unroll, total))
def build_attention0(nc, io, x1):
    HEADS, HD = 16, 16
    HC = 8
    with ExitStack() as ctx:
        def sb(name, shape, dt):
            return ctx.enter_context(nc.sbuf_tensor("a0_" + name, shape, dt))

        def ps(name, shape, dt=F32):
            return ctx.enter_context(nc.psum_tensor("a0_" + name, shape, dt))

        S = Sems(nc, "a0")
        ctx.callback(S.clear)

        w_stage = sb("w_stage", [128, PC, D], F32)
        w_emb = sb("w_emb", [128, 2, PC, D], F16)
        w_stage4 = sb("w_stage4", [128, 4, DC, D], F32)
        w_qkvo = sb("w_qkvo", [128, 2, 4, DC, D], F16)
        eye = sb("eye", [128, 128], F16)
        eye_ws = sb("eye_ws", [128, 128], F16)
        bias_in = sb("bias_in", [128, 4, DC], F32)
        bias_ws = sb("bias_ws", [128, 4, DC], F32)
        pos_t = sb("pos_t", [128, DC, SEQ], F32)
        cls_t = sb("cls_t", [128, DC, 1], F32)
        bo = sb("bo", [1, D], F32)
        bo_hl = sb("bo_hl", [1, 2, D], F16)
        ones = sb("ones", [1, 128], F16)
        head_mask = sb("head_mask", [128, HC], F32)
        odd_mask = sb("odd_mask", [128, 1], F32)
        even_mask = sb("even_mask", [128, 1], F32)
        half_power = sb("half_power", [128, 1], F32)

        x_in = sb("x_in", [128, 4, PC, 2 * PATCHES], F32)
        x_hl = sb("x_hl", [128, 2, 2, PC, 2 * PATCHES], F16)
        h0 = sb("h0", [128, 4, DC, 2, SEQ], F32)
        h0_hl = sb("h0_hl", [128, 4, 2, DC, 2, SLOT], F16)
        q_hl = sb("q_hl", [128, 2, 2, DC, PAIR], F16)
        k_hl = sb("k_hl", [128, 2, 2, DC, PAIR], F16)
        v_hl = sb("v_hl", [128, 4, 2, D], F16)
        LAST = HC - 3
        q_wide = sb("q_wide", [128, 2, 2, DC, 2, LAST * SEQ + 128], F16)
        qbd = q_wide[:, :, :, :, :, 0:HC * SEQ].rearrange("p b a c i (h q) -> p b a c i h q", q=SEQ)
        row_max = sb("row_max", [TRIO, 12], F32)
        row_sum = sb("row_sum", [TRIO, 12], F32)
        row_inv = sb("row_inv", [TRIO, 12], F32)
        prob = sb("prob", [TRIO, 2, 12, SEQ], F32)
        p_hl = sb("p_hl", [TRIO, 2, 2, 6, 2, SLOT], F16)
        pt_hl = sb("pt_hl", [128, 2, DC, 3 * TRIO], F16)
        odd = sb("odd", [128, 2, DC, SEQ], F32)
        ctx_f = sb("ctx_f", [128, DC, 2, SLOT], F32)
        ctx_hl = sb("ctx_hl", [128, 2, DC, 2, SLOT], F16)
        stats = sb("stats", [128, 6], F32)
        moments = sb("moments", [128, 2], F32)
        var_eps = sb("var_eps", [128, 1], F32)
        rstd = sb("rstd", [128, 1], F32)
        h1 = sb("h1", [128, 2, D], F32)

        psEQK = ps("psEQK", [128, DC * 2 * PATCHES + 2 * DC * PAIR])
        psE = psEQK[:, 0:DC * 2 * PATCHES].rearrange("p (c n) -> p c n", c=DC)
        psQK = psEQK[:, DC * 2 * PATCHES:].rearrange("p (z c n) -> p z c n", z=2, c=DC)
        psO = ps("psO", [128, D])
        psV = ps("psV", [128, D])
        psS = ps("psS", [128, 2, 6, SEQ])
        psT0 = ps("psT0", [128, 1024], F16)
        psT1 = ps("psT1", [128, 1024], F16)
        psC = [ps("psC0", [128, DC, PAIR]), ps("psC1", [128, DC, PAIR])]
        psT = [psT0[:, 0:672].rearrange("p (t c) -> p t c", t=6), psT1[:, 0:672].rearrange("p (t c) -> p t c", t=6)]

        N_SETUP = 8
        run = lambda eng, body: run_steps(eng, PAIRS, 6, body)
        block = ctx.enter_context(nc.Block())

        @block.sync
        def _(sp):
            sp.dma_start(w_stage[:], io["emb_w"]).then_inc(S("setup_in"), 16)
            sp.dma_start(w_stage4[:], io["qkvo_w"]).then_inc(S("setup_in"), 16)
            sp.dma_start(bias_in[:], io["bias0"]).then_inc(S("setup_in"), 16)
            sp.dma_start(pos_t[:], io["pos_t"]).then_inc(S("setup_in"), 16)
            sp.dma_start(cls_t[:], io["cls_t"]).then_inc(S("setup_in"), 16)
            sp.dma_start(bo[:], io["bo"]).then_inc(S("setup_in"), 16)
            sp.dma_start(head_mask[:], io["head_mask"]).then_inc(S("setup_in"), 16)
            sp.dma_start(eye[:], io["eye"]).then_inc(S("setup_in"), 16)

            sp.dma_start(x1[TOKENS:ROWS, :], io["zero_rows"]).then_inc(S("dummy_out"), 16)

            def step(st):
                if st.active(0):
                    p, b, hp, b4 = st.item(0)
                    wait(sp, S("x_high"), p - 3)
                    wait(sp, S("x_low"), p - 3)
                    sp.dma_start(x_in[:, b4], io["patches"][bass.ds(p, 1)].rearrange("a k c n -> k (a c) n")).then_inc(S(f"x_in{b4}"), 16)
                if st.active(6):
                    p, b, hp, _ = st.item(6)
                    wait(sp, S("h1"), p + 1)
                    for i in range(2):
                        sp.dma_start(x1[bass.ds(p * PAIR + i * SEQ, SEQ), :],
                                     h1[i * SLOT:i * SLOT + SEQ, b]).then_inc(S(f"h1_out{b}"), 16)

            run(sp, step)
            sp.wait_ge(S("dummy_out"), 16)
            for b in range(2):
                sp.wait_ge(S(f"h1_out{b}"), 32 * (PAIRS // 2))

        @block.tensor
        def _(pe):
            def products(out, left, right, first=True, last=True):
                n = 0
                todo = [(a, b, c) for c in left[1] for a, b in ((0, 0), (0, 1), (1, 0))]
                for a, b, c in todo:
                    ins = nc.tensor.matmul(out, left[0](a, c), right[0](b, c), start=first and n == 0,
                                           stop=last and n == len(todo) - 1)
                    n += 1
                return ins

            def embed(st):
                p, b, _, _ = st.item(1)
                if isinstance(p, int) and p == 0:
                    pe.wait_ge(S("w_ready"), 2)
                pe.wait_ge(S("x_high"), p + 1)
                pe.wait_ge(S("x_low"), p + 1)
                wait(pe, S("h0"), 2 * p)
                wait(pe, S("qk_low"), 2 * p)
                for m in range(DC):
                    ins = products(psE[:, m], (lambda a, c: w_emb[:, a, c, m * 128:(m + 1) * 128], range(PC)),
                                   (lambda a, c: x_hl[:, b, a, c], range(PC)))
                ins.then_inc(S("embedded"), 1)

            def project(st):
                p, b, _, b4 = st.item(2)
                if isinstance(p, int) and p == 0:
                    pe.wait_ge(S("w_ready"), 4)
                pe.wait_ge(S("h0_high"), p + 1)
                pe.wait_ge(S("h0_low"), p + 1)
                wait(pe, S("qk_low"), 2 * p)
                for z in range(2):
                    for m in range(DC):
                        ins = products(psQK[:, z, m].rearrange("p (i q) -> p i q", i=2), (lambda a, c: w_qkvo[:, a, z, c, m * 128:(m + 1) * 128], range(DC)),
                                       (lambda a, c: h0_hl[:, b4, a, c, :, 0:SEQ], range(DC)))
                ins.then_inc(S("qk"), 1)

            def project_values(st):
                p, b, _, b4 = st.item(2)
                wait(pe, S("v_low"), p)
                products(psV[:], (lambda a, c: h0_hl[:, b4, a, c], range(DC)),
                         (lambda a, c: w_qkvo[:, a, 2, c], range(DC))).then_inc(S("v"), 1)

            def transpose_probs(st):
                p, b, _, _ = st.item(4)
                pe.wait_ge(S("p_high"), p + 1)
                pe.wait_ge(S("p_low"), p + 1)
                wait(pe, S("pt_high"), p)
                wait(pe, S("pt_low"), p)
                for a in range(2):
                    for t in range(6):
                        ins = nc.tensor.transpose(psT[a][:, t, 0:TRIO], p_hl[:, b, a, t].rearrange("r i k -> r (i k)"), eye[0:TRIO, 0:TRIO])
                    ins.then_inc(S("pt"), 1)

            def scores(st):
                p, b, _, _ = st.item(3)
                pe.wait_ge(S("qbd_high"), p + 1)
                pe.wait_ge(S("qbd_low"), p + 1)
                wait(pe, S("shifted"), p)
                for i in range(2):
                    for c in range(DC):
                        for t in range(3):
                            at = min(3 * t, LAST) * SEQ
                            for n, (a, z) in enumerate(((0, 0), (0, 1), (1, 0))):
                                ins = nc.tensor.matmul(psS[:, i, 3 * c + t], q_wide[:, b, a, c, i, at:at + 128],
                                                       k_hl[:, b, z, c, i * SEQ:(i + 1) * SEQ], start=n == 0, stop=n == 2)
                ins.then_inc(S("scored"), 1)

            def values(st):
                p, b, _, b4 = st.item(5)
                pe.wait_ge(S("pt_high"), p + 1)
                pe.wait_ge(S("pt_low"), p + 1)
                wait_alone(pe, S, "ctx", 2 * p)
                for i in range(2):
                    rows = slice(i * SLOT, i * SLOT + SEQ)
                    for c in range(DC):
                        for j in range(4):
                            at = PAIR * j + (SEQ if j == 3 else 0)
                            for n, (a, z) in enumerate(((0, 0), (0, 1), (1, 0))):
                                ins = nc.tensor.matmul(psC[i][32 * j:32 * j + 32, c],
                                                       v_hl[rows, b4, z, c * 128 + 32 * j:c * 128 + 32 * j + 32],
                                                       pt_hl[rows, a, c, at:at + PAIR], start=n == 0, stop=n == 2)
                    ins.then_inc(S("mixed"), 1)

            def residual(st):
                p, b, _, b4 = st.item(5)
                wait(pe, S("h1"), p)
                if isinstance(p, int) and p == 0:
                    pe.wait_ge(S("bo_ready"), 3)
                for a in range(2):
                    nc.tensor.matmul(psO[:], ones[:], bo_hl[:, a], start=a == 0, stop=False)
                for m in range(DC):
                    for a in range(2):
                        ins = nc.tensor.matmul(psO[:, m * 128:(m + 1) * 128], h0_hl[:, b4, a, m], eye_ws[:], start=False, stop=False)
                ins.then_inc(S("residual"), 1)

            def output(st):
                p, b, _, b4 = st.item(5)
                pe.wait_ge(S("ctx_high"), p + 1)
                pe.wait_ge(S("ctx_low"), p + 1)
                ins = products(psO[:], (lambda a, c: ctx_hl[:, a, c], range(DC)),
                               (lambda a, c: w_qkvo[:, a, 3, c], range(DC)), first=False)
                ins.then_inc(S("projected"), 1)

            def step(st):
                if st.active(2):
                    project(st)
                if st.active(2):
                    project_values(st)
                if st.active(5):
                    values(st)
                if st.active(3):
                    scores(st)
                if st.active(5):
                    residual(st)
                if st.active(1):
                    embed(st)
                if st.active(4):
                    transpose_probs(st)
                if st.active(5):
                    output(st)

            run(pe, step)

        @block.scalar
        def _(act):
            act.wait_ge(S("setup_in"), 16 * N_SETUP)
            nc.scalar.activation(w_emb[:, 0], w_stage[:], ACT.Copy, scale=WS).then_inc(S("w_high"), 1)
            nc.scalar.activation(w_qkvo[:, 0], w_stage4[:], ACT.Copy, scale=WS).then_inc(S("w_high"), 1)

            def step(st):
                if st.active(2):
                    p, b, _, b4 = st.item(2)
                    act.wait_ge(S("qk"), p + 1)
                    wait(act, S("qbd_low"), p - 1)
                    wait(act, S("qbd_high"), p - 1)
                    wait(act, S("scored"), p - 1)
                    for z, dst in ((0, q_hl), (1, k_hl)):
                        for c in range(DC):
                            ins = nc.scalar.activation(dst[:, b, 0, c], psQK[:, z, c], ACT.Identity, bias=bias_ws[:, 1 + z, c:c + 1])
                    ins.then_inc(S("qk_high"), 1)
                if st.active(4):
                    p, b, _, _ = st.item(4)
                    act.wait_ge(S("prob"), p + 1)
                    wait(act, S("pt"), 2 * (p - 1))
                    for i in range(2):
                        ins = nc.scalar.activation(p_hl[:, b, 0, :, i, 0:SEQ], prob[:, b, 6 * i:6 * i + 6], ACT.Copy)
                    ins.then_inc(S("p_high"), 1)
                if st.active(2):
                    p, b, _, b4 = st.item(2)
                    act.wait_ge(S("v"), p + 1)
                    wait(act, S("mixed"), 2 * (p - 3))
                    nc.scalar.activation(v_hl[:, b4, 0], psV[:], ACT.Copy).then_inc(S("v_high"), 1)
                if st.active(5):
                    p, b, _, _ = st.item(5)
                    for i in range(2):
                        act.wait_ge(S("mixed"), 2 * p + 1 + i)
                        wait(act, S("ctx"), 2 * p)
                        for c in range(DC):
                            ins = nc.scalar.activation(odd[:, i, c], psC[i][:, c, SEQ:PAIR], ACT.Identity, scale=odd_mask[:, 0:1],
                                                       bias=bias_in[:, 3, c:c + 1])
                        ins.then_inc(S("odd"), 1)
                if st.active(0):
                    p, b, hp, b4 = st.item(0)
                    act.wait_ge(S(f"x_in{b4}"), 16 * st.h + 16)
                    wait(act, S("embedded"), p - 1)
                    nc.scalar.activation(x_hl[:, b, 0], x_in[:, b4], ACT.Copy).then_inc(S("x_high"), 1)
                if st.active(5):
                    p, b, _, _ = st.item(5)
                    act.wait_ge(S("ctx"), 2 * p + 2)
                    wait(act, S("projected"), p)
                    nc.scalar.activation(ctx_hl[:, 0, :, :, 0:SEQ], ctx_f[:, :, :, 0:SEQ], ACT.Copy).then_inc(S("ctx_high"), 1)
                if st.active(3):
                    p, b, _, _ = st.item(3)
                    act.wait_ge(S("shifted"), p + 1)
                    nc.scalar.activation(prob[:, b], prob[:, b], ACT.Exp, scale=1.0 / (WS * WS * HD ** 0.5)).then_inc(S("exp"), 1)
                if st.active(1):
                    p, b, _, b4 = st.item(1)
                    act.wait_ge(S("h0"), 2 * p + 2)
                    wait(act, S("residual"), p - 3)
                    nc.scalar.activation(h0_hl[:, b4, 0, :, :, 0:SEQ], h0[:, b4], ACT.Copy).then_inc(S("h0_high"), 1)
                if st.active(4):
                    p, b, _, _ = st.item(4)
                    act.wait_ge(S("pt"), 2 * p + 1)
                    wait(act, S("mixed"), 2 * p)
                    nc.scalar.activation(pt_hl[:, 0].rearrange("k c (t q) -> k (c t) q", t=3), psT[0][:, :, 0:TRIO], ACT.Copy).then_inc(S("pt_high"), 1)
                    act.wait_ge(S("pt"), 2 * p + 2)
                    nc.scalar.activation(pt_hl[:, 1].rearrange("k c (t q) -> k (c t) q", t=3), psT[1][:, :, 0:TRIO], ACT.Copy).then_inc(S("pt_low"), 1)

            run(act, step)

        @block.gpsimd
        def _(pool):
            nc.gpsimd.memset(h0_hl[:], 0.0).then_inc(S("zeroed"), 1)
            nc.gpsimd.memset(p_hl[:], 0.0).then_inc(S("zeroed"), 1)
            nc.gpsimd.memset(ctx_hl[:], 0.0).then_inc(S("zeroed"), 1)
            nc.gpsimd.memset(half_power[:], -0.5).then_inc(S("zeroed"), 1)
            nc.gpsimd.memset(q_wide[:], 0.0).then_inc(S("zeroed"), 1)
            pool.wait_ge(S("zeroed"), 5)

            def step(st):
                if st.active(4):
                    p, b, _, _ = st.item(4)
                    pool.wait_ge(S("p_high"), p + 1)
                    for i in range(2):
                        ins = nc.gpsimd.tensor_tensor(p_hl[:, b, 1, :, i, 0:SEQ], prob[:, b, 6 * i:6 * i + 6], p_hl[:, b, 0, :, i, 0:SEQ], ALU.subtract)
                    ins.then_inc(S("p_low"), 1)
                if st.active(2):
                    p, b, _, _ = st.item(2)
                    pool.wait_ge(S("qk_low"), 2 * p + 1)
                    wait_alone(pool, S, "scored", p - 1)
                    for h in range(HC // 2):
                        nc.gpsimd.tensor_scalar(qbd[:, b, 1, :, :, h], q_hl[:, b, 1].rearrange("p c (i q) -> p c i q", i=2),
                                                head_mask[:, h:h + 1], 1.0, ALU.mult, ALU.mult)
                if st.active(5):
                    p, b, _, _ = st.item(5)
                    pool.wait_ge(S("ctx_high"), p + 1)
                    nc.gpsimd.tensor_tensor(ctx_hl[:, 1, :, :, 0:SEQ], ctx_f[:, :, :, 0:SEQ], ctx_hl[:, 0, :, :, 0:SEQ],
                                            ALU.subtract).then_inc(S("ctx_low"), 1)
                if st.active(1):
                    p, b, _, b4 = st.item(1)
                    pool.wait_ge(S("h0_high"), p + 1)
                    nc.gpsimd.tensor_tensor(h0_hl[:, b4, 1, :, :, 0:SEQ], h0[:, b4], h0_hl[:, b4, 0, :, :, 0:SEQ],
                                            ALU.subtract).then_inc(S("h0_low"), 1)
                if st.active(2):
                    p, b, _, _ = st.item(2)
                    for h in range(HC // 2, HC):
                        ins = nc.gpsimd.tensor_scalar(qbd[:, b, 1, :, :, h], q_hl[:, b, 1].rearrange("p c (i q) -> p c i q", i=2),
                                                      head_mask[:, h:h + 1], 1.0, ALU.mult, ALU.mult)
                    ins.then_inc(S("qbd_low"), 1)
                if st.active(0):
                    p, b, _, b4 = st.item(0)
                    pool.wait_ge(S("x_high"), p + 1)
                    nc.gpsimd.tensor_tensor(x_hl[:, b, 1], x_in[:, b4], x_hl[:, b, 0], ALU.subtract).then_inc(S("x_low"), 1)
                if st.active(5):
                    p, b, _, _ = st.item(5)
                    pool.wait_ge(S("var_eps"), p + 1)
                    nc.gpsimd.tensor_tensor(rstd[:], var_eps[:], half_power[:], ALU.pow).then_inc(S("rstd"), 1)

            run(pool, step)

        @block.vector
        def _(dve):
            dve.wait_ge(S("setup_in"), 16 * N_SETUP)
            dve.wait_ge(S("w_high"), 1)
            nc.vector.scalar_tensor_tensor(w_emb[:, 1].rearrange("p c n -> p (c n)"), w_stage[:].rearrange("p c n -> p (c n)"), WS,
                                           w_emb[:, 0].rearrange("p c n -> p (c n)"), ALU.mult, ALU.subtract).then_inc(S("w_ready"), 1)
            nc.vector.tensor_scalar(eye_ws[:], eye[:], WS, None, ALU.mult).then_inc(S("w_ready"), 1)
            dve.wait_ge(S("w_high"), 2)
            nc.vector.scalar_tensor_tensor(w_qkvo[:, 1].rearrange("p z c n -> p (z c n)"), w_stage4[:].rearrange("p z c n -> p (z c n)"), WS,
                                           w_qkvo[:, 0].rearrange("p z c n -> p (z c n)"), ALU.mult, ALU.subtract).then_inc(S("w_ready"), 1)
            nc.vector.tensor_scalar(bias_ws[:], bias_in[:], WS, None, ALU.mult).then_inc(S("w_ready"), 1)
            nc.vector.memset(ones[:], 1.0).then_inc(S("bo_ready"), 1)
            nc.vector.tensor_scalar(bo_hl[:, 0], bo[:], WS, None, ALU.mult).then_inc(S("bo_ready"), 1)
            dve.wait_ge(S("bo_ready"), 2)
            nc.vector.scalar_tensor_tensor(bo_hl[:, 1], bo[:], WS, bo_hl[:, 0], ALU.mult, ALU.subtract).then_inc(S("bo_ready"), 1)
            nc.vector.tensor_tensor(odd_mask[:], head_mask[:, 1:2], head_mask[:, 3:4], ALU.add).then_inc(S("masks"), 1)
            for n, h in enumerate((5, 7)):
                dve.wait_ge(S("masks"), n + 1)
                nc.vector.tensor_tensor(odd_mask[:], odd_mask[:], head_mask[:, h:h + 1], ALU.add).then_inc(S("masks"), 1)
            dve.wait_ge(S("masks"), 3)
            nc.vector.tensor_scalar(even_mask[:], odd_mask[:], -1.0 / WS, 1.0 / WS, ALU.mult, ALU.add).then_inc(S("masks"), 1)
            dve.wait_ge(S("masks"), 4)
            nc.vector.tensor_scalar(odd_mask[:], odd_mask[:], 1.0 / WS, None, ALU.mult).then_inc(S("masks"), 1)
            nc.vector.tensor_tensor(cls_t[:], cls_t[:], pos_t[:, :, 0:1], ALU.add).then_inc(S("masks"), 1)
            for c in range(DC):
                nc.vector.tensor_scalar(pos_t[:, c, 1:SEQ], pos_t[:, c, 1:SEQ], bias_in[:, 0, c:c + 1], None, ALU.add).then_inc(S("masks"), 1)
            dve.wait_ge(S("masks"), 6 + DC)
            for b4 in range(4):
                for i in range(2):
                    nc.vector.tensor_copy(h0[:, b4, :, i, 0:1], cls_t[:]).then_inc(S("masks"), 1)
            dve.wait_ge(S("masks"), 14 + DC)

            def step(st):
                scored = psS[0:TRIO].rearrange("r i t k -> r (i t) k")
                if st.active(2):
                    p, b, _, b4 = st.item(2)
                    dve.wait_ge(S("qk_high"), p + 1)
                    for z, dst in ((0, q_hl), (1, k_hl)):
                        for c in range(DC):
                            ins = nc.vector.scalar_tensor_tensor(dst[:, b, 1, c], psQK[:, z, c], bias_ws[:, 1 + z, c:c + 1], dst[:, b, 0, c],
                                                                 ALU.add, ALU.subtract)
                        ins.then_inc(S("qk_low"), 1)
                if st.active(2):
                    p, b, _, b4 = st.item(2)
                    dve.wait_ge(S("v_high"), p + 1)
                    nc.vector.tensor_tensor(v_hl[:, b4, 1], psV[:], v_hl[:, b4, 0], ALU.subtract).then_inc(S("v_low"), 1)
                if st.active(6):
                    p, b, hp, b4 = st.item(6)
                    dve.wait_ge(S("rstd"), p + 1)
                    wait(dve, S(f"h1_out{b}"), 32 * hp)
                    nc.vector.tensor_scalar(h1[:, b], psO[:], moments[:, 0:1], rstd[:, 0:1], ALU.subtract, ALU.mult).then_inc(S("h1"), 1)
                if st.active(3):
                    p, b, _, _ = st.item(3)
                    dve.wait_ge(S("scored"), p + 1)
                    nc.vector.tensor_reduce(row_max[:], scored, AX.X, ALU.max).then_inc(S("row_max"), 1)
                if st.active(5):
                    p, b, _, b4 = st.item(5)
                    for i in range(2):
                        dve.wait_ge(S("odd"), 2 * p + 1 + i)
                        if i == 0:
                            wait(dve, S("ctx_low"), p)
                        nc.vector.scalar_tensor_tensor(ctx_f[:, :, i, 0:SEQ], psC[i][:, :, 0:SEQ], even_mask[:, 0:1], odd[:, i],
                                                       ALU.mult, ALU.add).then_inc(S("ctx"), 1)
                if st.active(3):
                    p, b, _, _ = st.item(3)
                    dve.wait_ge(S("row_max"), p + 1)
                    wait(dve, S("p_low"), p - 1)
                    nc.vector.tensor_tensor(prob[:, b], scored, row_max[:].unsqueeze(2).broadcast_to([TRIO, 12, SEQ]), ALU.subtract).then_inc(S("shifted"), 1)
                if st.active(1):
                    p, b, _, b4 = st.item(1)
                    dve.wait_ge(S("embedded"), p + 1)
                    wait(dve, S("h0_low"), p - 3)
                    for c in range(DC):
                        nc.vector.scalar_tensor_tensor(h0[:, b4, c, :, 1:SEQ], psE[:, c].rearrange("p (i n) -> p i n", i=2), 1.0 / WS,
                                                       pos_t[:, c:c + 1, 1:SEQ].broadcast_to([128, 2, PATCHES]), ALU.mult, ALU.add).then_inc(S("h0"), 1)
                if st.active(2):
                    p, b, _, b4 = st.item(2)
                    wait(dve, S("scored"), p - 1)
                    for h in range(HC):
                        ins = nc.vector.tensor_scalar(qbd[:, b, 0, :, :, h], q_hl[:, b, 0].rearrange("p c (i q) -> p c i q", i=2),
                                                      head_mask[:, h:h + 1], None, ALU.mult)
                    ins.then_inc(S("qbd_high"), 1)
                if st.active(3):
                    p, b, _, _ = st.item(3)
                    dve.wait_ge(S("exp"), p + 1)
                    nc.vector.tensor_reduce(row_sum[:], prob[:, b], AX.X, ALU.add).then_inc(S("row_sum"), 1)
                if st.active(3):
                    p, b, _, _ = st.item(3)
                    dve.wait_ge(S("row_sum"), p + 1)
                    nc.vector.reciprocal(row_inv[:], row_sum[:]).then_inc(S("row_inv"), 1)
                if st.active(5):
                    p, b, hp, b4 = st.item(5)
                    dve.wait_ge(S("projected"), p + 1)
                    nc.vector.bn_stats(stats[:], psO[:]).then_inc(S("stats"), 1)
                if st.active(3):
                    p, b, _, _ = st.item(3)
                    dve.wait_ge(S("row_inv"), p + 1)
                    nc.vector.tensor_tensor(prob[:, b], prob[:, b], row_inv[:].unsqueeze(2).broadcast_to([TRIO, 12, SEQ]), ALU.mult).then_inc(S("prob"), 1)
                if st.active(5):
                    p, b, hp, b4 = st.item(5)
                    wait_alone(dve, S, "stats", p + 1)
                    nc.vector.bn_aggr(moments[:], stats[:]).then_inc(S("moments"), 1)
                if st.active(5):
                    p, b, hp, b4 = st.item(5)
                    dve.wait_ge(S("moments"), p + 1)
                    nc.vector.tensor_scalar(var_eps[:], moments[:, 1:2], WS * WS * EPS, None, ALU.add).then_inc(S("var_eps"), 1)

            run(dve, step)
def build_routing(nc, io, x_rows, acc_rows, plan, layer):
    TT = TOK_TILES
    first = plan.first
    with ExitStack() as ctx:
        def sb(name, shape, dt=F32):
            return ctx.enter_context(nc.sbuf_tensor(f"r{layer}_" + name, shape, dt))

        S = Sems(nc, f"r{layer}")
        ctx.callback(S.clear)
        wr = sb("wr", [128, DC, TE])
        wr_hl = sb("wr_hl", [128, 2, DC, TE], F16)
        bias = sb("bias", [128, TE])
        eye = sb("eye", [128, 128])
        below = sb("below", [128, 128], F16)
        ones = sb("ones", [128, 128], F16)
        lane = sb("lane", [128, 128], F16)
        place = sb("place", [128, TE])
        valid = sb("valid", [128, TT])
        values = sb("values", [128, 2, TT * TE], F16)
        dummy_row = sb("dummy_row", [128, 1])
        steps = sb("steps", [1, TT - 1])

        x = sb("x", [128, 2, D])
        xt_hl = sb("xt_hl", [128, 2, 2, DC, 128], F16)
        z = sb("z", [128, TT, TE])
        score = sb("score", [128, TT, TE])
        work = sb("work", [128, TT, TE])
        pick = sb("pick", [128, TT, TE])
        top = sb("top", [128, TT])
        top2 = sb("top2", [128, TT])
        total = sb("total", [128, TT])
        mask = sb("mask", [128, TT + 1, TE], F16)
        earlier = sb("earlier", [128, TT + 1, TE], F16)
        rank = sb("rank", [128, TT * TE])
        rank_i = sb("rank_i", [128, TT * TE], I32)
        lane_i = sb("lane_i", [128, TT * TE], I32)
        tile_i = sb("tile_i", [128, TT * TE], I32)
        lane_f = sb("lane_f", [128, TT * TE])
        tile_f = sb("tile_f", [128, TT * TE], F16)
        w_hl = sb("w_hl", [128, 2, TT * TE], F16)
        in_tile = sb("in_tile", [128, TT, TT * TE], F16)
        spread = sb("spread", [128, 4, TT, TT * TE], F16)
        RING = 8
        in_lane = sb("in_lane", [128, RING, 128], F16)
        counts = sb("counts", [1, TE])
        over = sb("over", [1, TE, TT - 1])
        tiles = sb("tiles", [1, TE])
        starts = sb("starts", [1, first + TE + 1])
        slot_id = sb("slot_id", [128, TE, TT])
        empty = sb("empty", [128, TE, TT])

        psX = [ctx.enter_context(nc.psum_tensor(f"r{layer}_psX{b}", [128, DC, 128], F32)) for b in range(2)]
        psL = ctx.enter_context(nc.psum_tensor(f"r{layer}_psL", [128, TT, TE], F32))
        psR = ctx.enter_context(nc.psum_tensor(f"r{layer}_psR", [128, TT + 1, TE], F32))
        psT = [ctx.enter_context(nc.psum_tensor(f"r{layer}_psT{b}", [128, TE // 2, 4, TT], F32)) for b in range(2)]
        N_SETUP = 10
        block = ctx.enter_context(nc.Block())

        @block.sync
        def _(sp):
            for dst, name in ((wr, "wr"), (below, "below"), (lane, "lane"), (place, "place"), (valid, "valid"),
                              (values, "values"), (dummy_row, "dummy_row"), (steps, "steps"), (eye, "eye_f")):
                src = io[name + str(layer)] if name == "wr" else io[name]
                sp.dma_start(dst[:], src).then_inc(S("setup_in"), 16)
            sp.dma_start(bias[:], io[f"router_bias{layer}"].broadcast_to([128, TE])).then_inc(S("setup_in"), 16)
            for t in range(TT):
                if t >= 2:
                    sp.wait_ge(S("turned"), t - 1)
                sp.dma_start(x[:, t % 2], x_rows[t * 128:(t + 1) * 128, :]).then_inc(S(f"x_in{t % 2}"), 16)
            sp.dma_start(acc_rows, x_rows).then_inc(S("acc_out"), 16)
            sp.wait_ge(S("acc_out"), 16)
            if first:
                sp.dma_start(plan.index[:, 0, :], io["all_index"]).then_inc(S("shared_in"), 16)
                sp.dma_start(plan.weight[:, 0, :], io["valid"]).then_inc(S("shared_in"), 16)
                sp.wait_ge(S("shared_in"), 32)

        @block.tensor
        def _(pe):
            pe.wait_ge(S("setup_in"), 16 * N_SETUP)
            pe.wait_ge(S("wr_ready"), 2)

            def logits(t):
                pe.wait_ge(S("xt_low"), t + 1)
                for n, (a, b, c) in enumerate((a, b, c) for c in range(DC) for a, b in ((0, 0), (0, 1), (1, 0))):
                    ins = nc.tensor.matmul(psL[:, t], xt_hl[:, t % 2, a, c], wr_hl[:, b, c], start=n == 0, stop=n == 3 * DC - 1)
                ins.then_inc(S("logits"), 1)

            for t in range(TT):
                pe.wait_ge(S(f"x_in{t % 2}"), 16 * (t // 2 + 1))
                if t >= 2:
                    pe.wait_ge(S("xt_low"), t - 1)
                for c in range(DC):
                    ins = nc.tensor.transpose(psX[t % 2][:, c], x[:, t % 2, c * 128:(c + 1) * 128], eye[:])
                ins.then_inc(S("turned"), 1)
                if t >= 1:
                    logits(t - 1)
            logits(TT - 1)
            pe.wait_ge(S("earlier"), TT + 1)
            nc.tensor.matmul(psR[:], below[:], mask[:], start=True, stop=False)
            nc.tensor.matmul(psR[:], ones[:], earlier[:], start=False, stop=True).then_inc(S("ranked"), 1)
            pe.wait_ge(S("spread"), 2)
            for e in range(TE):
                for t in range(TT):
                    n = e * TT + t
                    pe.wait_ge(S("in_lane"), n + 1)
                    nc.tensor.matmul(psT[e // 4][:, e % 4], in_lane[:, n % RING], spread[:, :, :, t * TE + e],
                                     start=t == 0, stop=t == TT - 1).then_inc(S("placed"), 1)

        @block.scalar
        def _(act):
            act.wait_ge(S("setup_in"), 16 * N_SETUP)
            nc.scalar.activation(wr_hl[:, 0], wr[:], ACT.Copy, scale=WS).then_inc(S("wr_high"), 1)
            for t in range(TT):
                act.wait_ge(S("turned"), t + 1)
                if t >= 2:
                    act.wait_ge(S("logits"), t - 1)
                nc.scalar.activation(xt_hl[:, t % 2, 0], psX[t % 2][:], ACT.Copy).then_inc(S("xt_high"), 1)
            if layer == 0:
                act.wait_ge(S("z"), 1)
                nc.scalar.activation(score[:], z[:], ACT.Exp, scale=-1.0).then_inc(S("exp"), 1)
            else:
                act.wait_ge(S("z_shifted"), 1)
                nc.scalar.activation(score[:], work[:], ACT.Exp).then_inc(S("exp"), 1)

        @block.gpsimd
        def _(pool):
            nc.gpsimd.memset(ones[:], 1.0).then_inc(S("ones"), 1)
            pool.wait_ge(S("in_tile"), TT)
            pool.wait_ge(S("setup_in"), 16 * N_SETUP)
            for v in range(2):
                ins = nc.gpsimd.tensor_tensor(spread[:, v], in_tile[:], values[:, v:v + 1].broadcast_to([128, TT, TT * TE]), ALU.mult)
            ins.then_inc(S("spread"), 1)

        @block.vector
        def _(dve):
            made = [0]

            def then(ins):
                made[0] += 1
                ins.then_inc(S("link"), 1)
                dve.wait_ge(S("link"), made[0])

            over_tiles = lambda v: v.unsqueeze(1).broadcast_to([128, TT, TE])
            over_experts = lambda v: v.unsqueeze(2).broadcast_to([128, TT, TE])
            dve.wait_ge(S("setup_in"), 16 * N_SETUP)
            dve.wait_ge(S("wr_high"), 1)
            dve.wait_ge(S("ones"), 1)
            nc.vector.scalar_tensor_tensor(wr_hl[:, 1], wr[:], WS, wr_hl[:, 0], ALU.mult, ALU.subtract).then_inc(S("wr_ready"), 1)
            nc.vector.memset(mask[:], 0.0).then_inc(S("wr_ready"), 1)
            dve.wait_ge(S("wr_ready"), 2)
            for t in range(TT):
                dve.wait_ge(S("xt_high"), t + 1)
                if t >= 2:
                    dve.wait_ge(S("logits"), t - 1)
                nc.vector.tensor_tensor(xt_hl[:, t % 2, 1], psX[t % 2][:], xt_hl[:, t % 2, 0], ALU.subtract).then_inc(S("xt_low"), 1)
            dve.wait_ge(S("logits"), TT)
            nc.vector.scalar_tensor_tensor(z[:], psL[:], 1.0 / WS, over_tiles(bias[:]), ALU.mult, ALU.add).then_inc(S("z"), 1)
            dve.wait_ge(S("z"), 1)
            if layer == 0:
                dve.wait_ge(S("exp"), 1)
                then(nc.vector.tensor_scalar(score[:], score[:], 1.0, None, ALU.add))
                then(nc.vector.reciprocal(z[:], score[:]))

            def take_first(src, top, out):
                then(nc.vector.tensor_reduce(top[:], src[:], AX.X, ALU.max))
                then(nc.vector.tensor_tensor(out[:], src[:], over_experts(top[:]), ALU.is_equal))
                then(nc.vector.tensor_tensor(out[:], out[:], over_tiles(place[:]), ALU.mult))
                then(nc.vector.tensor_reduce(total[:], out[:], AX.X, ALU.max))
                then(nc.vector.tensor_tensor(out[:], out[:], over_experts(total[:]), ALU.is_equal))

            take_first(z, top, pick)
            then(nc.vector.scalar_tensor_tensor(work[:], pick[:], -3.0e38, z[:], ALU.mult, ALU.add))
            if layer == 0:
                take_first(work, top2, score)
                then(nc.vector.tensor_tensor(pick[:], pick[:], score[:], ALU.add))
            else:
                then(nc.vector.tensor_reduce(top2[:], work[:], AX.X, ALU.max))
                then(nc.vector.tensor_tensor(pick[:], z[:], over_experts(top2[:]), ALU.is_ge))
            then(nc.vector.tensor_tensor(pick[:], pick[:], over_experts(valid[:]), ALU.mult))
            nc.vector.tensor_copy(mask[:, 0:TT], pick[:]).then_inc(S("mask"), 1)
            dve.wait_ge(S("mask"), 1)
            nc.vector.memset(earlier[:, 0], 0.0).then_inc(S("earlier"), 1)
            for t in range(TT):
                dve.wait_ge(S("earlier"), t + 1)
                nc.vector.tensor_tensor(earlier[:, t + 1], earlier[:, t], mask[:, t], ALU.add).then_inc(S("earlier"), 1)
            if layer == 0:
                then(nc.vector.tensor_tensor(work[:], z[:], pick[:], ALU.mult))
            else:
                nc.vector.tensor_tensor(work[:], z[:], over_experts(top[:]), ALU.subtract).then_inc(S("z_shifted"), 1)
                dve.wait_ge(S("exp"), 1)
                then(nc.vector.tensor_tensor(work[:], score[:], pick[:], ALU.mult))
                then(nc.vector.tensor_reduce(total[:], work[:], AX.X, ALU.add))
                then(nc.vector.tensor_scalar(total[:], total[:], 1.0e-30, None, ALU.max))
                then(nc.vector.reciprocal(top2[:], total[:]))
                then(nc.vector.tensor_tensor(work[:], work[:], over_experts(top2[:]), ALU.mult))
            flat = work[:].rearrange("p t e -> p (t e)")
            then(nc.vector.tensor_copy(w_hl[:, 0], flat))
            then(nc.vector.tensor_tensor(w_hl[:, 1], flat, w_hl[:, 0], ALU.subtract))
            dve.wait_ge(S("ranked"), 1)
            then(nc.vector.scalar_tensor_tensor(rank[:].rearrange("p (t e) -> p t e", e=TE), psR[:, 0:TT], 1.0, pick[:], ALU.add, ALU.mult))
            then(nc.vector.tensor_scalar(rank_i[:], rank[:], -1.0, None, ALU.add))
            then(nc.vector.tensor_scalar(lane_i[:], rank_i[:], 127, None, ALU.bitwise_and))
            then(nc.vector.tensor_scalar(tile_i[:], rank_i[:], 7, None, ALU.arith_shift_right))
            then(nc.vector.tensor_copy(lane_f[:], lane_i[:]))
            then(nc.vector.tensor_copy(tile_f[:], tile_i[:]))
            for c in range(TT):
                nc.vector.tensor_scalar(in_tile[:, c], tile_f[:], float(c), None, ALU.is_equal).then_inc(S("in_tile"), 1)
            dve.wait_ge(S("in_tile"), TT)
            for v in range(2):
                ins = nc.vector.tensor_tensor(spread[:, 2 + v], in_tile[:], w_hl[:, v:v + 1].broadcast_to([128, TT, TT * TE]), ALU.mult)
            ins.then_inc(S("spread"), 1)
            for e in range(TE):
                for t in range(TT):
                    n = e * TT + t
                    if n >= RING:
                        dve.wait_ge(S("placed"), n - RING + 1)
                    nc.vector.tensor_scalar(in_lane[:, n % RING], lane[:], lane_f[:, t * TE + e:t * TE + e + 1], None,
                                            ALU.is_equal).then_inc(S("in_lane"), 1)
            then(nc.vector.tensor_copy(counts[:], psR[0:1, TT]))
            then(nc.vector.tensor_tensor(over[:], counts[:].unsqueeze(2).broadcast_to([1, TE, TT - 1]),
                                         steps[:].unsqueeze(1).broadcast_to([1, TE, TT - 1]), ALU.is_gt))
            then(nc.vector.tensor_reduce(tiles[:], over[:], AX.X, ALU.add))
            then(nc.vector.tensor_scalar(tiles[:], tiles[:], 1.0, float(MIN_TILES), ALU.add, ALU.max))
            then(nc.vector.memset(starts[:], 0.0))
            if first:
                then(nc.vector.memset(starts[:, 1:2], float(TT)))
            for e in range(TE):
                then(nc.vector.tensor_tensor(starts[:, first + e + 1:first + e + 2], starts[:, first + e:first + e + 1], tiles[:, e:e + 1], ALU.add))
            then(nc.vector.tensor_scalar(plan.bounds[:], starts[:], -float(MIN_TILES), None, ALU.add))
            dve.wait_ge(S("placed"), TE * TT)
            for g in range(2):
                half = slice(4 * g, 4 * g + 4)
                then(nc.vector.tensor_copy(slot_id[:, half], psT[g][:, :, 1]))
                then(nc.vector.scalar_tensor_tensor(slot_id[:, half], psT[g][:, :, 0], 128.0, slot_id[:, half], ALU.mult, ALU.add))
                out = plan.weight[:, first + 4 * g:first + 4 * g + 4]
                then(nc.vector.tensor_copy(out, psT[g][:, :, 2]))
                then(nc.vector.tensor_tensor(out, psT[g][:, :, 3], out, ALU.add))
            then(nc.vector.tensor_scalar(empty[:], slot_id[:], 0.0, None, ALU.is_equal))
            then(nc.vector.scalar_tensor_tensor(slot_id[:], empty[:], dummy_row[:, 0:1], slot_id[:], ALU.mult, ALU.add))
            then(nc.vector.tensor_scalar(plan.index[:, first:], slot_id[:], -1.0, None, ALU.add))


MIN_TILES = 2


class Plan:

    def __init__(self, nc, ctx, layer, first):
        self.first = first
        self.experts = first + TE
        self.index = ctx.enter_context(nc.sbuf_tensor(f"plan{layer}_index", [128, self.experts, TOK_TILES], I32))
        self.weight = ctx.enter_context(nc.sbuf_tensor(f"plan{layer}_weight", [128, self.experts, TOK_TILES], F32))
        self.bounds = ctx.enter_context(nc.sbuf_tensor(f"plan{layer}_bounds", [1, self.experts + 1], I32))


def build_experts(nc, io, x_rows, acc_rows, plan, layer):
    gated = layer == 0
    NE = plan.experts
    HID = 512 if gated else 1024
    HC = HID // 128
    UP = DC * HID
    W = UP * (2 if gated else 1) + HC * D
    PARTS = HC // 2
    NB = 2 if gated else 4
    with ExitStack() as ctx:
        def sb(name, shape, dt=F32):
            return ctx.enter_context(nc.sbuf_tensor(f"e{layer}_" + name, shape, dt))

        S = Sems(nc, f"e{layer}")
        ctx.callback(S.clear)
        eye = sb("eye", [128, 128])
        w_stage = sb("w_stage", [128, W])
        w_hl = sb("w_hl", [128, 2, 2, W], F16)
        x = sb("x", [128, D])
        xt_hl = sb("xt_hl", [128, 2, DC, 128], F16)
        gate = sb("gate", [128, HC, 128])
        hidden = sb("hidden", [128, HC, 128])
        hid_hl = sb("hid_hl", [128, 2, HC, 128], F16)
        y = sb("y", [128, D])
        y_sum = sb("y_sum", [128, D])
        slot_w = sb("slot_w", [128, 1])
        idx = [sb(f"idx{n}", [128, 1], I32) for n in range(3)]
        if not gated:
            b1 = sb("b1", [128, 2, HC])
            b2 = sb("b2", [128, 2, D])
        psX = ctx.enter_context(nc.psum_tensor(f"e{layer}_psX", [128, DC, 128], F32))
        psH = [ctx.enter_context(nc.psum_tensor(f"e{layer}_psH{n}", [128, 2 if gated else 1, 2, 128], F32)) for n in range(NB)]
        psY = ctx.enter_context(nc.psum_tensor(f"e{layer}_psY", [128, D], F32))

        def up_w(b, a, z, c, m):
            at = z * UP + c * HID + m * 128
            return w_hl[:, b, a, at:at + 128]

        def down_w(b, a, m):
            at = W - HC * D + m * D
            return w_hl[:, b, a, at:at + D]

        def tiles_before(eng, n):
            return eng.value_load(plan.bounds[0:1, bass.ds(n, 1)], min_val=0, max_val=NE * TOK_TILES - MIN_TILES) + MIN_TILES

        def over_experts(eng, tile, finish):
            def expert(n, b):
                lo = 0 if isinstance(n, int) and n == 0 else tiles_before(eng, n)
                hi = tiles_before(eng, n + 1)
                tile(lo, n, lo, b, 1 - b, True)
                with eng.Fori(lo + 1, hi) as T:
                    tile(T, n, lo, b, b, False)
                return hi

            last = expert(0, 0)
            with eng.Fori(1, 7, 2) as n:
                expert(n, 1)
                expert(n + 1, 0)
            for n in range(7, NE):
                last = expert(n, n % 2)
            if finish:
                finish(last, (NE - 1) % 2)

        def column(T, n, lo):
            if isinstance(T, int):
                return T
            return nc.s_assert_within(n * TOK_TILES + T - lo, 0, NE * TOK_TILES - 1,
                                      skip_runtime_bounds_check_because="an expert has at most TOK_TILES tiles")

        SPLIT = 4
        piece = lambda k: slice(k * W // SPLIT, (k + 1) * W // SPLIT)
        block = ctx.enter_context(nc.Block())

        @block.sync
        def _(sp):
            sp.dma_start(eye[:], io["eye_f"]).then_inc(S("eye_in"), 16)
            sp.dma_start(w_stage[:], io[f"experts{layer}"][0]).then_inc(S("w_in"), 16)
            if not gated:
                for n in range(2):
                    sp.dma_start(b1[:, n], io["b1"][n]).then_inc(S(f"b_in{n}"), 16)
                    sp.dma_start(b2[:, n], io["b2"][n].broadcast_to([128, D])).then_inc(S(f"b_in{n}"), 16)

            def load(n, b):
                sp.wait_ge(S("w_low"), n * SPLIT)
                sp.wait_ge(S("w_high"), n * SPLIT)
                sp.dma_start(w_stage[:], io[f"experts{layer}"][bass.ds(n, 1)].rearrange("a p w -> (a p) w")).then_inc(S("w_in"), 16)
                if not gated and not (isinstance(n, int) and n < 2):
                    lo = tiles_before(sp, n - 1)
                    sp.wait_ge(S("y"), lo + 1)
                    sp.dma_start(b1[:, b], io["b1"][bass.ds(n, 1)].rearrange("a p c -> (a p) c")).then_inc(S(f"b_in{b}"), 16)
                    sp.dma_start(b2[:, b], io["b2"][bass.ds(n, 1)].rearrange("a o d -> (a o) d").broadcast_to([128, D])).then_inc(S(f"b_in{b}"), 16)

            load(1, 1)
            with sp.Fori(2, NE - 1, 2) as n:
                load(n, 0)
                load(n + 1, 1)
            if NE % 2:
                load(NE - 1, 0)

        @block.tensor
        def _(pe):
            pe.wait_ge(S("eye_in"), 16)

            def second(T, b):
                wait(pe, S("y_sum"), T)
                for m in range(HC):
                    if m % 2 == 0:
                        pe.wait_ge(S("hid_low"), T * PARTS + m // 2 + 1)
                    for a, z in ((0, 0), (0, 1), (1, 0)):
                        ins = nc.tensor.matmul(psY[:], hid_hl[:, a, m], down_w(b, z, m),
                                               start=m == 0 and (a, z) == (0, 0), stop=m == HC - 1 and a == 1)
                ins.then_inc(S("second"), 1)

            def tile(T, n, lo, b, b_prev, is_first):
                start = isinstance(T, int)
                pe.wait_ge(S("gathered"), T * 16 + 16)
                wait(pe, S("xt_low"), T)
                for c in range(DC):
                    ins = nc.tensor.transpose(psX[:, c], x[:, c * 128:(c + 1) * 128], eye[:])
                ins.then_inc(S("turned"), 1)
                if not start:
                    second(T - 1, b_prev)
                if is_first:
                    pe.wait_ge(S("w_low"), n * SPLIT + SPLIT)
                pe.wait_ge(S("xt_low"), T + 1)
                for k in range(PARTS):
                    if not (start and k < NB):
                        pe.wait_ge(S("hid"), T * PARTS + k + 1 - NB)
                    for mm in range(2):
                        for z in range(2 if gated else 1):
                            for i, (a, r, c) in enumerate((a, r, c) for c in range(DC) for a, r in ((0, 0), (0, 1), (1, 0))):
                                ins = nc.tensor.matmul(psH[k % NB][:, z, mm], up_w(b, a, z, c, 2 * k + mm), xt_hl[:, r, c],
                                                       start=i == 0, stop=i == 3 * DC - 1)
                    ins.then_inc(S("first"), 1)

            over_experts(pe, tile, lambda last, b: second(last - 1, b))

        @block.scalar
        def _(act):
            act.wait_ge(S("w_in"), 16)
            for k in range(SPLIT):
                nc.scalar.activation(w_hl[:, 0, 0, piece(k)], w_stage[:, piece(k)], ACT.Copy, scale=WS).then_inc(S("w_high"), 1)

            def split(n, lo, b, k):
                if k == 0:
                    act.wait_ge(S("w_in"), n * 16 + 32)
                    wait(act, S("second"), lo)
                nc.scalar.activation(w_hl[:, 1 - b, 0, piece(k)], w_stage[:, piece(k)], ACT.Copy, scale=WS).then_inc(S("w_high"), 1)

            def tile(T, n, lo, b, b_prev, is_first):
                start = isinstance(T, int)
                more = is_first and not (isinstance(n, int) and n == NE - 1)
                act.wait_ge(S("turned"), T + 1)
                wait(act, S("first"), T * PARTS)
                nc.scalar.activation(xt_hl[:, 0], psX[:], ACT.Copy).then_inc(S("xt_high"), 1)
                if is_first and not gated:
                    if start:
                        act.wait_ge(S("b_in0"), 32)
                    else:
                        act.wait_ge(S(f"b_in{b}"), (n // 2 + 1) * 32 if isinstance(n, int) else (n * 16 + (32 if b == 0 else 16)))
                for k in range(PARTS):
                    act.wait_ge(S("first"), T * PARTS + k + 1)
                    if gated:
                        wait(act, S("hid"), (T - 1) * PARTS + k + 1 if not start else 0)
                        nc.scalar.activation(gate[:, 2 * k:2 * k + 2], psH[k % NB][:, 0], ACT.Silu, scale=1.0 / WS).then_inc(S("gate"), 1)
                    else:
                        wait(act, S("hid_low"), (T - 1) * PARTS + k + 1 if not start else 0)
                        for mm in range(2):
                            m = 2 * k + mm
                            ins = nc.scalar.activation(hidden[:, m], psH[k % NB][:, 0, mm], ACT.Gelu, scale=1.0 / WS, bias=b1[:, b, m:m + 1])
                        ins.then_inc(S("hid"), 1)
                    if more and not gated:
                        split(n, lo, b, k)
                if gated:
                    for k in range(PARTS):
                        act.wait_ge(S("hid"), T * PARTS + k + 1)
                        wait(act, S("second"), T)
                        nc.scalar.activation(hid_hl[:, 0, 2 * k:2 * k + 2], hidden[:, 2 * k:2 * k + 2], ACT.Copy).then_inc(S("hid_high"), 1)
                        if more:
                            split(n, lo, b, 2 * k)
                            split(n, lo, b, 2 * k + 1)

            over_experts(act, tile, None)

        @block.gpsimd
        def _(pool):
            nc.gpsimd.memset(y[:], 0.0).then_inc(S("y"), 1)
            nc.gpsimd.iota(idx[1][:], [[0, 1]], base=TOKENS, channel_multiplier=1).then_inc(S("idx"), 1)
            nc.gpsimd.iota(idx[0][:], [[0, 1]], base=TOKENS, channel_multiplier=1).then_inc(S("idx"), 1)
            pool.wait_ge(S("y"), 1)

            def shift(T):
                pool.wait_ge(S("idx"), T * 3 + 2)
                wait_alone(pool, S, "scattered", T * 16)
                nc.gpsimd.tensor_copy(idx[2][:], idx[1][:]).then_inc(S("idx"), 1)
                wait_alone(pool, S, "idx", T * 3 + 3)
                nc.gpsimd.tensor_copy(idx[1][:], idx[0][:]).then_inc(S("idx"), 1)
                wait_alone(pool, S, "idx", T * 3 + 4)

            def scatter(T):
                wait_alone(pool, S, "y", T)
                nc.gpsimd.indirect_dma_start(out=acc_rows, out_offset=bass.IndirectOffsetOnAxis(ap=idx[2][:, 0:1], axis=0), in_=y[:],
                                             in_offset=None, compute_op=ALU.add).then_inc(S("scattered"), 16)

            def tile(T, n, lo, b, b_prev, is_first):
                col = column(T, n, lo)
                wait(pool, S("turned"), T)
                shift(T)
                nc.gpsimd.tensor_copy(idx[0][:], plan.index[:].rearrange("p n c -> p (n c)")[:, bass.ds(col, 1)]).then_inc(S("idx"), 1)
                wait_alone(pool, S, "idx", T * 3 + 5)
                nc.gpsimd.indirect_dma_start(out=x[:], out_offset=None, in_=x_rows,
                                             in_offset=bass.IndirectOffsetOnAxis(ap=idx[0][:, 0:1], axis=0)).then_inc(S("gathered"), 16)
                scatter(T)

            def finish(last, b):
                shift(last)
                scatter(last)
                pool.wait_ge(S("scattered"), last * 16 + 16)
                wait_alone(pool, S, "y", last + 1)
                nc.gpsimd.indirect_dma_start(out=acc_rows, out_offset=bass.IndirectOffsetOnAxis(ap=idx[1][:, 0:1], axis=0), in_=y[:],
                                             in_offset=None, compute_op=ALU.add).then_inc(S("scattered"), 16)
                pool.wait_ge(S("scattered"), last * 16 + 32)

            over_experts(pool, tile, finish)

        @block.vector
        def _(dve):
            dve.wait_ge(S("w_in"), 16)
            for k in range(SPLIT):
                dve.wait_ge(S("w_high"), k + 1)
                nc.vector.scalar_tensor_tensor(w_hl[:, 0, 1, piece(k)], w_stage[:, piece(k)], WS, w_hl[:, 0, 0, piece(k)],
                                               ALU.mult, ALU.subtract).then_inc(S("w_low"), 1)

            def split(n, b, k):
                dve.wait_ge(S("w_high"), n * SPLIT + SPLIT + k + 1)
                nc.vector.scalar_tensor_tensor(w_hl[:, 1 - b, 1, piece(k)], w_stage[:, piece(k)], WS, w_hl[:, 1 - b, 0, piece(k)],
                                               ALU.mult, ALU.subtract).then_inc(S("w_low"), 1)

            def sum_rows(T, b):
                dve.wait_ge(S("slot_w"), T + 1)
                dve.wait_ge(S("second"), T + 1)
                if gated:
                    dve.wait_ge(S("scattered"), T * 16 + 32)
                    ins = nc.vector.tensor_scalar(y[:], psY[:], slot_w[:, 0:1], 1.0 / (WS * WS), ALU.mult, ALU.mult)
                    ins.then_inc(S("y_sum"), 1)
                    dve.wait_ge(S("y_sum"), T + 1)
                    ins = nc.vector.tensor_copy(y_sum[:, 0:1], slot_w[:]).then_inc(S("y"), 1)
                else:
                    nc.vector.scalar_tensor_tensor(y_sum[:], psY[:], 1.0 / WS, b2[:, b], ALU.mult, ALU.add).then_inc(S("y_sum"), 1)
                    dve.wait_ge(S("y_sum"), T + 1)
                    dve.wait_ge(S("scattered"), T * 16 + 32)
                    nc.vector.tensor_scalar(y[:], y_sum[:], slot_w[:, 0:1], None, ALU.mult).then_inc(S("y"), 1)

            def tile(T, n, lo, b, b_prev, is_first):
                start = isinstance(T, int)
                more = is_first and not (isinstance(n, int) and n == NE - 1)
                col = column(T, n, lo)
                dve.wait_ge(S("xt_high"), T + 1)
                nc.vector.tensor_tensor(xt_hl[:, 1], psX[:], xt_hl[:, 0], ALU.subtract).then_inc(S("xt_low"), 1)
                if not start:
                    sum_rows(T - 1, b_prev)
                    dve.wait_ge(S("y"), T + 1)
                nc.vector.tensor_copy(slot_w[:], plan.weight[:].rearrange("p n c -> p (n c)")[:, bass.ds(col, 1)]).then_inc(S("slot_w"), 1)
                for k in range(PARTS):
                    part = slice(2 * k, 2 * k + 2)
                    if gated:
                        dve.wait_ge(S("gate"), T * PARTS + k + 1)
                        wait(dve, S("hid_low"), (T - 1) * PARTS + k + 1 if not start else 0)
                        nc.vector.tensor_tensor(hidden[:, part], psH[k % NB][:, 1], gate[:, part], ALU.mult).then_inc(S("hid"), 1)
                for k in range(PARTS):
                    part = slice(2 * k, 2 * k + 2)
                    if not gated:
                        dve.wait_ge(S("hid"), T * PARTS + k + 1)
                        wait(dve, S("second"), T)
                        nc.vector.tensor_copy(hid_hl[:, 0, part], hidden[:, part]).then_inc(S("hid_high"), 1)
                    dve.wait_ge(S("hid_high"), T * PARTS + k + 1)
                    nc.vector.tensor_tensor(hid_hl[:, 1, part], hidden[:, part], hid_hl[:, 0, part], ALU.subtract).then_inc(S("hid_low"), 1)
                    if more:
                        for kk in range(k * SPLIT // PARTS, (k + 1) * SPLIT // PARTS):
                            split(n, b, kk)

            def finish(last, b):
                sum_rows(last - 1, b)

            over_experts(dve, tile, finish)
def build_attention1(nc, io, acc_rows, x3):
    NH, DK, DL, DR = 8, 128, 32, 32
    QK = DL + DR + 1
    CAT = 2 * DL + DR
    QS = 4.0
    TOP = 64
    with ExitStack() as ctx:
        def sb(name, shape, dt=F32):
            return ctx.enter_context(nc.sbuf_tensor("a1_" + name, shape, dt))

        def ps(name, shape, dt=F32):
            return ctx.enter_context(nc.psum_tensor("a1_" + name, shape, dt))

        S = Sems(nc, "a1")
        ctx.callback(S.clear)
        uq_t = sb("uq_t", [DK, NH, DL + 1])
        uk_t = sb("uk_t", [DK, NH, DL + 1])
        uv_t = sb("uv_t", [DK, NH, DL])
        wo = sb("wo", [DK, NH, D])
        buv = sb("buv", [DK, NH])
        buv_wide = sb("buv_wide", [DK, NH, 128])
        bo_rows = sb("bo_rows", [128, D])
        qr = sb("qr", [TOP + DL + 1, NH, DR])
        w_cat = sb("w_cat", [128, DC, CAT])
        b_cat = sb("b_cat", [CAT, 1])
        b_kv4 = sb("b_kv4", [128, 1])
        m_f = sb("m_f", [TOP + DL + 1, NH, QK])
        n_f = sb("n_f", [128, DC, D])
        out_bias = sb("out_bias", [128, D])
        eye = sb("eye", [128, 128])
        eye16 = sb("eye16", [128, 128], F16)
        half_power = sb("half_power", [128, 1])
        w_cat_hl = sb("w_cat_hl", [128, 2, DC, CAT], F16)
        m_hl = sb("m_hl", [TOP + DL + 1, 2, NH, QK], F16)
        n_hl = sb("n_hl", [128, 2, DC, D], F16)
        b_cat_ws = sb("b_cat_ws", [CAT, 1])
        b_kv_ws = sb("b_kv_ws", [128, 1])

        x = sb("x", [128, 2, D])
        stats = sb("stats", [128, 6])
        moments = sb("moments", [128, 2])
        var_eps = sb("var_eps", [128, 1])
        rstd = sb("rstd", [128, 1])
        h2 = sb("h2", [128, 2, D])
        h2_bias = sb("h2_bias", [128, 4, D])
        ht_hl = sb("ht_hl", [128, 2, 2, DC, 128], F16)
        k_hl = sb("k_hl", [QK, 4, 2, PAIR], F16)
        c_hl = sb("c_hl", [TOP + DL + 1, 2, 2, PAIR], F16)
        v_hl = sb("v_hl", [128, 4, 2, DL], F16)
        q_hl = sb("q_hl", [QK, 2, 2, 2, NH, SEQ], F16)
        row_max = sb("row_max", [TRIO, 6])
        row_sum = sb("row_sum", [TRIO, 6])
        row_inv = sb("row_inv", [TRIO, 6])
        prob = sb("prob", [TRIO, 2, 3, 2, SEQ])
        p_hl = sb("p_hl", [TRIO, 2, 2, 3, 2, SLOT], F16)
        pt_hl = sb("pt_hl", [128, 2, NH, SEQ], F16)
        ctx_hl = sb("ctx_hl", [128, 2, DC, 2, SLOT], F16)
        r = sb("r", [128, D])
        stats2 = sb("stats2", [128, 6])
        moments2 = sb("moments2", [128, 2])
        var_eps2 = sb("var_eps2", [128, 1])
        rstd2 = sb("rstd2", [128, 1])
        h3 = sb("h3", [128, 2, D])

        psX = ps("psX", [128, DC, 128])
        psC = ps("psC", [CAT, PAIR + DL])
        psVO = ps("psVO", [128, 512])
        psV = psVO[:, 0:DL]
        psO = psVO[:, 256:256 + D]
        psQ = [ps("psQ0", [QK, 2, NH // 2, SEQ]), ps("psQ1", [QK, 2, NH // 2, SEQ])]
        psST = ps("psST", [128, 512])
        psS = psST[0:TRIO, 0:6 * SEQ].rearrange("r (t i k) -> r t i k", t=3, i=2)
        psT = ps("psT", [128, 2, 3, 112], F16)
        psM = [ps("psM", [128, 512])]
        psA = [psM[0][:, 0:2 * SEQ].rearrange("p (c q) -> p c q", c=DC), psX[:].rearrange("p c n -> p (c n)")[:, 0:2 * SEQ].rearrange("p (c q) -> p c q", c=DC)]

        N_SETUP = 12
        run = lambda eng, body: run_steps(eng, PAIRS, 4, body)
        block = ctx.enter_context(nc.Block())

        @block.sync
        def _(sp):
            for dst, name in ((uq_t[:], "uq_t"), (uk_t[:], "uk_t"), (uv_t[:], "uv_t"), (wo[:], "wo1"), (buv[:], "buv"),
                              (qr[TOP:TOP + DL + 1], "qr"), (w_cat[:], "w_cat"), (b_cat[:], "b_cat"), (b_kv4[:], "b_kv4"),
                              (eye[:], "eye_f"), (eye16[:], "eye")):
                sp.dma_start(dst, io[name]).then_inc(S("setup_in"), 16)
            sp.dma_start(bo_rows[:], io["bo1"].broadcast_to([128, D])).then_inc(S("setup_in"), 16)
            sp.dma_start(x3[TOKENS:ROWS, :], io["zero_rows"]).then_inc(S("dummy_out"), 16)
            sp.wait_ge(S("zeroed"), 4)

            def step(st):
                if st.active(0):
                    p, b, hp, _ = st.item(0)
                    wait(sp, S("h2"), p - 1)
                    for i in range(2):
                        sp.dma_start(x[i * SLOT:i * SLOT + SEQ, b], acc_rows[bass.ds(p * PAIR + i * SEQ, SEQ), :]).then_inc(S(f"x_in{b}"), 16)
                if st.active(4):
                    p, b, hp, _ = st.item(4)
                    wait(sp, S("h3"), p + 1)
                    for i in range(2):
                        sp.dma_start(x3[bass.ds(p * PAIR + i * SEQ, SEQ), :], h3[i * SLOT:i * SLOT + SEQ, b]).then_inc(S(f"h3_out{b}"), 16)

            run(sp, step)
            sp.wait_ge(S("dummy_out"), 16)
            for b in range(2):
                sp.wait_ge(S(f"h3_out{b}"), 32 * (PAIRS // 2))

        @block.tensor
        def _(pe):
            def products(out, left, right, chunks):
                todo = [(a, b, c) for c in range(chunks) for a, b in ((0, 0), (0, 1), (1, 0))]
                for n, (a, b, c) in enumerate(todo):
                    ins = nc.tensor.matmul(out, left(a, c), right(b, c), start=n == 0, stop=n == len(todo) - 1)
                return ins

            pe.wait_ge(S("setup_in"), 16 * N_SETUP)
            pe.wait_ge(S("buv_wide"), 1)
            for h in range(NH):
                ins = nc.tensor.matmul(psVO[TOP:TOP + DL + 1, 33 * h:33 * h + 33], uq_t[:, h], uk_t[:, h], start=True, stop=True)
            ins.then_inc(S("joined"), 1)
            for h in range(NH):
                ins = nc.tensor.matmul((psM[0], psST)[h // 4][32 * (h % 4):32 * (h % 4) + 32, 0:D], uv_t[:, h], wo[:, h], start=True, stop=True)
            ins.then_inc(S("joined"), 1)
            for h in range(NH):
                ins = nc.tensor.matmul(psX[:].rearrange("p c n -> p (c n)"), buv_wide[:, h], wo[:, h], start=h == 0, stop=h == NH - 1)
            ins.then_inc(S("joined"), 1)
            pe.wait_ge(S("w_ready"), 6)
            pe.wait_ge(S("ones"), 4)
            pe.wait_ge(S("zeroed"), 4)

            def turn(st):
                p, b, _, _ = st.item(1)
                pe.wait_ge(S("h2"), p + 1)
                wait(pe, S("ht_low"), p)
                wait(pe, S("ctx_low"), 2 * (p - 3))
                for c in range(DC):
                    ins = nc.tensor.transpose(psX[:, c], h2[:, b, c * 128:(c + 1) * 128], eye[:])
                ins.then_inc(S("turned"), 1)

            def latents(st):
                p, b, _, _ = st.item(1)
                pe.wait_ge(S("ht_high"), p + 1)
                pe.wait_ge(S("ht_low"), p + 1)
                wait(pe, S("c_low"), p)
                by_image = lambda a, c: ht_hl[:, b, a, c].rearrange("p (i q) -> p i q", i=2)[:, :, 0:SEQ]
                products(psC[:, 0:PAIR].rearrange("p (i q) -> p i q", i=2), lambda a, c: w_cat_hl[:, a, c], by_image, DC).then_inc(S("cat"), 1)
                wait(pe, S("v_low"), p)
                wait(pe, S("r"), p - 3)
                products(psV, lambda a, c: ht_hl[:, b, a, c], lambda a, c: w_cat_hl[:, a, c, 0:DL], DC).then_inc(S("v"), 1)

            def queries(st):
                p, b, _, _ = st.item(2)
                pe.wait_ge(S("c_high"), p + 1)
                pe.wait_ge(S("c_low"), p + 1)
                wait(pe, S("q_low"), 2 * p)
                for h in range(NH):
                    ins = products(psQ[h // 4][:, :, h % 4], lambda a, c: m_hl[TOP:TOP + DL + 1, a, h],
                                   lambda a, c: c_hl[TOP:TOP + DL + 1, b, a].rearrange("r (i q) -> r i q", i=2), 1)
                    if h % 4 == 3:
                        ins.then_inc(S("q"), 1)

            def scores(st):
                p, b, _, b4 = st.item(3)
                pe.wait_ge(S("q_high"), 2 * p + 2)
                pe.wait_ge(S("q_low"), 2 * p + 2)
                wait(pe, S("shifted"), p)
                for t in range(3):
                    h = min(3 * t, NH - 3)
                    for i in range(2):
                        ins = products(psS[:, t, i], lambda a, c: q_hl[:, b, a, i, h:h + 3].rearrange("r h q -> r (h q)"),
                                       lambda a, c: k_hl[:, b4, a, i * SEQ:(i + 1) * SEQ], 1)
                ins.then_inc(S("scored"), 1)

            def transpose_probs(st):
                p, b, _, _ = st.item(4)
                pe.wait_ge(S("p_high"), p + 1)
                pe.wait_ge(S("p_low"), p + 1)
                wait(pe, S("pt_copied"), 2 * p)
                for a in range(2):
                    for t in range(3):
                        ins = nc.tensor.transpose(psT[:, a, t, 0:TRIO], p_hl[:, b, a, t].rearrange("r i k -> r (i k)"), eye16[0:TRIO, 0:TRIO])
                ins.then_inc(S("pt"), 1)

            def mix(st):
                p, b, _, b4 = st.item(4)
                pe.wait_ge(S("pt_copied"), 2 * p + 2)
                wait(pe, S("ctx_low"), 2 * p)
                wait_alone(pe, S, "ht_low", min(p + 4, PAIRS) if isinstance(p, int) else p + 4)
                for i in range(2):
                    rows = slice(i * SLOT, i * SLOT + SEQ)
                    for h in range(NH):
                        j, c = h % 4, h // 4
                        for n, (a, z) in enumerate(((0, 0), (0, 1), (1, 0))):
                            ins = nc.tensor.matmul(psA[i][32 * j:32 * j + 32, c], v_hl[rows, b4, z], pt_hl[rows, a, h],
                                                   start=n == 0, stop=n == 2)
                    ins.then_inc(S("mixed"), 1)

            def output(st):
                p, b, _, _ = st.item(4)
                pe.wait_ge(S("ctx_high"), 2 * p + 2)
                pe.wait_ge(S("ctx_low"), 2 * p + 2)
                wait(pe, S("r"), p)
                wait(pe, S("v_low"), min(p + 4, PAIRS) if isinstance(p, int) else p + 4)
                products(psO, lambda a, c: ctx_hl[:, a, c], lambda a, c: n_hl[:, a, c], DC).then_inc(S("projected"), 1)

            def step(st):
                if st.active(1):
                    turn(st)
                if st.active(3):
                    scores(st)
                if st.active(4):
                    transpose_probs(st)
                if st.active(1):
                    latents(st)
                if st.active(2):
                    queries(st)
                if st.active(4):
                    mix(st)
                    output(st)

            run(pe, step)

        @block.scalar
        def _(act):
            act.wait_ge(S("setup_in"), 16 * N_SETUP)
            nc.scalar.activation(w_cat_hl[:, 0], w_cat[:], ACT.Copy, scale=WS).then_inc(S("w_high"), 1)
            act.wait_ge(S("m_ready"), 2)
            nc.scalar.activation(m_hl[TOP:TOP + DL + 1, 0], m_f[TOP:TOP + DL + 1], ACT.Copy, scale=16.0).then_inc(S("w_high"), 1)
            act.wait_ge(S("n_ready"), 2)
            nc.scalar.activation(n_hl[:, 0], n_f[:], ACT.Copy, scale=WS).then_inc(S("w_high"), 1)

            def step(st):
                if st.active(3):
                    p, b, _, _ = st.item(3)
                    act.wait_ge(S("shifted"), p + 1)
                    nc.scalar.activation(prob[:, b], prob[:, b], ACT.Exp, scale=1.0 / (QS * WS * (DK + DR) ** 0.5)).then_inc(S("exp"), 1)
                if st.active(1):
                    p, b, _, b4 = st.item(1)
                    act.wait_ge(S("turned"), p + 1)
                    wait(act, S("v"), p - 1)
                    nc.scalar.activation(ht_hl[:, b, 0], psX[:], ACT.Copy).then_inc(S("ht_high"), 1)
                if st.active(4):
                    p, b, _, _ = st.item(4)
                    act.wait_ge(S("pt"), p + 1)
                    wait(act, S("mixed"), 2 * p)
                    nc.scalar.activation(pt_hl[:, :, 0:6].rearrange("k a (t h) q -> k a t (h q)", t=2), psT[:, :, 0:2, 0:TRIO], ACT.Copy).then_inc(S("pt_copied"), 1)
                    nc.scalar.activation(pt_hl[:, :, 6:8].rearrange("k a h q -> k a (h q)"), psT[:, :, 2, SEQ:TRIO], ACT.Copy).then_inc(S("pt_copied"), 1)
                if st.active(1):
                    p, b, _, b4 = st.item(1)
                    act.wait_ge(S("cat"), p + 1)
                    wait(act, S("scored"), p - 3)
                    wait(act, S("q"), 2 * (p - 1))
                    nc.scalar.activation(k_hl[0:TOP, b4, 0], psC[0:TOP, 0:PAIR], ACT.Identity, bias=b_cat_ws[0:TOP, 0:1])
                    nc.scalar.activation(c_hl[TOP:CAT, b, 0], psC[TOP:CAT, 0:PAIR], ACT.Identity, bias=b_cat_ws[TOP:CAT, 0:1]).then_inc(S("c_high"), 1)
                    act.wait_ge(S("v"), p + 1)
                    wait(act, S("mixed"), 2 * (p - 3))
                    nc.scalar.activation(v_hl[:, b4, 0], psV, ACT.Copy).then_inc(S("v_high"), 1)
                if st.active(2):
                    p, b, _, _ = st.item(2)
                    wait(act, S("scored"), p - 1)
                    for g in range(2):
                        act.wait_ge(S("q"), 2 * p + g + 1)
                        nc.scalar.activation(q_hl[:, b, 0, :, 4 * g:4 * g + 4], psQ[g][:], ACT.Copy, scale=QS / (16.0 * WS)).then_inc(S("q_high"), 1)
                if st.active(4):
                    p, b, _, _ = st.item(4)
                    wait(act, S("projected"), p)
                    for i in range(2):
                        act.wait_ge(S("mixed"), 2 * p + 1 + i)
                        nc.scalar.activation(ctx_hl[:, 0, :, i, 0:SEQ], psA[i], ACT.Identity, bias=b_kv_ws[:, 0:1]).then_inc(S("ctx_high"), 1)
                if st.active(3):
                    p, b, _, _ = st.item(3)
                    act.wait_ge(S("prob"), p + 1)
                    wait(act, S("pt"), p - 1)
                    nc.scalar.activation(p_hl[:, b, 0, :, :, 0:SEQ], prob[:, b], ACT.Copy).then_inc(S("p_high"), 1)

            run(act, step)

        @block.gpsimd
        def _(pool):
            for t, v in ((p_hl, 0.0), (ctx_hl, 0.0), (x, 0.0), (half_power, -0.5)):
                nc.gpsimd.memset(t[:], v).then_inc(S("zeroed"), 1)
            pool.wait_ge(S("zeroed"), 4)

            def step(st):
                if st.active(0):
                    p, b, _, b4 = st.item(0)
                    pool.wait_ge(S("var_eps"), p + 1)
                    nc.gpsimd.tensor_tensor(rstd[:], var_eps[:], half_power[:], ALU.pow).then_inc(S("rstd"), 1)
                    pool.wait_ge(S("h2"), p + 1)
                    wait(pool, S("r"), p - 3)
                    if isinstance(p, int) and p == 0:
                        pool.wait_ge(S("w_ready"), 6)
                    nc.gpsimd.tensor_tensor(h2_bias[:, b4], h2[:, b], out_bias[:], ALU.add).then_inc(S("h2_bias"), 1)
                if st.active(3):
                    p, b, _, _ = st.item(3)
                    pool.wait_ge(S("p_high"), p + 1)
                    nc.gpsimd.tensor_tensor(p_hl[:, b, 1, :, :, 0:SEQ], prob[:, b], p_hl[:, b, 0, :, :, 0:SEQ], ALU.subtract).then_inc(S("p_low"), 1)
                if st.active(4):
                    p, b, _, _ = st.item(4)
                    pool.wait_ge(S("var_eps2"), p + 1)
                    nc.gpsimd.tensor_tensor(rstd2[:], var_eps2[:], half_power[:], ALU.pow).then_inc(S("rstd2"), 1)

            run(pool, step)

        @block.vector
        def _(dve):
            hl = lambda t, a: t[:, a].rearrange("p c n -> p (c n)")
            rows = slice(TOP, TOP + DL + 1)
            nc.vector.memset(k_hl[TOP:TOP + 1, :, 1], 0.0).then_inc(S("ones"), 1)
            nc.vector.memset(k_hl[TOP:TOP + 1, :, 0], WS).then_inc(S("ones"), 1)
            nc.vector.memset(c_hl[CAT:CAT + 1, :, 1], 0.0).then_inc(S("ones"), 1)
            nc.vector.memset(c_hl[CAT:CAT + 1, :, 0], WS).then_inc(S("ones"), 1)
            dve.wait_ge(S("setup_in"), 16 * N_SETUP)
            nc.vector.tensor_copy(buv_wide[:], buv[:].unsqueeze(2).broadcast_to([DK, NH, 128])).then_inc(S("buv_wide"), 1)
            dve.wait_ge(S("w_high"), 1)
            nc.vector.scalar_tensor_tensor(hl(w_cat_hl, 1), w_cat[:].rearrange("p c n -> p (c n)"), WS, hl(w_cat_hl, 0), ALU.mult, ALU.subtract).then_inc(S("w_ready"), 1)
            nc.vector.tensor_scalar(b_cat_ws[:], b_cat[:], WS, None, ALU.mult).then_inc(S("w_ready"), 1)
            nc.vector.tensor_scalar(b_kv_ws[:], b_kv4[:], WS, None, ALU.mult).then_inc(S("w_ready"), 1)
            dve.wait_ge(S("joined"), 1)
            joined = psVO[rows, 0:NH * (DL + 1)].rearrange("r (h n) -> r h n", h=NH)
            nc.vector.tensor_copy(m_f[rows, :, 0:DL], joined[:, :, 0:DL])
            nc.vector.tensor_copy(m_f[rows, :, QK - 1:QK], joined[:, :, DL:DL + 1]).then_inc(S("m_ready"), 1)
            nc.vector.tensor_copy(m_f[rows, :, DL:DL + DR], qr[rows]).then_inc(S("m_ready"), 1)
            dve.wait_ge(S("joined"), 3)
            nc.vector.tensor_copy(n_f[:, 0], psM[0][:, 0:D]).then_inc(S("n_ready"), 1)
            nc.vector.tensor_copy(n_f[:, 1], psST[:, 0:D]).then_inc(S("n_ready"), 1)
            nc.vector.tensor_tensor(out_bias[:], psX[:].rearrange("p c n -> p (c n)"), bo_rows[:], ALU.add).then_inc(S("w_ready"), 1)
            dve.wait_ge(S("w_high"), 3)
            dve.wait_ge(S("m_ready"), 2)
            dve.wait_ge(S("n_ready"), 2)
            nc.vector.scalar_tensor_tensor(m_hl[rows, 1].rearrange("r h n -> r (h n)"), m_f[rows].rearrange("r h n -> r (h n)"), 16.0,
                                           m_hl[rows, 0].rearrange("r h n -> r (h n)"), ALU.mult, ALU.subtract).then_inc(S("w_ready"), 1)
            nc.vector.scalar_tensor_tensor(hl(n_hl, 1), n_f[:].rearrange("p c n -> p (c n)"), WS, hl(n_hl, 0), ALU.mult, ALU.subtract).then_inc(S("w_ready"), 1)

            def normalise(p, src, stats, moments, var_eps, rstd, out, name, n):
                nc.vector.bn_stats(stats[:], src).then_inc(S("stats" + n), 1)
                wait_alone(dve, S, "stats" + n, p + 1)
                nc.vector.bn_aggr(moments[:], stats[:]).then_inc(S("moments" + n), 1)
                dve.wait_ge(S("moments" + n), p + 1)
                nc.vector.tensor_scalar(var_eps[:], moments[:, 1:2], EPS, None, ALU.add).then_inc(S("var_eps" + n), 1)
                dve.wait_ge(S("rstd" + n), p + 1)
                nc.vector.tensor_scalar(out, src, moments[:, 0:1], rstd[:, 0:1], ALU.subtract, ALU.mult).then_inc(S(name), 1)

            def step(st):
                if st.active(3):
                    p, b, _, _ = st.item(3)
                    dve.wait_ge(S("scored"), p + 1)
                    flat = psS.rearrange("r t i k -> r (t i) k")
                    nc.vector.tensor_reduce(row_max[:], flat, AX.X, ALU.max).then_inc(S("row_max"), 1)
                    dve.wait_ge(S("row_max"), p + 1)
                    wait(dve, S("p_low"), p - 1)
                    nc.vector.tensor_tensor(prob[:, b].rearrange("r t i k -> r (t i) k"), flat, row_max[:].unsqueeze(2).broadcast_to([TRIO, 6, SEQ]), ALU.subtract).then_inc(S("shifted"), 1)
                if st.active(1):
                    p, b, _, b4 = st.item(1)
                    dve.wait_ge(S("ht_high"), p + 1)
                    nc.vector.tensor_tensor(ht_hl[:, b, 1], psX[:], ht_hl[:, b, 0], ALU.subtract).then_inc(S("ht_low"), 1)
                if st.active(1):
                    p, b, _, b4 = st.item(1)
                    dve.wait_ge(S("c_high"), p + 1)
                    nc.vector.scalar_tensor_tensor(k_hl[0:TOP, b4, 1], psC[0:TOP, 0:PAIR], b_cat_ws[0:TOP, 0:1], k_hl[0:TOP, b4, 0], ALU.add, ALU.subtract)
                    nc.vector.scalar_tensor_tensor(c_hl[TOP:CAT, b, 1], psC[TOP:CAT, 0:PAIR], b_cat_ws[TOP:CAT, 0:1], c_hl[TOP:CAT, b, 0], ALU.add, ALU.subtract).then_inc(S("c_low"), 1)
                    dve.wait_ge(S("v_high"), p + 1)
                    nc.vector.tensor_tensor(v_hl[:, b4, 1], psV, v_hl[:, b4, 0], ALU.subtract).then_inc(S("v_low"), 1)
                if st.active(3):
                    p, b, _, _ = st.item(3)
                    flat = prob[:, b].rearrange("r t i k -> r (t i) k")
                    dve.wait_ge(S("exp"), p + 1)
                    nc.vector.tensor_reduce(row_sum[:], flat, AX.X, ALU.add).then_inc(S("row_sum"), 1)
                    dve.wait_ge(S("row_sum"), p + 1)
                    nc.vector.reciprocal(row_inv[:], row_sum[:]).then_inc(S("row_inv"), 1)
                    dve.wait_ge(S("row_inv"), p + 1)
                    nc.vector.tensor_tensor(flat, flat, row_inv[:].unsqueeze(2).broadcast_to([TRIO, 6, SEQ]), ALU.mult).then_inc(S("prob"), 1)
                if st.active(2):
                    p, b, _, _ = st.item(2)
                    for g in range(2):
                        dve.wait_ge(S("q_high"), 2 * p + g + 1)
                        part = lambda a: q_hl[:, b, a, :, 4 * g:4 * g + 4].rearrange("r i h q -> r i (h q)")
                        nc.vector.scalar_tensor_tensor(part(1), psQ[g][:].rearrange("r i h q -> r i (h q)"), QS / (16.0 * WS), part(0),
                                                       ALU.mult, ALU.subtract).then_inc(S("q_low"), 1)
                if st.active(0):
                    p, b, hp, b4 = st.item(0)
                    dve.wait_ge(S(f"x_in{b}"), 32 * hp + 32)
                    wait(dve, S("turned"), p - 1)
                    wait(dve, S("h2_bias"), p - 1)
                    normalise(p, x[:, b], stats, moments, var_eps, rstd, h2[:, b], "h2", "")
                if st.active(4):
                    p, b, hp, b4 = st.item(4)
                    for i in range(2):
                        dve.wait_ge(S("ctx_high"), 2 * p + 1 + i)
                        nc.vector.scalar_tensor_tensor(ctx_hl[:, 1, :, i, 0:SEQ], psA[i], b_kv_ws[:, 0:1], ctx_hl[:, 0, :, i, 0:SEQ],
                                                       ALU.add, ALU.subtract).then_inc(S("ctx_low"), 1)
                    dve.wait_ge(S("projected"), p + 1)
                    nc.vector.scalar_tensor_tensor(r[:], psO, 1.0 / (WS * WS), h2_bias[:, b4], ALU.mult, ALU.add).then_inc(S("r"), 1)
                    dve.wait_ge(S("r"), p + 1)
                    wait(dve, S(f"h3_out{b}"), 32 * hp)
                    normalise(p, r[:], stats2, moments2, var_eps2, rstd2, h3[:, b], "h3", "2")

            run(dve, step)


def build_final_norm(nc, acc_rows, out_rows):
    with ExitStack() as ctx:
        def sb(name, shape):
            return ctx.enter_context(nc.sbuf_tensor("f_" + name, shape, F32))

        S = Sems(nc, "f")
        ctx.callback(S.clear)
        R = SEQ * 3
        NT = -(-TOKENS // 128)
        size = lambda t: min(128, TOKENS - 128 * t)
        x = sb("x", [128, 4, D])
        y = sb("y", [128, 4, D])
        stats = sb("stats", [128, 4, 6])
        moments = sb("moments", [128, 4, 2])
        var_eps = sb("var_eps", [128, 4])
        rstd = sb("rstd", [128, 4])
        half_power = sb("half_power", [128, 1])
        block = ctx.enter_context(nc.Block())

        @block.sync
        def _(sp):
            for t in range(NT):
                if t >= 4:
                    sp.wait_ge(S("y"), t - 3)
                sp.dma_start(x[0:size(t), t % 4], acc_rows[t * 128:t * 128 + size(t), :]).then_inc(S(f"x_in{t % 4}"), 16)

        @block.scalar
        def _(act):
            for t in range(NT):
                act.wait_ge(S("y"), t + 1)
                act.dma_start(out_rows[t * 128:t * 128 + size(t), :], y[0:size(t), t % 4]).then_inc(S(f"y_out{t % 4}"), 16)
            for b in range(4):
                act.wait_ge(S(f"y_out{b}"), 16 * len(range(b, NT, 4)))

        @block.gpsimd
        def _(pool):
            nc.gpsimd.memset(half_power[:], -0.5).then_inc(S("half_power"), 1)
            pool.wait_ge(S("half_power"), 1)
            for t in range(NT):
                b, n = t % 4, size(t)
                pool.wait_ge(S("var_eps"), t + 1)
                nc.gpsimd.tensor_tensor(rstd[0:n, b:b + 1], var_eps[0:n, b:b + 1], half_power[0:n], ALU.pow).then_inc(S("rstd"), 1)

        @block.vector
        def _(dve):
            def scale(t):
                b, n = t % 4, size(t)
                dve.wait_ge(S("rstd"), t + 1)
                if t >= 4:
                    dve.wait_ge(S(f"y_out{b}"), 16 * (t // 4))
                nc.vector.tensor_scalar(y[0:n, b], x[0:n, b], moments[0:n, b, 0:1], rstd[0:n, b:b + 1], ALU.subtract, ALU.mult).then_inc(S("y"), 1)

            for t in range(NT):
                b, n = t % 4, size(t)
                dve.wait_ge(S(f"x_in{b}"), 16 * (t // 4 + 1))
                nc.vector.bn_stats(stats[0:n, b], x[0:n, b]).then_inc(S("stats"), 1)
                if t >= 1:
                    scale(t - 1)
                dve.wait_ge(S("stats"), t + 1)
                nc.vector.bn_aggr(moments[0:n, b], stats[0:n, b]).then_inc(S("moments"), 1)
                dve.wait_ge(S("moments"), t + 1)
                nc.vector.tensor_scalar(var_eps[0:n, b:b + 1], moments[0:n, b, 1:2], EPS, None, ALU.add).then_inc(S("var_eps"), 1)
            scale(NT - 1)


def build(nc, io, out):
    x1, sum0, x3, sum1 = (nc.dram_tensor(n, (ROWS, D), F32).ap() for n in ("x1", "sum0", "x3", "sum1"))
    build_attention0(nc, io, x1)
    for layer, x, total in ((0, x1, sum0), (1, x3, sum1)):
        if layer == 1:
            build_attention1(nc, io, sum0, x3)
        with ExitStack() as ctx:
            plan = Plan(nc, ctx, layer, 1 if layer == 0 else 0)
            build_routing(nc, io, x, total, plan, layer)
            build_experts(nc, io, x, total, plan, layer)
    build_final_norm(nc, sum1, out)


def lay_out(x, **w):
    import numpy as np

    def feat(v):
        return np.ascontiguousarray(v.reshape(-1, 128).T)

    def rows(m):
        k, n = m.shape
        return np.ascontiguousarray(m.reshape(k // 128, 128, n).transpose(1, 0, 2))

    p = x.reshape(PAIRS, 2, 3, GRID, 16, GRID, 16).transpose(0, 2, 4, 6, 1, 3, 5)
    p = p.reshape(PAIRS, PC, 128, 2 * PATCHES).transpose(0, 2, 1, 3)
    part = np.arange(128)
    a = {
        "patches": p,
        "emb_w": rows(w["L0_tok_W"].T),
        "qkvo_w": np.stack([rows(w[f"L0_attn_W{z}"].T) for z in "qkvo"], axis=1),
        "bias0": np.stack([feat(w["L0_tok_b"])] + [feat(w[f"L0_attn_b{z}"]) for z in "qkv"], axis=1),
        "pos_t": w["L0_tok_pos_embed"][0].T.reshape(DC, 128, SEQ).transpose(1, 0, 2),
        "cls_t": feat(w["L0_tok_cls_token"][0, 0])[:, :, None],
        "bo": w["L0_attn_bo"][None],
        "head_mask": (part[:, None] // 16 == np.arange(8)[None]).astype(np.float32),
        "eye": np.eye(128, dtype=np.float16),
    }

    experts0 = [(w["L0_ffn_Wg_s"], w["L0_ffn_Wu_s"], w["L0_ffn_Wd_s"])]
    experts0 += [(w["L0_ffn_Wg"][e], w["L0_ffn_Wu"][e], w["L0_ffn_Wd"][e]) for e in range(TE)]
    tok = np.arange(TOK_TILES * 128).reshape(TOK_TILES, 128).T
    te = TOK_TILES * TE
    a |= {
        "experts0": np.stack([np.concatenate([rows(m.T).reshape(128, -1) for m in e], axis=1) for e in experts0]),
        "experts1": np.stack([np.concatenate([rows(w["L1_ffn_W1"][e]).reshape(128, -1), rows(w["L1_ffn_W2"][e]).reshape(128, -1)], axis=1)
                              for e in range(TE)]),
        "b1": np.stack([feat(w["L1_ffn_b1"][e]) for e in range(TE)]),
        "b2": w["L1_ffn_b2"][:, None, :],
        "wr0": rows(w["L0_ffn_Wr"].T),
        "wr1": rows(w["L1_ffn_Wr"]),
        "router_bias0": w["L0_ffn_rb"][None],
        "router_bias1": w["L1_ffn_br"][None],
        "eye_f": np.eye(128, dtype=np.float32),
        "below": np.triu(np.ones((128, 128), np.float16), 1),
        "lane": np.broadcast_to(np.arange(128, dtype=np.float16), (128, 128)),
        "place": np.broadcast_to(np.arange(TE, 0, -1, dtype=np.float32), (128, TE)),
        "valid": (tok < TOKENS).astype(np.float32),
        "all_index": tok.astype(np.int32),
        "values": np.stack([np.broadcast_to(np.repeat(np.arange(TOK_TILES), TE), (128, te)),
                            np.broadcast_to(part[:, None] + 1, (128, te))], axis=1).astype(np.float16),
        "dummy_row": (TOKENS + 1 + part[:, None]).astype(np.float32),
        "steps": (128.0 * np.arange(1, TOK_TILES))[None].astype(np.float32),
    }
    heads = lambda m: m.reshape(m.shape[0], 8, -1)
    with_bias = lambda m, b: np.concatenate([m, b[None]], axis=0)
    a |= {
        "uq_t": heads(with_bias(w["L1_attn_W_UQ"], w["L1_attn_b_UQ"])).transpose(2, 1, 0),
        "uk_t": heads(with_bias(w["L1_attn_W_UK"], w["L1_attn_b_UK"])).transpose(2, 1, 0),
        "uv_t": heads(w["L1_attn_W_UV"]).transpose(2, 1, 0),
        "wo1": w["L1_attn_W_O"].reshape(8, 128, D).transpose(1, 0, 2),
        "buv": w["L1_attn_b_UV"].reshape(8, 128).T,
        "qr": heads(with_bias(w["L1_attn_W_QR"], w["L1_attn_b_QR"])),
        "w_cat": rows(np.concatenate([w["L1_attn_W_DKV"], w["L1_attn_W_KR"], w["L1_attn_W_DQ"]], axis=1)),
        "b_cat": np.concatenate([w["L1_attn_b_DKV"], w["L1_attn_b_KR"], w["L1_attn_b_DQ"]])[:, None],
        "b_kv4": np.tile(w["L1_attn_b_DKV"], 4)[:, None],
        "zero_rows": np.zeros((DUMMY, D), np.float32),
        "bo1": w["L1_attn_b_O"][None],
    }
    return {k: np.ascontiguousarray(v) for k, v in a.items()}


def kernel(**inputs):
    import numpy as np
    import concourse.bacc as bacc
    from concourse.bass_utils import run_bass_kernel_spmd

    arrays = lay_out(**{k: np.asarray(v) for k, v in inputs.items()})
    nc = bacc.Bacc("TRN2", target_bir_lowering=False, num_devices=1)
    io = {k: nc.dram_tensor(k, v.shape, mybir.dt.from_np(v.dtype), kind="ExternalInput").ap() for k, v in arrays.items()}
    out = nc.dram_tensor("out", (TOKENS, D), F32, kind="ExternalOutput").ap()
    build(nc, io, out)
    result = run_bass_kernel_spmd(nc, [arrays], core_ids=[0])
    return result.results[0]["out"].reshape(IMAGES, SEQ, D)
```

```python
from contextlib import ExitStack

import concourse.bass as bass
from concourse import mybir

F32 = mybir.dt.float32
F16 = mybir.dt.float16
I32 = mybir.dt.int32
ALU = mybir.AluOpType
ACT = mybir.ActivationFunctionType
AX = mybir.AxisListType

IMAGES = 64
GRID = 6
PATCHES = GRID * GRID
SEQ = PATCHES + 1
TOKENS = IMAGES * SEQ
D = 256
DC = D // 128
PATCH_DIM = 768
PC = PATCH_DIM // 128
PAIRS = IMAGES // 2
SLOT = 64
PAIR = 2 * SEQ
TRIO = 3 * SEQ
EPS = 1e-5
WS = 64.0

DUMMY = 128
ROWS = TOKENS + DUMMY
TOK_TILES = -(-TOKENS // 128)
TE = 8


class Sems:

    def __init__(self, nc, prefix):
        self.nc, self.prefix, self.made = nc, prefix, {}

    def __call__(self, name):
        if name not in self.made:
            self.made[name] = self.nc.alloc_semaphore(f"{self.prefix}_{name}")
        return self.made[name]

    def clear(self):
        self.nc.clear_and_free_semaphores(list(self.made.values()))
        self.nc.all_engine_barrier()


def wait(eng, sem, count):
    if isinstance(count, int) and count <= 0:
        return
    eng.wait_ge(sem, count)


def wait_alone(eng, S, name, count):
    wait(eng, S(name), count)
    if not isinstance(count, int):
        eng.sem_inc(S("passed"), 1)


class Step:

    def __init__(self, h, u, unroll, total):
        self.h, self.u, self.unroll, self.total = h, u, unroll, total

    def active(self, skew):
        if not isinstance(self.h, int):
            return True
        return 0 <= self.unroll * self.h + self.u - skew < self.total

    def item(self, skew):
        s = self.u - skew
        return (self.h * self.unroll + s, s % 2, self.h * (self.unroll // 2) + s // 2, s % self.unroll)


def run_steps(eng, total, skews, body, unroll=4):
    first = -(-(skews + 2) // unroll)
    last = total // unroll
    for h in range(first):
        for u in range(unroll):
            body(Step(h, u, unroll, total))
    with eng.Fori(first, last) as h:
        for u in range(unroll):
            body(Step(h, u, unroll, total))
    for t in range(last * unroll, total + skews):
        body(Step(t // unroll, t % unroll, unroll, total))
def build_attention0(nc, io, x1):
    HEADS, HD = 16, 16
    HC = 8
    with ExitStack() as ctx:
        def sb(name, shape, dt):
            return ctx.enter_context(nc.sbuf_tensor("a0_" + name, shape, dt))

        def ps(name, shape, dt=F32):
            return ctx.enter_context(nc.psum_tensor("a0_" + name, shape, dt))

        S = Sems(nc, "a0")
        ctx.callback(S.clear)

        w_stage = sb("w_stage", [128, PC, D], F32)
        w_emb = sb("w_emb", [128, 2, PC, D], F16)
        w_stage4 = sb("w_stage4", [128, 4, DC, D], F32)
        w_qkvo = sb("w_qkvo", [128, 2, 4, DC, D], F16)
        eye = sb("eye", [128, 128], F16)
        eye_ws = sb("eye_ws", [128, 128], F16)
        bias_in = sb("bias_in", [128, 4, DC], F32)
        bias_ws = sb("bias_ws", [128, 4, DC], F32)
        pos_t = sb("pos_t", [128, DC, SEQ], F32)
        cls_t = sb("cls_t", [128, DC, 1], F32)
        bo = sb("bo", [1, D], F32)
        bo_hl = sb("bo_hl", [1, 2, D], F16)
        ones = sb("ones", [1, 128], F16)
        head_mask = sb("head_mask", [128, HC], F32)
        odd_mask = sb("odd_mask", [128, 1], F32)
        even_mask = sb("even_mask", [128, 1], F32)
        half_power = sb("half_power", [128, 1], F32)

        x_in = sb("x_in", [128, 4, PC, 2 * PATCHES], F32)
        x_hl = sb("x_hl", [128, 2, 2, PC, 2 * PATCHES], F16)
        h0 = sb("h0", [128, 4, DC, 2, SEQ], F32)
        h0_hl = sb("h0_hl", [128, 4, 2, DC, 2, SLOT], F16)
        q_hl = sb("q_hl", [128, 2, 2, DC, PAIR], F16)
        k_hl = sb("k_hl", [128, 2, 2, DC, PAIR], F16)
        v_hl = sb("v_hl", [128, 4, 2, D], F16)
        LAST = HC - 3
        q_wide = sb("q_wide", [128, 2, 2, DC, 2, LAST * SEQ + 128], F16)
        qbd = q_wide[:, :, :, :, :, 0:HC * SEQ].rearrange("p b a c i (h q) -> p b a c i h q", q=SEQ)
        row_max = sb("row_max", [TRIO, 12], F32)
        row_sum = sb("row_sum", [TRIO, 12], F32)
        row_inv = sb("row_inv", [TRIO, 12], F32)
        prob = sb("prob", [TRIO, 2, 12, SEQ], F32)
        p_hl = sb("p_hl", [TRIO, 2, 2, 6, 2, SLOT], F16)
        pt_hl = sb("pt_hl", [128, 2, DC, 3 * TRIO], F16)
        odd = sb("odd", [128, 2, DC, SEQ], F32)
        ctx_f = sb("ctx_f", [128, DC, 2, SLOT], F32)
        ctx_hl = sb("ctx_hl", [128, 2, DC, 2, SLOT], F16)
        stats = sb("stats", [128, 6], F32)
        moments = sb("moments", [128, 2], F32)
        var_eps = sb("var_eps", [128, 1], F32)
        rstd = sb("rstd", [128, 1], F32)
        h1 = sb("h1", [128, 2, D], F32)

        psEQK = ps("psEQK", [128, DC * 2 * PATCHES + 2 * DC * PAIR])
        psE = psEQK[:, 0:DC * 2 * PATCHES].rearrange("p (c n) -> p c n", c=DC)
        psQK = psEQK[:, DC * 2 * PATCHES:].rearrange("p (z c n) -> p z c n", z=2, c=DC)
        psO = ps("psO", [128, D])
        psV = ps("psV", [128, D])
        psS = ps("psS", [128, 2, 6, SEQ])
        psT0 = ps("psT0", [128, 1024], F16)
        psT1 = ps("psT1", [128, 1024], F16)
        psC = [ps("psC0", [128, DC, PAIR]), ps("psC1", [128, DC, PAIR])]
        psT = [psT0[:, 0:672].rearrange("p (t c) -> p t c", t=6), psT1[:, 0:672].rearrange("p (t c) -> p t c", t=6)]

        N_SETUP = 8
        run = lambda eng, body: run_steps(eng, PAIRS, 6, body)
        block = ctx.enter_context(nc.Block())

        @block.sync
        def _(sp):
            sp.dma_start(w_stage[:], io["emb_w"]).then_inc(S("setup_in"), 16)
            sp.dma_start(w_stage4[:], io["qkvo_w"]).then_inc(S("setup_in"), 16)
            sp.dma_start(bias_in[:], io["bias0"]).then_inc(S("setup_in"), 16)
            sp.dma_start(pos_t[:], io["pos_t"]).then_inc(S("setup_in"), 16)
            sp.dma_start(cls_t[:], io["cls_t"]).then_inc(S("setup_in"), 16)
            sp.dma_start(bo[:], io["bo"]).then_inc(S("setup_in"), 16)
            sp.dma_start(head_mask[:], io["head_mask"]).then_inc(S("setup_in"), 16)
            sp.dma_start(eye[:], io["eye"]).then_inc(S("setup_in"), 16)

            sp.dma_start(x1[TOKENS:ROWS, :], io["zero_rows"]).then_inc(S("dummy_out"), 16)

            def step(st):
                if st.active(0):
                    p, b, hp, b4 = st.item(0)
                    wait(sp, S("x_high"), p - 3)
                    wait(sp, S("x_low"), p - 3)
                    sp.dma_start(x_in[:, b4], io["patches"][bass.ds(p, 1)].rearrange("a k c n -> k (a c) n")).then_inc(S(f"x_in{b4}"), 16)
                if st.active(6):
                    p, b, hp, _ = st.item(6)
                    wait(sp, S("h1"), p + 1)
                    for i in range(2):
                        sp.dma_start(x1[bass.ds(p * PAIR + i * SEQ, SEQ), :],
                                     h1[i * SLOT:i * SLOT + SEQ, b]).then_inc(S(f"h1_out{b}"), 16)

            run(sp, step)
            sp.wait_ge(S("dummy_out"), 16)
            for b in range(2):
                sp.wait_ge(S(f"h1_out{b}"), 32 * (PAIRS // 2))

        @block.tensor
        def _(pe):
            def products(out, left, right, first=True, last=True):
                n = 0
                todo = [(a, b, c) for c in left[1] for a, b in ((0, 0), (0, 1), (1, 0))]
                for a, b, c in todo:
                    ins = nc.tensor.matmul(out, left[0](a, c), right[0](b, c), start=first and n == 0,
                                           stop=last and n == len(todo) - 1)
                    n += 1
                return ins

            def embed(st):
                p, b, _, _ = st.item(1)
                if isinstance(p, int) and p == 0:
                    pe.wait_ge(S("w_ready"), 2)
                pe.wait_ge(S("x_high"), p + 1)
                pe.wait_ge(S("x_low"), p + 1)
                wait(pe, S("h0"), 2 * p)
                wait(pe, S("qk_low"), 2 * p)
                for m in range(DC):
                    ins = products(psE[:, m], (lambda a, c: w_emb[:, a, c, m * 128:(m + 1) * 128], range(PC)),
                                   (lambda a, c: x_hl[:, b, a, c], range(PC)))
                ins.then_inc(S("embedded"), 1)

            def project(st):
                p, b, _, b4 = st.item(2)
                if isinstance(p, int) and p == 0:
                    pe.wait_ge(S("w_ready"), 4)
                pe.wait_ge(S("h0_high"), p + 1)
                pe.wait_ge(S("h0_low"), p + 1)
                wait(pe, S("qk_low"), 2 * p)
                for z in range(2):
                    for m in range(DC):
                        ins = products(psQK[:, z, m].rearrange("p (i q) -> p i q", i=2), (lambda a, c: w_qkvo[:, a, z, c, m * 128:(m + 1) * 128], range(DC)),
                                       (lambda a, c: h0_hl[:, b4, a, c, :, 0:SEQ], range(DC)))
                ins.then_inc(S("qk"), 1)

            def project_values(st):
                p, b, _, b4 = st.item(2)
                wait(pe, S("v_low"), p)
                products(psV[:], (lambda a, c: h0_hl[:, b4, a, c], range(DC)),
                         (lambda a, c: w_qkvo[:, a, 2, c], range(DC))).then_inc(S("v"), 1)

            def transpose_probs(st):
                p, b, _, _ = st.item(4)
                pe.wait_ge(S("p_high"), p + 1)
                pe.wait_ge(S("p_low"), p + 1)
                wait(pe, S("pt_high"), p)
                wait(pe, S("pt_low"), p)
                for a in range(2):
                    for t in range(6):
                        ins = nc.tensor.transpose(psT[a][:, t, 0:TRIO], p_hl[:, b, a, t].rearrange("r i k -> r (i k)"), eye[0:TRIO, 0:TRIO])
                    ins.then_inc(S("pt"), 1)

            def scores(st):
                p, b, _, _ = st.item(3)
                pe.wait_ge(S("qbd_high"), p + 1)
                pe.wait_ge(S("qbd_low"), p + 1)
                wait(pe, S("shifted"), p)
                for i in range(2):
                    for c in range(DC):
                        for t in range(3):
                            at = min(3 * t, LAST) * SEQ
                            for n, (a, z) in enumerate(((0, 0), (0, 1), (1, 0))):
                                ins = nc.tensor.matmul(psS[:, i, 3 * c + t], q_wide[:, b, a, c, i, at:at + 128],
                                                       k_hl[:, b, z, c, i * SEQ:(i + 1) * SEQ], start=n == 0, stop=n == 2)
                ins.then_inc(S("scored"), 1)

            def values(st):
                p, b, _, b4 = st.item(5)
                pe.wait_ge(S("pt_high"), p + 1)
                pe.wait_ge(S("pt_low"), p + 1)
                wait_alone(pe, S, "ctx", 2 * p)
                for i in range(2):
                    rows = slice(i * SLOT, i * SLOT + SEQ)
                    for c in range(DC):
                        for j in range(4):
                            at = PAIR * j + (SEQ if j == 3 else 0)
                            for n, (a, z) in enumerate(((0, 0), (0, 1), (1, 0))):
                                ins = nc.tensor.matmul(psC[i][32 * j:32 * j + 32, c],
                                                       v_hl[rows, b4, z, c * 128 + 32 * j:c * 128 + 32 * j + 32],
                                                       pt_hl[rows, a, c, at:at + PAIR], start=n == 0, stop=n == 2)
                    ins.then_inc(S("mixed"), 1)

            def residual(st):
                p, b, _, b4 = st.item(5)
                wait(pe, S("h1"), p)
                if isinstance(p, int) and p == 0:
                    pe.wait_ge(S("bo_ready"), 3)
                for a in range(2):
                    nc.tensor.matmul(psO[:], ones[:], bo_hl[:, a], start=a == 0, stop=False)
                for m in range(DC):
                    for a in range(2):
                        ins = nc.tensor.matmul(psO[:, m * 128:(m + 1) * 128], h0_hl[:, b4, a, m], eye_ws[:], start=False, stop=False)
                ins.then_inc(S("residual"), 1)

            def output(st):
                p, b, _, b4 = st.item(5)
                pe.wait_ge(S("ctx_high"), p + 1)
                pe.wait_ge(S("ctx_low"), p + 1)
                ins = products(psO[:], (lambda a, c: ctx_hl[:, a, c], range(DC)),
                               (lambda a, c: w_qkvo[:, a, 3, c], range(DC)), first=False)
                ins.then_inc(S("projected"), 1)

            def step(st):
                if st.active(2):
                    project(st)
                if st.active(2):
                    project_values(st)
                if st.active(5):
                    values(st)
                if st.active(3):
                    scores(st)
                if st.active(5):
                    residual(st)
                if st.active(1):
                    embed(st)
                if st.active(4):
                    transpose_probs(st)
                if st.active(5):
                    output(st)

            run(pe, step)

        @block.scalar
        def _(act):
            act.wait_ge(S("setup_in"), 16 * N_SETUP)
            nc.scalar.activation(w_emb[:, 0], w_stage[:], ACT.Copy, scale=WS).then_inc(S("w_high"), 1)
            nc.scalar.activation(w_qkvo[:, 0], w_stage4[:], ACT.Copy, scale=WS).then_inc(S("w_high"), 1)

            def step(st):
                if st.active(2):
                    p, b, _, b4 = st.item(2)
                    act.wait_ge(S("qk"), p + 1)
                    wait(act, S("qbd_low"), p - 1)
                    wait(act, S("qbd_high"), p - 1)
                    wait(act, S("scored"), p - 1)
                    for z, dst in ((0, q_hl), (1, k_hl)):
                        for c in range(DC):
                            ins = nc.scalar.activation(dst[:, b, 0, c], psQK[:, z, c], ACT.Identity, bias=bias_ws[:, 1 + z, c:c + 1])
                    ins.then_inc(S("qk_high"), 1)
                if st.active(4):
                    p, b, _, _ = st.item(4)
                    act.wait_ge(S("prob"), p + 1)
                    wait(act, S("pt"), 2 * (p - 1))
                    for i in range(2):
                        ins = nc.scalar.activation(p_hl[:, b, 0, :, i, 0:SEQ], prob[:, b, 6 * i:6 * i + 6], ACT.Copy)
                    ins.then_inc(S("p_high"), 1)
                if st.active(2):
                    p, b, _, b4 = st.item(2)
                    act.wait_ge(S("v"), p + 1)
                    wait(act, S("mixed"), 2 * (p - 3))
                    nc.scalar.activation(v_hl[:, b4, 0], psV[:], ACT.Copy).then_inc(S("v_high"), 1)
                if st.active(5):
                    p, b, _, _ = st.item(5)
                    for i in range(2):
                        act.wait_ge(S("mixed"), 2 * p + 1 + i)
                        wait(act, S("ctx"), 2 * p)
                        for c in range(DC):
                            ins = nc.scalar.activation(odd[:, i, c], psC[i][:, c, SEQ:PAIR], ACT.Identity, scale=odd_mask[:, 0:1],
                                                       bias=bias_in[:, 3, c:c + 1])
                        ins.then_inc(S("odd"), 1)
                if st.active(0):
                    p, b, hp, b4 = st.item(0)
                    act.wait_ge(S(f"x_in{b4}"), 16 * st.h + 16)
                    wait(act, S("embedded"), p - 1)
                    nc.scalar.activation(x_hl[:, b, 0], x_in[:, b4], ACT.Copy).then_inc(S("x_high"), 1)
                if st.active(5):
                    p, b, _, _ = st.item(5)
                    act.wait_ge(S("ctx"), 2 * p + 2)
                    wait(act, S("projected"), p)
                    nc.scalar.activation(ctx_hl[:, 0, :, :, 0:SEQ], ctx_f[:, :, :, 0:SEQ], ACT.Copy).then_inc(S("ctx_high"), 1)
                if st.active(3):
                    p, b, _, _ = st.item(3)
                    act.wait_ge(S("shifted"), p + 1)
                    nc.scalar.activation(prob[:, b], prob[:, b], ACT.Exp, scale=1.0 / (WS * WS * HD ** 0.5)).then_inc(S("exp"), 1)
                if st.active(1):
                    p, b, _, b4 = st.item(1)
                    act.wait_ge(S("h0"), 2 * p + 2)
                    wait(act, S("residual"), p - 3)
                    nc.scalar.activation(h0_hl[:, b4, 0, :, :, 0:SEQ], h0[:, b4], ACT.Copy).then_inc(S("h0_high"), 1)
                if st.active(4):
                    p, b, _, _ = st.item(4)
                    act.wait_ge(S("pt"), 2 * p + 1)
                    wait(act, S("mixed"), 2 * p)
                    nc.scalar.activation(pt_hl[:, 0].rearrange("k c (t q) -> k (c t) q", t=3), psT[0][:, :, 0:TRIO], ACT.Copy).then_inc(S("pt_high"), 1)
                    act.wait_ge(S("pt"), 2 * p + 2)
                    nc.scalar.activation(pt_hl[:, 1].rearrange("k c (t q) -> k (c t) q", t=3), psT[1][:, :, 0:TRIO], ACT.Copy).then_inc(S("pt_low"), 1)

            run(act, step)

        @block.gpsimd
        def _(pool):
            nc.gpsimd.memset(h0_hl[:], 0.0).then_inc(S("zeroed"), 1)
            nc.gpsimd.memset(p_hl[:], 0.0).then_inc(S("zeroed"), 1)
            nc.gpsimd.memset(ctx_hl[:], 0.0).then_inc(S("zeroed"), 1)
            nc.gpsimd.memset(half_power[:], -0.5).then_inc(S("zeroed"), 1)
            nc.gpsimd.memset(q_wide[:], 0.0).then_inc(S("zeroed"), 1)
            pool.wait_ge(S("zeroed"), 5)

            def step(st):
                if st.active(4):
                    p, b, _, _ = st.item(4)
                    pool.wait_ge(S("p_high"), p + 1)
                    for i in range(2):
                        ins = nc.gpsimd.tensor_tensor(p_hl[:, b, 1, :, i, 0:SEQ], prob[:, b, 6 * i:6 * i + 6], p_hl[:, b, 0, :, i, 0:SEQ], ALU.subtract)
                    ins.then_inc(S("p_low"), 1)
                if st.active(2):
                    p, b, _, _ = st.item(2)
                    pool.wait_ge(S("qk_low"), 2 * p + 1)
                    wait_alone(pool, S, "scored", p - 1)
                    for h in range(HC // 2):
                        nc.gpsimd.tensor_scalar(qbd[:, b, 1, :, :, h], q_hl[:, b, 1].rearrange("p c (i q) -> p c i q", i=2),
                                                head_mask[:, h:h + 1], 1.0, ALU.mult, ALU.mult)
                if st.active(5):
                    p, b, _, _ = st.item(5)
                    pool.wait_ge(S("ctx_high"), p + 1)
                    nc.gpsimd.tensor_tensor(ctx_hl[:, 1, :, :, 0:SEQ], ctx_f[:, :, :, 0:SEQ], ctx_hl[:, 0, :, :, 0:SEQ],
                                            ALU.subtract).then_inc(S("ctx_low"), 1)
                if st.active(1):
                    p, b, _, b4 = st.item(1)
                    pool.wait_ge(S("h0_high"), p + 1)
                    nc.gpsimd.tensor_tensor(h0_hl[:, b4, 1, :, :, 0:SEQ], h0[:, b4], h0_hl[:, b4, 0, :, :, 0:SEQ],
                                            ALU.subtract).then_inc(S("h0_low"), 1)
                if st.active(2):
                    p, b, _, _ = st.item(2)
                    for h in range(HC // 2, HC):
                        ins = nc.gpsimd.tensor_scalar(qbd[:, b, 1, :, :, h], q_hl[:, b, 1].rearrange("p c (i q) -> p c i q", i=2),
                                                      head_mask[:, h:h + 1], 1.0, ALU.mult, ALU.mult)
                    ins.then_inc(S("qbd_low"), 1)
                if st.active(0):
                    p, b, _, b4 = st.item(0)
                    pool.wait_ge(S("x_high"), p + 1)
                    nc.gpsimd.tensor_tensor(x_hl[:, b, 1], x_in[:, b4], x_hl[:, b, 0], ALU.subtract).then_inc(S("x_low"), 1)
                if st.active(5):
                    p, b, _, _ = st.item(5)
                    pool.wait_ge(S("var_eps"), p + 1)
                    nc.gpsimd.tensor_tensor(rstd[:], var_eps[:], half_power[:], ALU.pow).then_inc(S("rstd"), 1)

            run(pool, step)

        @block.vector
        def _(dve):
            dve.wait_ge(S("setup_in"), 16 * N_SETUP)
            dve.wait_ge(S("w_high"), 1)
            nc.vector.scalar_tensor_tensor(w_emb[:, 1].rearrange("p c n -> p (c n)"), w_stage[:].rearrange("p c n -> p (c n)"), WS,
                                           w_emb[:, 0].rearrange("p c n -> p (c n)"), ALU.mult, ALU.subtract).then_inc(S("w_ready"), 1)
            nc.vector.tensor_scalar(eye_ws[:], eye[:], WS, None, ALU.mult).then_inc(S("w_ready"), 1)
            dve.wait_ge(S("w_high"), 2)
            nc.vector.scalar_tensor_tensor(w_qkvo[:, 1].rearrange("p z c n -> p (z c n)"), w_stage4[:].rearrange("p z c n -> p (z c n)"), WS,
                                           w_qkvo[:, 0].rearrange("p z c n -> p (z c n)"), ALU.mult, ALU.subtract).then_inc(S("w_ready"), 1)
            nc.vector.tensor_scalar(bias_ws[:], bias_in[:], WS, None, ALU.mult).then_inc(S("w_ready"), 1)
            nc.vector.memset(ones[:], 1.0).then_inc(S("bo_ready"), 1)
            nc.vector.tensor_scalar(bo_hl[:, 0], bo[:], WS, None, ALU.mult).then_inc(S("bo_ready"), 1)
            dve.wait_ge(S("bo_ready"), 2)
            nc.vector.scalar_tensor_tensor(bo_hl[:, 1], bo[:], WS, bo_hl[:, 0], ALU.mult, ALU.subtract).then_inc(S("bo_ready"), 1)
            nc.vector.tensor_tensor(odd_mask[:], head_mask[:, 1:2], head_mask[:, 3:4], ALU.add).then_inc(S("masks"), 1)
            for n, h in enumerate((5, 7)):
                dve.wait_ge(S("masks"), n + 1)
                nc.vector.tensor_tensor(odd_mask[:], odd_mask[:], head_mask[:, h:h + 1], ALU.add).then_inc(S("masks"), 1)
            dve.wait_ge(S("masks"), 3)
            nc.vector.tensor_scalar(even_mask[:], odd_mask[:], -1.0 / WS, 1.0 / WS, ALU.mult, ALU.add).then_inc(S("masks"), 1)
            dve.wait_ge(S("masks"), 4)
            nc.vector.tensor_scalar(odd_mask[:], odd_mask[:], 1.0 / WS, None, ALU.mult).then_inc(S("masks"), 1)
            nc.vector.tensor_tensor(cls_t[:], cls_t[:], pos_t[:, :, 0:1], ALU.add).then_inc(S("masks"), 1)
            for c in range(DC):
                nc.vector.tensor_scalar(pos_t[:, c, 1:SEQ], pos_t[:, c, 1:SEQ], bias_in[:, 0, c:c + 1], None, ALU.add).then_inc(S("masks"), 1)
            dve.wait_ge(S("masks"), 6 + DC)
            for b4 in range(4):
                for i in range(2):
                    nc.vector.tensor_copy(h0[:, b4, :, i, 0:1], cls_t[:]).then_inc(S("masks"), 1)
            dve.wait_ge(S("masks"), 14 + DC)

            def step(st):
                scored = psS[0:TRIO].rearrange("r i t k -> r (i t) k")
                if st.active(2):
                    p, b, _, b4 = st.item(2)
                    dve.wait_ge(S("qk_high"), p + 1)
                    for z, dst in ((0, q_hl), (1, k_hl)):
                        for c in range(DC):
                            ins = nc.vector.scalar_tensor_tensor(dst[:, b, 1, c], psQK[:, z, c], bias_ws[:, 1 + z, c:c + 1], dst[:, b, 0, c],
                                                                 ALU.add, ALU.subtract)
                        ins.then_inc(S("qk_low"), 1)
                if st.active(2):
                    p, b, _, b4 = st.item(2)
                    dve.wait_ge(S("v_high"), p + 1)
                    nc.vector.tensor_tensor(v_hl[:, b4, 1], psV[:], v_hl[:, b4, 0], ALU.subtract).then_inc(S("v_low"), 1)
                if st.active(6):
                    p, b, hp, b4 = st.item(6)
                    dve.wait_ge(S("rstd"), p + 1)
                    wait(dve, S(f"h1_out{b}"), 32 * hp)
                    nc.vector.tensor_scalar(h1[:, b], psO[:], moments[:, 0:1], rstd[:, 0:1], ALU.subtract, ALU.mult).then_inc(S("h1"), 1)
                if st.active(3):
                    p, b, _, _ = st.item(3)
                    dve.wait_ge(S("scored"), p + 1)
                    nc.vector.tensor_reduce(row_max[:], scored, AX.X, ALU.max).then_inc(S("row_max"), 1)
                if st.active(5):
                    p, b, _, b4 = st.item(5)
                    for i in range(2):
                        dve.wait_ge(S("odd"), 2 * p + 1 + i)
                        if i == 0:
                            wait(dve, S("ctx_low"), p)
                        nc.vector.scalar_tensor_tensor(ctx_f[:, :, i, 0:SEQ], psC[i][:, :, 0:SEQ], even_mask[:, 0:1], odd[:, i],
                                                       ALU.mult, ALU.add).then_inc(S("ctx"), 1)
                if st.active(3):
                    p, b, _, _ = st.item(3)
                    dve.wait_ge(S("row_max"), p + 1)
                    wait(dve, S("p_low"), p - 1)
                    nc.vector.tensor_tensor(prob[:, b], scored, row_max[:].unsqueeze(2).broadcast_to([TRIO, 12, SEQ]), ALU.subtract).then_inc(S("shifted"), 1)
                if st.active(1):
                    p, b, _, b4 = st.item(1)
                    dve.wait_ge(S("embedded"), p + 1)
                    wait(dve, S("h0_low"), p - 3)
                    for c in range(DC):
                        nc.vector.scalar_tensor_tensor(h0[:, b4, c, :, 1:SEQ], psE[:, c].rearrange("p (i n) -> p i n", i=2), 1.0 / WS,
                                                       pos_t[:, c:c + 1, 1:SEQ].broadcast_to([128, 2, PATCHES]), ALU.mult, ALU.add).then_inc(S("h0"), 1)
                if st.active(2):
                    p, b, _, b4 = st.item(2)
                    wait(dve, S("scored"), p - 1)
                    for h in range(HC):
                        ins = nc.vector.tensor_scalar(qbd[:, b, 0, :, :, h], q_hl[:, b, 0].rearrange("p c (i q) -> p c i q", i=2),
                                                      head_mask[:, h:h + 1], None, ALU.mult)
                    ins.then_inc(S("qbd_high"), 1)
                if st.active(3):
                    p, b, _, _ = st.item(3)
                    dve.wait_ge(S("exp"), p + 1)
                    nc.vector.tensor_reduce(row_sum[:], prob[:, b], AX.X, ALU.add).then_inc(S("row_sum"), 1)
                if st.active(3):
                    p, b, _, _ = st.item(3)
                    dve.wait_ge(S("row_sum"), p + 1)
                    nc.vector.reciprocal(row_inv[:], row_sum[:]).then_inc(S("row_inv"), 1)
                if st.active(5):
                    p, b, hp, b4 = st.item(5)
                    dve.wait_ge(S("projected"), p + 1)
                    nc.vector.bn_stats(stats[:], psO[:]).then_inc(S("stats"), 1)
                if st.active(3):
                    p, b, _, _ = st.item(3)
                    dve.wait_ge(S("row_inv"), p + 1)
                    nc.vector.tensor_tensor(prob[:, b], prob[:, b], row_inv[:].unsqueeze(2).broadcast_to([TRIO, 12, SEQ]), ALU.mult).then_inc(S("prob"), 1)
                if st.active(5):
                    p, b, hp, b4 = st.item(5)
                    wait_alone(dve, S, "stats", p + 1)
                    nc.vector.bn_aggr(moments[:], stats[:]).then_inc(S("moments"), 1)
                if st.active(5):
                    p, b, hp, b4 = st.item(5)
                    dve.wait_ge(S("moments"), p + 1)
                    nc.vector.tensor_scalar(var_eps[:], moments[:, 1:2], WS * WS * EPS, None, ALU.add).then_inc(S("var_eps"), 1)

            run(dve, step)
def build_routing(nc, io, x_rows, acc_rows, plan, layer):
    TT = TOK_TILES
    first = plan.first
    with ExitStack() as ctx:
        def sb(name, shape, dt=F32):
            return ctx.enter_context(nc.sbuf_tensor(f"r{layer}_" + name, shape, dt))

        S = Sems(nc, f"r{layer}")
        ctx.callback(S.clear)
        wr = sb("wr", [128, DC, TE])
        wr_hl = sb("wr_hl", [128, 2, DC, TE], F16)
        bias = sb("bias", [128, TE])
        eye = sb("eye", [128, 128])
        below = sb("below", [128, 128], F16)
        ones = sb("ones", [128, 128], F16)
        lane = sb("lane", [128, 128], F16)
        place = sb("place", [128, TE])
        valid = sb("valid", [128, TT])
        values = sb("values", [128, 1, TT * TE], F16)
        lane_number = sb("lane_number", [128, 1])
        dummy_row = sb("dummy_row", [128, 1])
        steps = sb("steps", [1, TT - 1])

        x = sb("x", [128, TT, D])
        xt_hl = sb("xt_hl", [128, 2, 2, DC, 128], F16)
        z = sb("z", [128, TT, TE])
        score = sb("score", [128, TT, TE])
        work = sb("work", [128, TT, TE])
        pick = sb("pick", [128, TT, TE])
        top = sb("top", [128, TT])
        top2 = sb("top2", [128, TT])
        total = sb("total", [128, TT])
        mask = sb("mask", [128, 2 * TT + 1, TE], F16)
        rank = sb("rank", [128, TT * TE])
        rank_i = sb("rank_i", [128, TT * TE], I32)
        lane_i = sb("lane_i", [128, TT * TE], I32)
        tile_i = sb("tile_i", [128, TT * TE], I32)
        lane_f = sb("lane_f", [128, TT * TE])
        lane_neg = sb("lane_neg", [128, TT * TE])
        tile_f = sb("tile_f", [128, TT * TE], F16)
        w_hl = sb("w_hl", [128, 2, TT * TE], F16)
        in_tile = sb("in_tile", [128, TT, TT * TE], F16)
        spread = sb("spread", [128, 4, TT, TT * TE], F16)
        makers = [m for m, _ in zip("dpdadpdad" * (TT * TE), range(TT * TE))]
        RING = 6
        in_lane = {m: sb("in_lane_" + m, [128, RING, 128], F16) for m in "dpa"}
        distance = sb("distance", [128, 2, 128], F16)
        counts = sb("counts", [1, TE])
        over = sb("over", [1, TE, TT - 1])
        tiles = sb("tiles", [1, TE])
        starts = sb("starts", [1, first + TE + 1])
        slot_id = sb("slot_id", [128, TE, TT])
        empty = sb("empty", [128, TE, TT])

        psX = [ctx.enter_context(nc.psum_tensor(f"r{layer}_psX{b}", [128, DC, 128], F32)) for b in range(2)]
        psL = ctx.enter_context(nc.psum_tensor(f"r{layer}_psL", [128, TT, TE], F32))
        psR = ctx.enter_context(nc.psum_tensor(f"r{layer}_psR", [128, TT + 1, TE], F32))
        psT = [ctx.enter_context(nc.psum_tensor(f"r{layer}_psT{b}", [128, TE // 2, 4, TT], F32)) for b in range(2)]
        N_SETUP = 11
        GROUP = 5

        def load(eng, *pairs):
            for dst, name in pairs:
                eng.dma_start(dst[:], io[name]).then_inc(S("setup_in"), 16)


        def lanes_of(m, eng, make):
            mine = [n for n in range(TT * TE) if makers[n] == m]
            for i, n in enumerate(mine):
                if i >= RING:
                    eng.wait_ge(S("placed"), mine[i - RING] + 1)
                make(i, (n % TT) * TE + n // TT, in_lane[m][:, i % RING]).then_inc(S("in_lane_" + m), 1)

        block = ctx.enter_context(nc.Block())

        @block.sync
        def _(sp):
            load(sp, (wr, f"wr{layer}"))
            for g in range(0, TT, GROUP):
                last = min(g + GROUP, TT)
                sp.dma_start(x[:, g:last], x_rows[g * 128:last * 128, :].rearrange("(t p) d -> p t d", p=128)).then_inc(S(f"x_in{g // GROUP}"), 16)
            load(sp, (lane, "lane"), (values, "tile_number"), (lane_number, "lane_number"), (dummy_row, "dummy_row"), (steps, "steps"))
            sp.dma_start(bias[:], io[f"router_bias{layer}"].broadcast_to([128, TE])).then_inc(S("setup_in"), 16)
            sp.dma_start(plan.w_stage[:], io[f"experts{layer}"][0]).then_inc(S("w_in"), 16)
            sp.wait_ge(S("w_in"), 16)
            sp.dma_start(acc_rows, x_rows).then_inc(S("acc_out"), 16)
            sp.wait_ge(S("acc_out"), 16)
            if first:
                sp.dma_start(plan.index[:, 0, :], io["all_index"]).then_inc(S("shared_in"), 16)
                sp.dma_start(plan.weight[:, 0, :], io["valid"]).then_inc(S("shared_in"), 16)
                sp.wait_ge(S("shared_in"), 32)

        @block.tensor
        def _(pe):
            pe.wait_ge(S("setup_in"), 16 * N_SETUP)
            pe.wait_ge(S("wr_ready"), 2)

            def logits(t):
                pe.wait_ge(S("xt_low"), t + 1)
                for n, (a, b, c) in enumerate((a, b, c) for c in range(DC) for a, b in ((0, 0), (0, 1), (1, 0))):
                    ins = nc.tensor.matmul(psL[:, t], xt_hl[:, t % 2, a, c], wr_hl[:, b, c], start=n == 0, stop=n == 3 * DC - 1)
                ins.then_inc(S("logits"), 1)

            for t in range(TT):
                pe.wait_ge(S(f"x_in{t // GROUP}"), 16)
                if t >= 2:
                    pe.wait_ge(S("xt_low"), t - 1)
                for c in range(DC):
                    ins = nc.tensor.transpose(psX[t % 2][:, c], x[:, t, c * 128:(c + 1) * 128], eye[:])
                ins.then_inc(S("turned"), 1)
                if t >= 1:
                    logits(t - 1)
            logits(TT - 1)
            pe.wait_ge(S("mask"), 1)
            pe.wait_ge(S("ones"), 1)
            nc.tensor.matmul(psR[:], below[:], mask[:, TT:], start=True, stop=False)
            for d in range(1, TT + 1):
                nc.tensor.matmul(psR[:], ones[:], mask[:, TT - d:2 * TT + 1 - d], start=False, stop=d == TT).then_inc(S("ranked"), 1)
            pe.wait_ge(S("spread"), 1)
            pe.wait_ge(S("spread_lane"), 1)
            for e in range(TE):
                for t in range(TT):
                    n = e * TT + t
                    i = makers[:n].count(makers[n])
                    pe.wait_ge(S("in_lane_" + makers[n]), i + 1)
                    nc.tensor.matmul(psT[e // 4][:, e % 4], in_lane[makers[n]][:, i % RING], spread[:, :, :, t * TE + e],
                                     start=t == 0, stop=t == TT - 1).then_inc(S("placed"), 1)

        @block.scalar
        def _(act):
            load(act, (eye, "eye_f"), (below, "below"), (place, "place"), (valid, "valid"))
            act.wait_ge(S("setup_in"), 16 * N_SETUP)
            nc.scalar.activation(wr_hl[:, 0], wr[:], ACT.Copy, scale=WS).then_inc(S("wr_high"), 1)
            for t in range(TT):
                act.wait_ge(S("turned"), t + 1)
                if t >= 2:
                    act.wait_ge(S("logits"), t - 1)
                nc.scalar.activation(xt_hl[:, t % 2, 0], psX[t % 2][:], ACT.Copy).then_inc(S("xt_high"), 1)
            if layer == 0:
                act.wait_ge(S("z"), 1)
                nc.scalar.activation(score[:], z[:], ACT.Exp, scale=-1.0).then_inc(S("exp"), 1)
            else:
                act.wait_ge(S("z_shifted"), 1)
                nc.scalar.activation(score[:], work[:], ACT.Exp).then_inc(S("exp"), 1)
            act.wait_ge(S("in_tile"), TT)
            nc.scalar.activation(spread[:, 1], in_tile[:], ACT.Copy, scale=lane_number[:, 0:1]).then_inc(S("spread_lane"), 1)

            def make(i, at, out):
                nc.scalar.activation(distance[:, i % 2], lane[:], ACT.Abs, bias=lane_neg[:, at:at + 1]).then_inc(S("distance"), 1)
                act.wait_ge(S("distance"), i + 1)
                return nc.scalar.activation(out, distance[:, i % 2], ACT.Relu, scale=-1.0, bias=1.0)

            lanes_of("a", act, make)

        @block.gpsimd
        def _(pool):
            nc.gpsimd.memset(ones[:], 1.0).then_inc(S("ones"), 1)
            pool.wait_ge(S("setup_in"), 16 * N_SETUP)
            pool.wait_ge(S("lane_ready"), 1)
            lanes_of("p", pool, lambda i, at, out: nc.gpsimd.tensor_scalar(out, lane[:], lane_f[:, at:at + 1], 1.0, ALU.is_equal, ALU.mult))

        @block.vector
        def _(dve):
            made = [0]

            def then(ins):
                made[0] += 1
                ins.then_inc(S("link"), 1)
                dve.wait_ge(S("link"), made[0])

            over_tiles = lambda v: v.unsqueeze(1).broadcast_to([128, TT, TE])
            over_experts = lambda v: v.unsqueeze(2).broadcast_to([128, TT, TE])
            dve.wait_ge(S("setup_in"), 16 * N_SETUP)
            dve.wait_ge(S("wr_high"), 1)
            dve.wait_ge(S("ones"), 1)
            nc.vector.scalar_tensor_tensor(wr_hl[:, 1], wr[:], WS, wr_hl[:, 0], ALU.mult, ALU.subtract).then_inc(S("wr_ready"), 1)
            nc.vector.memset(mask[:], 0.0).then_inc(S("wr_ready"), 1)
            dve.wait_ge(S("wr_ready"), 2)
            for t in range(TT):
                dve.wait_ge(S("xt_high"), t + 1)
                if t >= 2:
                    dve.wait_ge(S("logits"), t - 1)
                nc.vector.tensor_tensor(xt_hl[:, t % 2, 1], psX[t % 2][:], xt_hl[:, t % 2, 0], ALU.subtract).then_inc(S("xt_low"), 1)
            dve.wait_ge(S("logits"), TT)
            nc.vector.scalar_tensor_tensor(z[:], psL[:], 1.0 / WS, over_tiles(bias[:]), ALU.mult, ALU.add).then_inc(S("z"), 1)
            dve.wait_ge(S("z"), 1)
            if layer == 0:
                dve.wait_ge(S("exp"), 1)
                then(nc.vector.tensor_scalar(score[:], score[:], 1.0, None, ALU.add))
                then(nc.vector.reciprocal(z[:], score[:]))

            def take_first(src, top, out):
                then(nc.vector.tensor_reduce(top[:], src[:], AX.X, ALU.max))
                then(nc.vector.tensor_tensor(out[:], src[:], over_experts(top[:]), ALU.is_equal))
                then(nc.vector.tensor_tensor(out[:], out[:], over_tiles(place[:]), ALU.mult))
                then(nc.vector.tensor_reduce(total[:], out[:], AX.X, ALU.max))
                then(nc.vector.tensor_tensor(out[:], out[:], over_experts(total[:]), ALU.is_equal))

            take_first(z, top, pick)
            then(nc.vector.scalar_tensor_tensor(work[:], pick[:], -3.0e38, z[:], ALU.mult, ALU.add))
            if layer == 0:
                take_first(work, top2, score)
                then(nc.vector.tensor_tensor(pick[:], pick[:], score[:], ALU.add))
            else:
                then(nc.vector.tensor_reduce(top2[:], work[:], AX.X, ALU.max))
                then(nc.vector.tensor_tensor(pick[:], z[:], over_experts(top2[:]), ALU.is_ge))
            then(nc.vector.tensor_tensor(pick[:], pick[:], over_experts(valid[:]), ALU.mult))
            nc.vector.tensor_copy(mask[:, TT:2 * TT], pick[:]).then_inc(S("mask"), 1)
            dve.wait_ge(S("mask"), 1)
            if layer == 0:
                then(nc.vector.tensor_tensor(work[:], z[:], pick[:], ALU.mult))
            else:
                nc.vector.tensor_tensor(work[:], z[:], over_experts(top[:]), ALU.subtract).then_inc(S("z_shifted"), 1)
                dve.wait_ge(S("exp"), 1)
                then(nc.vector.tensor_tensor(work[:], score[:], pick[:], ALU.mult))
                then(nc.vector.tensor_reduce(total[:], work[:], AX.X, ALU.add))
                then(nc.vector.tensor_scalar(total[:], total[:], 1.0e-30, None, ALU.max))
                then(nc.vector.reciprocal(top2[:], total[:]))
                then(nc.vector.tensor_tensor(work[:], work[:], over_experts(top2[:]), ALU.mult))
            flat = work[:].rearrange("p t e -> p (t e)")
            then(nc.vector.tensor_copy(w_hl[:, 0], flat))
            then(nc.vector.tensor_tensor(w_hl[:, 1], flat, w_hl[:, 0], ALU.subtract))
            dve.wait_ge(S("ranked"), TT)
            then(nc.vector.scalar_tensor_tensor(rank[:].rearrange("p (t e) -> p t e", e=TE), psR[:, 0:TT], 1.0, pick[:], ALU.add, ALU.mult))
            then(nc.vector.tensor_scalar(rank_i[:], rank[:], -1.0, None, ALU.add))
            then(nc.vector.tensor_scalar(lane_i[:], rank_i[:], 127, None, ALU.bitwise_and))
            then(nc.vector.tensor_scalar(tile_i[:], rank_i[:], 7, None, ALU.arith_shift_right))
            then(nc.vector.tensor_copy(lane_f[:], lane_i[:]))
            nc.vector.tensor_scalar(lane_neg[:], lane_f[:], -1.0, None, ALU.mult).then_inc(S("lane_ready"), 1)
            then(nc.vector.tensor_copy(tile_f[:], tile_i[:]))
            for c in range(TT):
                nc.vector.tensor_scalar(in_tile[:, c], tile_f[:], float(c), None, ALU.is_equal).then_inc(S("in_tile"), 1)
            dve.wait_ge(S("in_tile"), TT)
            for v, factor in ((0, values[:, 0:1]), (2, w_hl[:, 0:1]), (3, w_hl[:, 1:2])):
                ins = nc.vector.tensor_tensor(spread[:, v], in_tile[:], factor.broadcast_to([128, TT, TT * TE]), ALU.mult)
            ins.then_inc(S("spread"), 1)
            lanes_of("d", dve, lambda i, at, out: nc.vector.tensor_scalar(out, lane[:], lane_f[:, at:at + 1], None, ALU.is_equal))
            then(nc.vector.tensor_copy(counts[:], psR[0:1, TT]))
            then(nc.vector.tensor_tensor(over[:], counts[:].unsqueeze(2).broadcast_to([1, TE, TT - 1]),
                                         steps[:].unsqueeze(1).broadcast_to([1, TE, TT - 1]), ALU.is_gt))
            then(nc.vector.tensor_reduce(tiles[:], over[:], AX.X, ALU.add))
            then(nc.vector.tensor_scalar(tiles[:], tiles[:], 1.0, float(MIN_TILES), ALU.add, ALU.max))
            then(nc.vector.memset(starts[:], 0.0))
            if first:
                then(nc.vector.memset(starts[:, 1:2], float(TT)))
            for e in range(TE):
                then(nc.vector.tensor_tensor(starts[:, first + e + 1:first + e + 2], starts[:, first + e:first + e + 1], tiles[:, e:e + 1], ALU.add))
            then(nc.vector.tensor_scalar(plan.bounds[:], starts[:], -float(MIN_TILES), None, ALU.add))
            dve.wait_ge(S("placed"), TE * TT)
            for g in range(2):
                half = slice(4 * g, 4 * g + 4)
                then(nc.vector.tensor_copy(slot_id[:, half], psT[g][:, :, 1]))
                then(nc.vector.scalar_tensor_tensor(slot_id[:, half], psT[g][:, :, 0], 128.0, slot_id[:, half], ALU.mult, ALU.add))
                out = plan.weight[:, first + 4 * g:first + 4 * g + 4]
                then(nc.vector.tensor_copy(out, psT[g][:, :, 2]))
                then(nc.vector.tensor_tensor(out, psT[g][:, :, 3], out, ALU.add))
            then(nc.vector.tensor_scalar(empty[:], slot_id[:], 0.0, None, ALU.is_equal))
            then(nc.vector.scalar_tensor_tensor(slot_id[:], empty[:], dummy_row[:, 0:1], slot_id[:], ALU.mult, ALU.add))
            then(nc.vector.tensor_scalar(plan.index[:, first:], slot_id[:], -1.0, None, ALU.add))


MIN_TILES = 2


class Plan:

    def __init__(self, nc, ctx, layer, first):
        self.first = first
        self.experts = first + TE
        self.index = ctx.enter_context(nc.sbuf_tensor(f"plan{layer}_index", [128, self.experts, TOK_TILES], I32))
        self.weight = ctx.enter_context(nc.sbuf_tensor(f"plan{layer}_weight", [128, self.experts, TOK_TILES], F32))
        self.bounds = ctx.enter_context(nc.sbuf_tensor(f"plan{layer}_bounds", [1, self.experts + 1], I32))
        width = 3 * 2 * 512 if layer == 0 else 2 * 1024 + 8 * D
        self.w_stage = ctx.enter_context(nc.sbuf_tensor(f"plan{layer}_w_stage", [128, width], F32))


def build_experts(nc, io, x_rows, acc_rows, plan, layer):
    gated = layer == 0
    NE = plan.experts
    HID = 512 if gated else 1024
    HC = HID // 128
    UP = DC * HID
    W = UP * (2 if gated else 1) + HC * D
    PARTS = HC // 2
    NB = 2 if gated else 4
    with ExitStack() as ctx:
        def sb(name, shape, dt=F32):
            return ctx.enter_context(nc.sbuf_tensor(f"e{layer}_" + name, shape, dt))

        S = Sems(nc, f"e{layer}")
        ctx.callback(S.clear)
        eye = sb("eye", [128, 128])
        w_stage = plan.w_stage
        w_hl = sb("w_hl", [128, 2, 2, W], F16)
        x = sb("x", [128, D])
        xt_hl = sb("xt_hl", [128, 2, DC, 128], F16)
        gate = sb("gate", [128, HC, 128])
        hidden = sb("hidden", [128, HC, 128])
        hid_hl = sb("hid_hl", [128, 2, HC, 128], F16)
        y = sb("y", [128, D])
        y_sum = sb("y_sum", [128, D])
        slot_w = sb("slot_w", [128, 1])
        idx = sb("idx", [128, 1], I32)
        slot_row = sb("slot_row", [128, 1], I32)
        y_rows = sb("y_rows", [128, 1], I32)
        if not gated:
            b1 = sb("b1", [128, 2, HC])
            b2 = sb("b2", [128, 2, D])
        psX = ctx.enter_context(nc.psum_tensor(f"e{layer}_psX", [128, DC, 128], F32))
        psH = [ctx.enter_context(nc.psum_tensor(f"e{layer}_psH{n}", [128, 2 if gated else 1, 2, 128], F32)) for n in range(NB)]
        psY = ctx.enter_context(nc.psum_tensor(f"e{layer}_psY", [128, D], F32))

        def up_w(b, a, z, c, m):
            at = z * UP + c * HID + m * 128
            return w_hl[:, b, a, at:at + 128]

        def down_w(b, a, m):
            at = W - HC * D + m * D
            return w_hl[:, b, a, at:at + D]

        def tiles_before(eng, n):
            return eng.value_load(plan.bounds[0:1, bass.ds(n, 1)], min_val=0, max_val=NE * TOK_TILES - MIN_TILES) + MIN_TILES

        def over_experts(eng, tile, finish):
            def expert(n, b):
                lo = 0 if isinstance(n, int) and n == 0 else tiles_before(eng, n)
                hi = tiles_before(eng, n + 1)
                tile(lo, n, lo, b, 1 - b, True)
                with eng.Fori(lo + 1, hi) as T:
                    tile(T, n, lo, b, b, False)
                return hi

            last = expert(0, 0)
            with eng.Fori(1, 7, 2) as n:
                expert(n, 1)
                expert(n + 1, 0)
            for n in range(7, NE):
                last = expert(n, n % 2)
            if finish:
                finish(last, (NE - 1) % 2)

        def column(T, n, lo):
            if isinstance(T, int):
                return T
            return nc.s_assert_within(n * TOK_TILES + T - lo, 0, NE * TOK_TILES - 1,
                                      skip_runtime_bounds_check_because="an expert has at most TOK_TILES tiles")

        SPLIT = 4
        piece = lambda k: slice(k * W // SPLIT, (k + 1) * W // SPLIT)
        block = ctx.enter_context(nc.Block())

        @block.sync
        def _(sp):
            sp.dma_start(eye[:], io["eye_f"]).then_inc(S("eye_in"), 16)
            if not gated:
                for n in range(2):
                    sp.dma_start(b1[:, n], io["b1"][n]).then_inc(S(f"b_in{n}"), 16)
                    sp.dma_start(b2[:, n], io["b2"][n].broadcast_to([128, D])).then_inc(S(f"b_in{n}"), 16)

            def load(n, b):
                sp.wait_ge(S("w_low"), n * SPLIT)
                sp.wait_ge(S("w_high"), n * SPLIT)
                sp.dma_start(w_stage[:], io[f"experts{layer}"][bass.ds(n, 1)].rearrange("a p w -> (a p) w")).then_inc(S("w_in"), 16)
                if not gated and not (isinstance(n, int) and n < 2):
                    lo = tiles_before(sp, n - 1)
                    sp.wait_ge(S("y"), lo + 1)
                    sp.dma_start(b1[:, b], io["b1"][bass.ds(n, 1)].rearrange("a p c -> (a p) c")).then_inc(S(f"b_in{b}"), 16)
                    sp.dma_start(b2[:, b], io["b2"][bass.ds(n, 1)].rearrange("a o d -> (a o) d").broadcast_to([128, D])).then_inc(S(f"b_in{b}"), 16)

            load(1, 1)
            with sp.Fori(2, NE - 1, 2) as n:
                load(n, 0)
                load(n + 1, 1)
            if NE % 2:
                load(NE - 1, 0)

        @block.tensor
        def _(pe):
            pe.wait_ge(S("eye_in"), 16)

            def second(T, b, parts):
                if 0 in parts:
                    wait(pe, S("y_sum"), T)
                for k in parts:
                    pe.wait_ge(S("hid_low"), T * PARTS + k + 1)
                    for m in (2 * k, 2 * k + 1):
                        for a, z in ((0, 0), (0, 1), (1, 0)):
                            ins = nc.tensor.matmul(psY[:], hid_hl[:, a, m], down_w(b, z, m),
                                                   start=m == 0 and (a, z) == (0, 0), stop=m == HC - 1 and a == 1)
                if PARTS - 1 in parts:
                    ins.then_inc(S("second"), 1)

            def turn(T):
                pe.wait_ge(S("gathered"), T * 16 + 16)
                wait(pe, S("xt_low"), T)
                for c in range(DC):
                    ins = nc.tensor.transpose(psX[:, c], x[:, c * 128:(c + 1) * 128], eye[:])
                ins.then_inc(S("turned"), 1)

            def tile(T, n, lo, b, b_prev, is_first):
                start = isinstance(T, int)
                if start:
                    turn(0)
                if is_first:
                    pe.wait_ge(S("w_low"), n * SPLIT + SPLIT)
                pe.wait_ge(S("xt_low"), T + 1)
                for k in range(PARTS):
                    if k == 1 and not start:
                        second(T - 1, b_prev, (PARTS - 1,))
                    if not (start and k < NB):
                        pe.wait_ge(S("hid"), T * PARTS + k + 1 - NB)
                    for mm in range(2):
                        for z in range(2 if gated else 1):
                            for i, (a, r, c) in enumerate((a, r, c) for c in range(DC) for a, r in ((0, 0), (0, 1), (1, 0))):
                                ins = nc.tensor.matmul(psH[k % NB][:, z, mm], up_w(b, a, z, c, 2 * k + mm), xt_hl[:, r, c],
                                                       start=i == 0, stop=i == 3 * DC - 1)
                    ins.then_inc(S("first"), 1)
                turn(T + 1)
                second(T, b, range(PARTS - 1))

            over_experts(pe, tile, lambda last, b: second(last - 1, b, (PARTS - 1,)))

        @block.scalar
        def _(act):
            for k in range(SPLIT):
                nc.scalar.activation(w_hl[:, 0, 0, piece(k)], w_stage[:, piece(k)], ACT.Copy, scale=WS).then_inc(S("w_high"), 1)

            def split(n, lo, b, k):
                if k == 0:
                    act.wait_ge(S("w_in"), n * 16 + 16)
                    wait(act, S("second"), lo)
                nc.scalar.activation(w_hl[:, 1 - b, 0, piece(k)], w_stage[:, piece(k)], ACT.Copy, scale=WS).then_inc(S("w_high"), 1)

            def turned(T):
                act.wait_ge(S("turned"), T + 1)
                wait(act, S("first"), T * PARTS)
                nc.scalar.activation(xt_hl[:, 0], psX[:], ACT.Copy).then_inc(S("xt_high"), 1)

            def tile(T, n, lo, b, b_prev, is_first):
                start = isinstance(T, int)
                more = is_first and not (isinstance(n, int) and n == NE - 1)
                if start:
                    turned(0)
                if is_first and not gated:
                    if start:
                        act.wait_ge(S("b_in0"), 32)
                    else:
                        act.wait_ge(S(f"b_in{b}"), (n // 2 + 1) * 32 if isinstance(n, int) else (n * 16 + (32 if b == 0 else 16)))
                for k in range(PARTS):
                    if k == PARTS - 1:
                        turned(T + 1)
                    act.wait_ge(S("first"), T * PARTS + k + 1)
                    if gated:
                        wait(act, S("hid"), (T - 1) * PARTS + k + 1 if not start else 0)
                        nc.scalar.activation(gate[:, 2 * k:2 * k + 2], psH[k % NB][:, 0], ACT.Silu, scale=1.0 / WS).then_inc(S("gate"), 1)
                        act.wait_ge(S("hid"), T * PARTS + k + 1)
                        wait(act, S("second"), T)
                        nc.scalar.activation(hid_hl[:, 0, 2 * k:2 * k + 2], hidden[:, 2 * k:2 * k + 2], ACT.Copy).then_inc(S("hid_high"), 1)
                        if more:
                            split(n, lo, b, 2 * k)
                            split(n, lo, b, 2 * k + 1)
                    else:
                        wait(act, S("hid_low"), (T - 1) * PARTS + k + 1 if not start else 0)
                        for mm in range(2):
                            m = 2 * k + mm
                            ins = nc.scalar.activation(hidden[:, m], psH[k % NB][:, 0, mm], ACT.Gelu, scale=1.0 / WS, bias=b1[:, b, m:m + 1])
                        ins.then_inc(S("hid"), 1)
                        if more:
                            split(n, lo, b, k)

            over_experts(act, tile, None)

        @block.gpsimd
        def _(pool):
            nc.gpsimd.iota(y_rows[:], [[0, 1]], base=TOKENS, channel_multiplier=1).then_inc(S("y_set"), 1)
            nc.gpsimd.memset(y[:], 0.0).then_inc(S("y_set"), 1)
            pool.wait_ge(S("y_set"), 2)
            pool.sem_inc(S("y"), 1)

            def scatter(T):
                wait_alone(pool, S, "scattered", T * 16)
                wait_alone(pool, S, "y", T)
                nc.gpsimd.indirect_dma_start(out=acc_rows, out_offset=bass.IndirectOffsetOnAxis(ap=y_rows[:, 0:1], axis=0), in_=y[:],
                                             in_offset=None, compute_op=ALU.add).then_inc(S("scattered"), 16)

            def tile(T, n, lo, b, b_prev, is_first):
                col = column(T, n, lo)
                wait(pool, S("turned"), T)
                nc.gpsimd.tensor_copy(idx[:], plan.index[:].rearrange("p n c -> p (n c)")[:, bass.ds(col, 1)]).then_inc(S("idx"), 1)
                wait_alone(pool, S, "idx", T + 1)
                nc.gpsimd.indirect_dma_start(out=x[:], out_offset=None, in_=x_rows,
                                             in_offset=bass.IndirectOffsetOnAxis(ap=idx[:, 0:1], axis=0)).then_inc(S("gathered"), 16)
                scatter(T)

            def finish(last, b):
                wait_alone(pool, S, "turned", last)
                nc.gpsimd.indirect_dma_start(out=x[:], out_offset=None, in_=x_rows,
                                             in_offset=bass.IndirectOffsetOnAxis(ap=idx[:, 0:1], axis=0)).then_inc(S("gathered"), 16)
                scatter(last)
                pool.wait_ge(S("scattered"), last * 16 + 16)
                scatter(last + 1)
                pool.wait_ge(S("scattered"), last * 16 + 32)
                pool.wait_ge(S("gathered"), last * 16 + 16)

            over_experts(pool, tile, finish)

        @block.vector
        def _(dve):
            for k in range(SPLIT):
                dve.wait_ge(S("w_high"), k + 1)
                nc.vector.scalar_tensor_tensor(w_hl[:, 0, 1, piece(k)], w_stage[:, piece(k)], WS, w_hl[:, 0, 0, piece(k)],
                                               ALU.mult, ALU.subtract).then_inc(S("w_low"), 1)

            def split(n, b, k):
                dve.wait_ge(S("w_high"), n * SPLIT + SPLIT + k + 1)
                nc.vector.scalar_tensor_tensor(w_hl[:, 1 - b, 1, piece(k)], w_stage[:, piece(k)], WS, w_hl[:, 1 - b, 0, piece(k)],
                                               ALU.mult, ALU.subtract).then_inc(S("w_low"), 1)

            def sum_rows(T, b):
                dve.wait_ge(S("second"), T + 1)
                if gated:
                    dve.wait_ge(S("slot_w"), T + 1)
                    dve.wait_ge(S("scattered"), T * 16 + 32)
                    nc.vector.tensor_scalar(y[:], psY[:], slot_w[:, 0:1], 1.0 / (WS * WS), ALU.mult, ALU.mult).then_inc(S("y_sum"), 1)
                else:
                    nc.vector.scalar_tensor_tensor(y_sum[:], psY[:], 1.0 / WS, b2[:, b], ALU.mult, ALU.add).then_inc(S("y_sum"), 1)

            def weigh_rows(T):
                if not gated:
                    dve.wait_ge(S("slot_w"), T + 1)
                    dve.wait_ge(S("y_sum"), T + 1)
                    dve.wait_ge(S("scattered"), T * 16 + 32)
                    nc.vector.tensor_scalar(y[:], y_sum[:], slot_w[:, 0:1], None, ALU.mult).then_inc(S("y_out"), 1)
                nc.vector.tensor_copy(y_rows[:], slot_row[:]).then_inc(S("y"), 1)

            def turned(T):
                dve.wait_ge(S("xt_high"), T + 1)
                nc.vector.tensor_tensor(xt_hl[:, 1], psX[:], xt_hl[:, 0], ALU.subtract).then_inc(S("xt_low"), 1)

            def tile(T, n, lo, b, b_prev, is_first):
                start = isinstance(T, int)
                more = is_first and not (isinstance(n, int) and n == NE - 1)
                col = column(T, n, lo)
                if start:
                    turned(0)
                for k in range(PARTS):
                    part = slice(2 * k, 2 * k + 2)
                    if k == PARTS - 1:
                        turned(T + 1)
                    if gated:
                        dve.wait_ge(S("gate"), T * PARTS + k + 1)
                        wait(dve, S("hid_low"), (T - 1) * PARTS + k + 1 if not start else 0)
                        nc.vector.tensor_tensor(hidden[:, part], psH[k % NB][:, 1], gate[:, part], ALU.mult).then_inc(S("hid"), 1)
                        if k == 0 and not start:
                            sum_rows(T - 1, b_prev)
                    else:
                        dve.wait_ge(S("hid"), T * PARTS + k + 1)
                        wait(dve, S("second"), T)
                        nc.vector.tensor_copy(hid_hl[:, 0, part], hidden[:, part]).then_inc(S("hid_high"), 1)
                    dve.wait_ge(S("hid_high"), T * PARTS + k + 1)
                    nc.vector.tensor_tensor(hid_hl[:, 1, part], hidden[:, part], hid_hl[:, 0, part], ALU.subtract).then_inc(S("hid_low"), 1)
                    if not gated and k == 0 and not start:
                        sum_rows(T - 1, b_prev)
                    if k == (0 if gated else 2):
                        if not start:
                            weigh_rows(T - 1)
                            dve.wait_ge(S("y"), T + 1)
                        nc.vector.tensor_copy(slot_row[:], plan.index[:].rearrange("p n c -> p (n c)")[:, bass.ds(col, 1)])
                        nc.vector.tensor_copy(slot_w[:], plan.weight[:].rearrange("p n c -> p (n c)")[:, bass.ds(col, 1)]).then_inc(S("slot_w"), 1)
                    if more:
                        for kk in range(k * SPLIT // PARTS, (k + 1) * SPLIT // PARTS):
                            split(n, b, kk)

            def finish(last, b):
                sum_rows(last - 1, b)
                weigh_rows(last - 1)

            over_experts(dve, tile, finish)
def build_attention1(nc, io, acc_rows, x3):
    NH, DK, DL, DR = 8, 128, 32, 32
    QK = DL + DR + 1
    CAT = 2 * DL + DR
    QS = 4.0
    TOP = 64
    with ExitStack() as ctx:
        def sb(name, shape, dt=F32):
            return ctx.enter_context(nc.sbuf_tensor("a1_" + name, shape, dt))

        def ps(name, shape, dt=F32):
            return ctx.enter_context(nc.psum_tensor("a1_" + name, shape, dt))

        S = Sems(nc, "a1")
        ctx.callback(S.clear)
        uq_t = sb("uq_t", [DK, NH, DL + 1])
        uk_t = sb("uk_t", [DK, NH, DL + 1])
        uv_t = sb("uv_t", [DK, NH, DL])
        wo = sb("wo", [DK, NH, D])
        buv = sb("buv", [DK, NH])
        buv_wide = sb("buv_wide", [DK, NH, 128])
        bo_rows = sb("bo_rows", [128, D])
        qr = sb("qr", [TOP + DL + 1, NH, DR])
        w_cat = sb("w_cat", [128, DC, CAT])
        b_cat = sb("b_cat", [CAT, 1])
        b_kv4 = sb("b_kv4", [128, 1])
        m_f = sb("m_f", [TOP + DL + 1, NH, QK])
        n_f = sb("n_f", [128, DC, D])
        out_bias = sb("out_bias", [128, D])
        eye = sb("eye", [128, 128])
        eye16 = sb("eye16", [128, 128], F16)
        half_power = sb("half_power", [128, 1])
        w_cat_hl = sb("w_cat_hl", [128, 2, DC, CAT], F16)
        m_hl = sb("m_hl", [TOP + DL + 1, 2, NH, QK], F16)
        n_hl = sb("n_hl", [128, 2, DC, D], F16)
        b_cat_ws = sb("b_cat_ws", [CAT, 1])
        b_kv_ws = sb("b_kv_ws", [128, 1])

        x = sb("x", [128, 4, D])
        stats = sb("stats", [128, 6])
        moments = sb("moments", [128, 2])
        var_eps = sb("var_eps", [128, 1])
        rstd = sb("rstd", [128, 1])
        shift = sb("shift", [128, 1])
        h2 = sb("h2", [128, 4, D])
        h2_bias = sb("h2_bias", [128, 4, D])
        ht_hl = sb("ht_hl", [128, 2, 2, DC, 128], F16)
        k_hl = sb("k_hl", [QK, 4, 2, PAIR], F16)
        c_hl = sb("c_hl", [TOP + DL + 1, 2, 2, PAIR], F16)
        v_hl = sb("v_hl", [128, 4, 2, DL], F16)
        LAST = NH - 3
        q_wide = sb("q_wide", [QK, 2, 2, 2, LAST * SEQ + 128], F16)
        q_hl = q_wide[:, :, :, :, 0:NH * SEQ].rearrange("r b a i (h q) -> r b a i h q", q=SEQ)
        row_max = sb("row_max", [TRIO, 6])
        row_sum = sb("row_sum", [TRIO, 6])
        row_inv = sb("row_inv", [TRIO, 6])
        prob = sb("prob", [TRIO, 2, 3, 2, SEQ])
        p_hl = sb("p_hl", [TRIO, 2, 2, 3, 2, SLOT], F16)
        pt_hl = sb("pt_hl", [128, 2, NH, SEQ], F16)
        ctx_hl = sb("ctx_hl", [128, 2, DC, 2, SLOT], F16)
        r = sb("r", [128, D])
        stats2 = sb("stats2", [128, 6])
        moments2 = sb("moments2", [128, 2])
        var_eps2 = sb("var_eps2", [128, 1])
        rstd2 = sb("rstd2", [128, 1])
        shift2 = sb("shift2", [128, 1])
        h3 = sb("h3", [128, 2, D])

        psX = ps("psX", [128, DC, 128])
        psCV = ps("psCV", [128, PAIR + DL])
        psC = psCV[0:CAT, 0:PAIR]
        psV = psCV[:, PAIR:]
        psO = ps("psO", [128, 512])
        psQ = [ps("psQ0", [QK, 2, NH // 2, SEQ]), ps("psQ1", [QK, 2, NH // 2, SEQ])]
        psS = ps("psS", [128, 512])
        scored = psS[0:TRIO, 0:6 * SEQ].rearrange("r (n k) -> r n k", n=6)
        psT = ps("psT", [128, 2, 3, 112], F16)
        psM = ps("psM", [128, 512])
        psA = [t[:, 0:DC * SEQ].rearrange("p (c q) -> p c q", c=DC) for t in (psM[:], psX[:].rearrange("p c n -> p (c n)"))]

        N_SETUP = 12
        run = lambda eng, body: run_steps(eng, PAIRS, 7, body)
        block = ctx.enter_context(nc.Block())

        @block.sync
        def _(sp):
            for dst, name in ((uq_t[:], "uq_t"), (uk_t[:], "uk_t"), (uv_t[:], "uv_t"), (wo[:], "wo1"), (buv[:], "buv"),
                              (qr[TOP:TOP + DL + 1], "qr"), (w_cat[:], "w_cat"), (b_cat[:], "b_cat"), (b_kv4[:], "b_kv4"),
                              (eye[:], "eye_f"), (eye16[:], "eye")):
                sp.dma_start(dst, io[name]).then_inc(S("setup_in"), 16)
            sp.dma_start(bo_rows[:], io["bo1"].broadcast_to([128, D])).then_inc(S("setup_in"), 16)
            sp.dma_start(x3[TOKENS:ROWS, :], io["zero_rows"]).then_inc(S("dummy_out"), 16)
            sp.wait_ge(S("zeroed"), 5)

            def step(st):
                if st.active(0):
                    p, b, hp, b4 = st.item(0)
                    wait(sp, S("h2"), p - 3)
                    for i in range(2):
                        sp.dma_start(x[i * SLOT:i * SLOT + SEQ, b4], acc_rows[bass.ds(p * PAIR + i * SEQ, SEQ), :]).then_inc(S(f"x_in{b4}"), 16)
                if st.active(7):
                    p, b, hp, _ = st.item(7)
                    wait(sp, S("h3"), p + 1)
                    for i in range(2):
                        sp.dma_start(x3[bass.ds(p * PAIR + i * SEQ, SEQ), :], h3[i * SLOT:i * SLOT + SEQ, b]).then_inc(S(f"h3_out{b}"), 16)

            run(sp, step)
            sp.wait_ge(S("dummy_out"), 16)
            for b in range(2):
                sp.wait_ge(S(f"h3_out{b}"), 32 * (PAIRS // 2))

        @block.tensor
        def _(pe):
            def products(out, left, right, chunks):
                todo = [(a, b, c) for c in range(chunks) for a, b in ((0, 0), (0, 1), (1, 0))]
                for n, (a, b, c) in enumerate(todo):
                    ins = nc.tensor.matmul(out, left(a, c), right(b, c), start=n == 0, stop=n == len(todo) - 1)
                return ins

            pe.wait_ge(S("setup_in"), 16 * N_SETUP)
            pe.wait_ge(S("buv_wide"), 1)
            for h in range(NH):
                ins = nc.tensor.matmul(psO[TOP:TOP + DL + 1, (DL + 1) * h:(DL + 1) * (h + 1)], uq_t[:, h], uk_t[:, h], start=True, stop=True)
            ins.then_inc(S("joined"), 1)
            for h in range(NH):
                ins = nc.tensor.matmul((psM, psS)[h // 4][32 * (h % 4):32 * (h % 4) + 32, 0:D], uv_t[:, h], wo[:, h], start=True, stop=True)
            ins.then_inc(S("joined"), 1)
            for h in range(NH):
                ins = nc.tensor.matmul(psX[:].rearrange("p c n -> p (c n)"), buv_wide[:, h], wo[:, h], start=h == 0, stop=h == NH - 1)
            ins.then_inc(S("joined"), 1)
            pe.wait_ge(S("w_ready"), 6)
            pe.wait_ge(S("ones"), 4)
            pe.wait_ge(S("zeroed"), 5)

            def turn(st):
                p, b, _, b4 = st.item(2)
                pe.wait_ge(S("h2"), p + 1)
                wait(pe, S("ht_low"), p)
                wait(pe, S("ctx_low"), 2 * (p - 3))
                for c in range(DC):
                    ins = nc.tensor.transpose(psX[:, c], h2[:, b4, c * 128:(c + 1) * 128], eye[:])
                ins.then_inc(S("turned"), 1)

            def latents(st):
                p, b, _, _ = st.item(2)
                pe.wait_ge(S("ht_high"), p + 1)
                pe.wait_ge(S("ht_low"), p + 1)
                wait(pe, S("latent_low"), p)
                by_image = lambda a, c: ht_hl[:, b, a, c].rearrange("p (i q) -> p i q", i=2)[:, :, 0:SEQ]
                products(psC.rearrange("p (i q) -> p i q", i=2), lambda a, c: w_cat_hl[:, a, c], by_image, DC)
                products(psV, lambda a, c: ht_hl[:, b, a, c], lambda a, c: w_cat_hl[:, a, c, 0:DL], DC).then_inc(S("latent"), 1)

            def queries(st):
                p, b, _, _ = st.item(3)
                pe.wait_ge(S("latent_high"), p + 1)
                pe.wait_ge(S("latent_low"), p + 1)
                wait(pe, S("q_low"), 2 * p)
                for h in range(NH):
                    ins = products(psQ[h // 4][:, :, h % 4], lambda a, c: m_hl[TOP:TOP + DL + 1, a, h],
                                   lambda a, c: c_hl[TOP:TOP + DL + 1, b, a].rearrange("r (i q) -> r i q", i=2), 1)
                    if h % 4 == 3:
                        ins.then_inc(S("q"), 1)

            def scores(st):
                p, b, _, b4 = st.item(4)
                pe.wait_ge(S("q_high"), 2 * p + 2)
                pe.wait_ge(S("q_low"), 2 * p + 2)
                wait(pe, S("shifted"), p)
                for t in range(3):
                    at = min(3 * t, LAST) * SEQ
                    for i in range(2):
                        ins = products(psS[:, (2 * t + i) * SEQ:(2 * t + i + 1) * SEQ], lambda a, c: q_wide[:, b, a, i, at:at + 128],
                                       lambda a, c: k_hl[:, b4, a, i * SEQ:(i + 1) * SEQ], 1)
                ins.then_inc(S("scored"), 1)

            def transpose_probs(st):
                p, b, _, _ = st.item(5)
                pe.wait_ge(S("p_high"), p + 1)
                pe.wait_ge(S("p_low"), p + 1)
                wait(pe, S("pt_copied"), 2 * p)
                for a in range(2):
                    for t in range(3):
                        ins = nc.tensor.transpose(psT[:, a, t, 0:TRIO], p_hl[:, b, a, t].rearrange("r i k -> r (i k)"), eye16[0:TRIO, 0:TRIO])
                ins.then_inc(S("pt"), 1)

            def mix(st):
                p, b, _, b4 = st.item(5)
                pe.wait_ge(S("pt_copied"), 2 * p + 2)
                wait(pe, S("ctx_low"), 2 * p)
                wait_alone(pe, S, "ht_low", min(p + 4, PAIRS) if isinstance(p, int) else p + 4)
                for i in range(2):
                    rows = slice(i * SLOT, i * SLOT + SEQ)
                    for h in range(NH):
                        j, c = h % 4, h // 4
                        for n, (a, z) in enumerate(((0, 0), (0, 1), (1, 0))):
                            ins = nc.tensor.matmul(psA[i][32 * j:32 * j + 32, c], v_hl[rows, b4, z], pt_hl[rows, a, h],
                                                   start=n == 0, stop=n == 2)
                    ins.then_inc(S("mixed"), 1)

            def output(st):
                p, b, _, _ = st.item(6)
                pe.wait_ge(S("ctx_high"), 2 * p + 2)
                pe.wait_ge(S("ctx_low"), 2 * p + 2)
                wait(pe, S("r"), p)
                products(psO[:, 0:D], lambda a, c: ctx_hl[:, a, c], lambda a, c: n_hl[:, a, c], DC).then_inc(S("projected"), 1)

            def step(st):
                if st.active(4):
                    scores(st)
                if st.active(6):
                    output(st)
                if st.active(2):
                    turn(st)
                if st.active(5):
                    transpose_probs(st)
                if st.active(3):
                    queries(st)
                if st.active(5):
                    mix(st)
                if st.active(2):
                    latents(st)

            run(pe, step)

        @block.scalar
        def _(act):
            act.wait_ge(S("setup_in"), 16 * N_SETUP)
            nc.scalar.activation(w_cat_hl[:, 0], w_cat[:], ACT.Copy, scale=WS).then_inc(S("w_high"), 1)
            act.wait_ge(S("m_ready"), 2)
            nc.scalar.activation(m_hl[TOP:TOP + DL + 1, 0], m_f[TOP:TOP + DL + 1], ACT.Copy, scale=16.0).then_inc(S("w_high"), 1)
            act.wait_ge(S("n_ready"), 2)
            nc.scalar.activation(n_hl[:, 0], n_f[:], ACT.Copy, scale=WS).then_inc(S("w_high"), 1)

            def step(st):
                if st.active(6):
                    p, b, _, _ = st.item(6)
                    wait(act, S("projected"), p)
                    for i in range(2):
                        act.wait_ge(S("mixed"), 2 * p + 1 + i)
                        nc.scalar.activation(ctx_hl[:, 0, :, i, 0:SEQ], psA[i], ACT.Identity, bias=b_kv_ws[:, 0:1]).then_inc(S("ctx_high"), 1)
                if st.active(3):
                    p, b, _, b4 = st.item(3)
                    act.wait_ge(S("latent"), p + 1)
                    wait(act, S("scored"), p - 3)
                    wait(act, S("q"), 2 * (p - 1))
                    wait(act, S("mixed"), 2 * (p - 3))
                    nc.scalar.activation(k_hl[0:TOP, b4, 0], psC[0:TOP], ACT.Identity, bias=b_cat_ws[0:TOP, 0:1])
                    nc.scalar.activation(c_hl[TOP:CAT, b, 0], psC[TOP:CAT], ACT.Identity, bias=b_cat_ws[TOP:CAT, 0:1])
                    nc.scalar.activation(v_hl[:, b4, 0], psV, ACT.Copy).then_inc(S("latent_high"), 1)
                if st.active(1):
                    p, b, _, b4 = st.item(1)
                    act.wait_ge(S("shift"), p + 1)
                    wait(act, S("turned"), p - 3)
                    wait(act, S("h2_bias"), p - 3)
                    nc.scalar.activation(h2[:, b4], x[:, b4], ACT.Identity, scale=rstd[:, 0:1], bias=shift[:, 0:1]).then_inc(S("h2"), 1)
                if st.active(7):
                    p, b, hp, _ = st.item(7)
                    act.wait_ge(S("shift2"), p + 1)
                    wait(act, S(f"h3_out{b}"), 32 * hp)
                    nc.scalar.activation(h3[:, b], r[:], ACT.Identity, scale=rstd2[:, 0:1], bias=shift2[:, 0:1]).then_inc(S("h3"), 1)
                if st.active(4):
                    p, b, _, _ = st.item(4)
                    act.wait_ge(S("shifted"), p + 1)
                    nc.scalar.activation(prob[:, b], prob[:, b], ACT.Exp, scale=1.0 / (QS * WS * (DK + DR) ** 0.5)).then_inc(S("exp"), 1)
                if st.active(2):
                    p, b, _, b4 = st.item(2)
                    act.wait_ge(S("turned"), p + 1)
                    wait(act, S("latent"), p - 1)
                    nc.scalar.activation(ht_hl[:, b, 0], psX[:], ACT.Copy).then_inc(S("ht_high"), 1)
                if st.active(5):
                    p, b, _, _ = st.item(5)
                    act.wait_ge(S("pt"), p + 1)
                    wait(act, S("mixed"), 2 * p)
                    nc.scalar.activation(pt_hl[:, :, 0:6].rearrange("k a (t h) q -> k a t (h q)", t=2), psT[:, :, 0:2, 0:TRIO], ACT.Copy).then_inc(S("pt_copied"), 1)
                    nc.scalar.activation(pt_hl[:, :, 6:8].rearrange("k a h q -> k a (h q)"), psT[:, :, 2, SEQ:TRIO], ACT.Copy).then_inc(S("pt_copied"), 1)
                if st.active(3):
                    p, b, _, _ = st.item(3)
                    wait(act, S("scored"), p - 1)
                    for g in range(2):
                        act.wait_ge(S("q"), 2 * p + g + 1)
                        nc.scalar.activation(q_hl[:, b, 0, :, 4 * g:4 * g + 4], psQ[g][:], ACT.Copy, scale=QS / (16.0 * WS)).then_inc(S("q_high"), 1)
                if st.active(4):
                    p, b, _, _ = st.item(4)
                    act.wait_ge(S("prob"), p + 1)
                    wait(act, S("pt"), p - 1)
                    nc.scalar.activation(p_hl[:, b, 0, :, :, 0:SEQ], prob[:, b], ACT.Copy).then_inc(S("p_high"), 1)

            run(act, step)

        @block.gpsimd
        def _(pool):
            for t, v in ((p_hl, 0.0), (ctx_hl, 0.0), (x, 0.0), (half_power, -0.5), (q_wide, 0.0)):
                nc.gpsimd.memset(t[:], v).then_inc(S("zeroed"), 1)
            pool.wait_ge(S("zeroed"), 5)

            def step(st):
                if st.active(4):
                    p, b, _, b4 = st.item(4)
                    wait(pool, S("r"), p - 3)
                    pool.wait_ge(S("h2"), p + 1)
                    if isinstance(p, int) and p == 0:
                        pool.wait_ge(S("w_ready"), 6)
                    nc.gpsimd.tensor_tensor(h2_bias[:, b4], h2[:, b4], out_bias[:], ALU.add).then_inc(S("h2_bias"), 1)
                if st.active(6):
                    p, b, _, _ = st.item(6)
                    pool.wait_ge(S("var_eps2"), p + 1)
                    wait(pool, S("h3"), p)
                    nc.gpsimd.tensor_tensor(rstd2[:], var_eps2[:], half_power[:], ALU.pow).then_inc(S("rstd2"), 1)
                if st.active(0):
                    p, b, _, b4 = st.item(0)
                    pool.wait_ge(S("var_eps"), p + 1)
                    wait(pool, S("h2"), p)
                    nc.gpsimd.tensor_tensor(rstd[:], var_eps[:], half_power[:], ALU.pow).then_inc(S("rstd"), 1)
                if st.active(4):
                    p, b, _, _ = st.item(4)
                    pool.wait_ge(S("p_high"), p + 1)
                    nc.gpsimd.tensor_tensor(p_hl[:, b, 1, :, :, 0:SEQ], prob[:, b], p_hl[:, b, 0, :, :, 0:SEQ], ALU.subtract).then_inc(S("p_low"), 1)

            run(pool, step)

        @block.vector
        def _(dve):
            hl = lambda t, a: t[:, a].rearrange("p c n -> p (c n)")
            rows = slice(TOP, TOP + DL + 1)
            nc.vector.memset(k_hl[TOP:TOP + 1, :, 1], 0.0).then_inc(S("ones"), 1)
            nc.vector.memset(k_hl[TOP:TOP + 1, :, 0], WS).then_inc(S("ones"), 1)
            nc.vector.memset(c_hl[CAT:CAT + 1, :, 1], 0.0).then_inc(S("ones"), 1)
            nc.vector.memset(c_hl[CAT:CAT + 1, :, 0], WS).then_inc(S("ones"), 1)
            dve.wait_ge(S("setup_in"), 16 * N_SETUP)
            nc.vector.tensor_copy(buv_wide[:], buv[:].unsqueeze(2).broadcast_to([DK, NH, 128])).then_inc(S("buv_wide"), 1)
            dve.wait_ge(S("w_high"), 1)
            nc.vector.scalar_tensor_tensor(hl(w_cat_hl, 1), w_cat[:].rearrange("p c n -> p (c n)"), WS, hl(w_cat_hl, 0), ALU.mult, ALU.subtract).then_inc(S("w_ready"), 1)
            nc.vector.tensor_scalar(b_cat_ws[:], b_cat[:], WS, None, ALU.mult).then_inc(S("w_ready"), 1)
            nc.vector.tensor_scalar(b_kv_ws[:], b_kv4[:], WS, None, ALU.mult).then_inc(S("w_ready"), 1)
            dve.wait_ge(S("joined"), 1)
            joined = psO[rows, 0:NH * (DL + 1)].rearrange("r (h n) -> r h n", h=NH)
            nc.vector.tensor_copy(m_f[rows, :, 0:DL], joined[:, :, 0:DL])
            nc.vector.tensor_copy(m_f[rows, :, QK - 1:QK], joined[:, :, DL:DL + 1]).then_inc(S("m_ready"), 1)
            nc.vector.tensor_copy(m_f[rows, :, DL:DL + DR], qr[rows]).then_inc(S("m_ready"), 1)
            dve.wait_ge(S("joined"), 3)
            nc.vector.tensor_copy(n_f[:, 0], psM[:, 0:D]).then_inc(S("n_ready"), 1)
            nc.vector.tensor_copy(n_f[:, 1], psS[:, 0:D]).then_inc(S("n_ready"), 1)
            nc.vector.tensor_tensor(out_bias[:], psX[:].rearrange("p c n -> p (c n)"), bo_rows[:], ALU.add).then_inc(S("w_ready"), 1)
            dve.wait_ge(S("w_high"), 3)
            dve.wait_ge(S("m_ready"), 2)
            dve.wait_ge(S("n_ready"), 2)
            nc.vector.scalar_tensor_tensor(m_hl[rows, 1].rearrange("r h n -> r (h n)"), m_f[rows].rearrange("r h n -> r (h n)"), 16.0,
                                           m_hl[rows, 0].rearrange("r h n -> r (h n)"), ALU.mult, ALU.subtract).then_inc(S("w_ready"), 1)
            nc.vector.scalar_tensor_tensor(hl(n_hl, 1), n_f[:].rearrange("p c n -> p (c n)"), WS, hl(n_hl, 0), ALU.mult, ALU.subtract).then_inc(S("w_ready"), 1)

            def step(st):
                if st.active(6):
                    p, b, _, _ = st.item(6)
                    for i in range(2):
                        dve.wait_ge(S("ctx_high"), 2 * p + 1 + i)
                        nc.vector.scalar_tensor_tensor(ctx_hl[:, 1, :, i, 0:SEQ], psA[i], b_kv_ws[:, 0:1], ctx_hl[:, 0, :, i, 0:SEQ],
                                                       ALU.add, ALU.subtract).then_inc(S("ctx_low"), 1)
                if st.active(3):
                    p, b, _, b4 = st.item(3)
                    dve.wait_ge(S("latent_high"), p + 1)
                    nc.vector.scalar_tensor_tensor(k_hl[0:TOP, b4, 1], psC[0:TOP], b_cat_ws[0:TOP, 0:1], k_hl[0:TOP, b4, 0], ALU.add, ALU.subtract)
                    nc.vector.scalar_tensor_tensor(c_hl[TOP:CAT, b, 1], psC[TOP:CAT], b_cat_ws[TOP:CAT, 0:1], c_hl[TOP:CAT, b, 0], ALU.add, ALU.subtract)
                    nc.vector.tensor_tensor(v_hl[:, b4, 1], psV, v_hl[:, b4, 0], ALU.subtract).then_inc(S("latent_low"), 1)
                if st.active(1):
                    p, _, _, _ = st.item(1)
                    dve.wait_ge(S("rstd"), p + 1)
                    wait(dve, S("h2"), p)
                    nc.vector.scalar_tensor_tensor(shift[:], moments[:, 0:1], -1.0, rstd[:], ALU.mult, ALU.mult).then_inc(S("shift"), 1)
                if st.active(7):
                    p, _, _, _ = st.item(7)
                    dve.wait_ge(S("rstd2"), p + 1)
                    wait(dve, S("h3"), p)
                    nc.vector.scalar_tensor_tensor(shift2[:], moments2[:, 0:1], -1.0, rstd2[:], ALU.mult, ALU.mult).then_inc(S("shift2"), 1)
                if st.active(4):
                    p, b, _, _ = st.item(4)
                    dve.wait_ge(S("scored"), p + 1)
                    nc.vector.tensor_reduce(row_max[:], scored, AX.X, ALU.max).then_inc(S("row_max"), 1)
                    dve.wait_ge(S("row_max"), p + 1)
                    wait(dve, S("p_low"), p - 1)
                    nc.vector.tensor_tensor(prob[:, b].rearrange("r t i k -> r (t i) k"), scored, row_max[:].unsqueeze(2).broadcast_to([TRIO, 6, SEQ]), ALU.subtract).then_inc(S("shifted"), 1)
                if st.active(6):
                    p, b, hp, b4 = st.item(6)
                    dve.wait_ge(S("projected"), p + 1)
                    dve.wait_ge(S("h2_bias"), p + 1)
                    wait(dve, S("h3"), p)
                    nc.vector.scalar_tensor_tensor(r[:], psO[:, 0:D], 1.0 / (WS * WS), h2_bias[:, b4], ALU.mult, ALU.add).then_inc(S("r"), 1)
                if st.active(2):
                    p, b, _, b4 = st.item(2)
                    dve.wait_ge(S("ht_high"), p + 1)
                    nc.vector.tensor_tensor(ht_hl[:, b, 1], psX[:], ht_hl[:, b, 0], ALU.subtract).then_inc(S("ht_low"), 1)
                if st.active(6):
                    p, _, _, _ = st.item(6)
                    dve.wait_ge(S("r"), p + 1)
                    nc.vector.bn_stats(stats2[:], r[:]).then_inc(S("stats2"), 1)
                if st.active(4):
                    p, b, _, _ = st.item(4)
                    dve.wait_ge(S("exp"), p + 1)
                    nc.vector.tensor_reduce(row_sum[:], prob[:, b].rearrange("r t i k -> r (t i) k"), AX.X, ALU.add).then_inc(S("row_sum"), 1)
                if st.active(6):
                    p, _, _, _ = st.item(6)
                    wait_alone(dve, S, "stats2", p + 1)
                    wait_alone(dve, S, "shift2", p)
                    nc.vector.bn_aggr(moments2[:], stats2[:]).then_inc(S("moments2"), 1)
                if st.active(0):
                    p, _, _, b4 = st.item(0)
                    dve.wait_ge(S(f"x_in{b4}"), 32 * st.h + 32)
                    nc.vector.bn_stats(stats[:], x[:, b4]).then_inc(S("stats"), 1)
                if st.active(6):
                    p, _, _, _ = st.item(6)
                    dve.wait_ge(S("moments2"), p + 1)
                    nc.vector.tensor_scalar(var_eps2[:], moments2[:, 1:2], EPS, None, ALU.add).then_inc(S("var_eps2"), 1)
                if st.active(4):
                    p, _, _, _ = st.item(4)
                    dve.wait_ge(S("row_sum"), p + 1)
                    nc.vector.reciprocal(row_inv[:], row_sum[:]).then_inc(S("row_inv"), 1)
                if st.active(0):
                    p, _, _, _ = st.item(0)
                    wait_alone(dve, S, "stats", p + 1)
                    wait_alone(dve, S, "shift", p)
                    nc.vector.bn_aggr(moments[:], stats[:]).then_inc(S("moments"), 1)
                if st.active(4):
                    p, b, _, _ = st.item(4)
                    flat = prob[:, b].rearrange("r t i k -> r (t i) k")
                    dve.wait_ge(S("row_inv"), p + 1)
                    nc.vector.tensor_tensor(flat, flat, row_inv[:].unsqueeze(2).broadcast_to([TRIO, 6, SEQ]), ALU.mult).then_inc(S("prob"), 1)
                if st.active(0):
                    p, _, _, _ = st.item(0)
                    dve.wait_ge(S("moments"), p + 1)
                    nc.vector.tensor_scalar(var_eps[:], moments[:, 1:2], EPS, None, ALU.add).then_inc(S("var_eps"), 1)
                if st.active(3):
                    p, b, _, _ = st.item(3)
                    for g in range(2):
                        dve.wait_ge(S("q_high"), 2 * p + g + 1)
                        part = lambda a: q_hl[:, b, a, :, 4 * g:4 * g + 4].rearrange("r i h q -> r i (h q)")
                        nc.vector.scalar_tensor_tensor(part(1), psQ[g][:].rearrange("r i h q -> r i (h q)"), QS / (16.0 * WS), part(0),
                                                       ALU.mult, ALU.subtract).then_inc(S("q_low"), 1)

            run(dve, step)


def build_final_norm(nc, acc_rows, out_rows):
    with ExitStack() as ctx:
        def sb(name, shape):
            return ctx.enter_context(nc.sbuf_tensor("f_" + name, shape, F32))

        S = Sems(nc, "f")
        ctx.callback(S.clear)
        R = SEQ * 3
        NT = -(-TOKENS // 128)
        size = lambda t: min(128, TOKENS - 128 * t)
        x = sb("x", [128, 4, D])
        y = sb("y", [128, 4, D])
        stats = sb("stats", [128, 4, 6])
        moments = sb("moments", [128, 4, 2])
        var_eps = sb("var_eps", [128, 4])
        rstd = sb("rstd", [128, 4])
        half_power = sb("half_power", [128, 1])
        block = ctx.enter_context(nc.Block())

        @block.sync
        def _(sp):
            for t in range(NT):
                if t >= 4:
                    sp.wait_ge(S("y"), t - 3)
                sp.dma_start(x[0:size(t), t % 4], acc_rows[t * 128:t * 128 + size(t), :]).then_inc(S(f"x_in{t % 4}"), 16)

        @block.scalar
        def _(act):
            for t in range(NT):
                act.wait_ge(S("y"), t + 1)
                act.dma_start(out_rows[t * 128:t * 128 + size(t), :], y[0:size(t), t % 4]).then_inc(S(f"y_out{t % 4}"), 16)
            for b in range(4):
                act.wait_ge(S(f"y_out{b}"), 16 * len(range(b, NT, 4)))

        @block.gpsimd
        def _(pool):
            nc.gpsimd.memset(half_power[:], -0.5).then_inc(S("half_power"), 1)
            pool.wait_ge(S("half_power"), 1)
            for t in range(NT):
                b, n = t % 4, size(t)
                pool.wait_ge(S("var_eps"), t + 1)
                nc.gpsimd.tensor_tensor(rstd[0:n, b:b + 1], var_eps[0:n, b:b + 1], half_power[0:n], ALU.pow).then_inc(S("rstd"), 1)

        @block.vector
        def _(dve):
            def scale(t):
                b, n = t % 4, size(t)
                dve.wait_ge(S("rstd"), t + 1)
                if t >= 4:
                    dve.wait_ge(S(f"y_out{b}"), 16 * (t // 4))
                nc.vector.tensor_scalar(y[0:n, b], x[0:n, b], moments[0:n, b, 0:1], rstd[0:n, b:b + 1], ALU.subtract, ALU.mult).then_inc(S("y"), 1)

            for t in range(NT):
                b, n = t % 4, size(t)
                dve.wait_ge(S(f"x_in{b}"), 16 * (t // 4 + 1))
                nc.vector.bn_stats(stats[0:n, b], x[0:n, b]).then_inc(S("stats"), 1)
                if t >= 1:
                    scale(t - 1)
                dve.wait_ge(S("stats"), t + 1)
                nc.vector.bn_aggr(moments[0:n, b], stats[0:n, b]).then_inc(S("moments"), 1)
                dve.wait_ge(S("moments"), t + 1)
                nc.vector.tensor_scalar(var_eps[0:n, b:b + 1], moments[0:n, b, 1:2], EPS, None, ALU.add).then_inc(S("var_eps"), 1)
            scale(NT - 1)


def build(nc, io, out):
    x1, sum0, x3, sum1 = (nc.dram_tensor(n, (ROWS, D), F32).ap() for n in ("x1", "sum0", "x3", "sum1"))
    build_attention0(nc, io, x1)
    for layer, x, total in ((0, x1, sum0), (1, x3, sum1)):
        if layer == 1:
            build_attention1(nc, io, sum0, x3)
        with ExitStack() as ctx:
            plan = Plan(nc, ctx, layer, 1 if layer == 0 else 0)
            build_routing(nc, io, x, total, plan, layer)
            build_experts(nc, io, x, total, plan, layer)
    build_final_norm(nc, sum1, out)


def lay_out(x, **w):
    import numpy as np

    def feat(v):
        return np.ascontiguousarray(v.reshape(-1, 128).T)

    def rows(m):
        k, n = m.shape
        return np.ascontiguousarray(m.reshape(k // 128, 128, n).transpose(1, 0, 2))

    p = x.reshape(PAIRS, 2, 3, GRID, 16, GRID, 16).transpose(0, 2, 4, 6, 1, 3, 5)
    p = p.reshape(PAIRS, PC, 128, 2 * PATCHES).transpose(0, 2, 1, 3)
    part = np.arange(128)
    a = {
        "patches": p,
        "emb_w": rows(w["L0_tok_W"].T),
        "qkvo_w": np.stack([rows(w[f"L0_attn_W{z}"].T) for z in "qkvo"], axis=1),
        "bias0": np.stack([feat(w["L0_tok_b"])] + [feat(w[f"L0_attn_b{z}"]) for z in "qkv"], axis=1),
        "pos_t": w["L0_tok_pos_embed"][0].T.reshape(DC, 128, SEQ).transpose(1, 0, 2),
        "cls_t": feat(w["L0_tok_cls_token"][0, 0])[:, :, None],
        "bo": w["L0_attn_bo"][None],
        "head_mask": (part[:, None] // 16 == np.arange(8)[None]).astype(np.float32),
        "eye": np.eye(128, dtype=np.float16),
    }

    experts0 = [(w["L0_ffn_Wg_s"], w["L0_ffn_Wu_s"], w["L0_ffn_Wd_s"])]
    experts0 += [(w["L0_ffn_Wg"][e], w["L0_ffn_Wu"][e], w["L0_ffn_Wd"][e]) for e in range(TE)]
    tok = np.arange(TOK_TILES * 128).reshape(TOK_TILES, 128).T
    te = TOK_TILES * TE
    a |= {
        "experts0": np.stack([np.concatenate([rows(m.T).reshape(128, -1) for m in e], axis=1) for e in experts0]),
        "experts1": np.stack([np.concatenate([rows(w["L1_ffn_W1"][e]).reshape(128, -1), rows(w["L1_ffn_W2"][e]).reshape(128, -1)], axis=1)
                              for e in range(TE)]),
        "b1": np.stack([feat(w["L1_ffn_b1"][e]) for e in range(TE)]),
        "b2": w["L1_ffn_b2"][:, None, :],
        "wr0": rows(w["L0_ffn_Wr"].T),
        "wr1": rows(w["L1_ffn_Wr"]),
        "router_bias0": w["L0_ffn_rb"][None],
        "router_bias1": w["L1_ffn_br"][None],
        "eye_f": np.eye(128, dtype=np.float32),
        "below": np.triu(np.ones((128, 128), np.float16), 1),
        "lane": np.broadcast_to(np.arange(128, dtype=np.float16), (128, 128)),
        "place": np.broadcast_to(np.arange(TE, 0, -1, dtype=np.float32), (128, TE)),
        "valid": (tok < TOKENS).astype(np.float32),
        "all_index": tok.astype(np.int32),
        "tile_number": np.broadcast_to(np.repeat(np.arange(TOK_TILES), TE), (128, 1, te)).astype(np.float16),
        "lane_number": (part[:, None] + 1).astype(np.float32),
        "dummy_row": (TOKENS + 1 + part[:, None]).astype(np.float32),
        "steps": (128.0 * np.arange(1, TOK_TILES))[None].astype(np.float32),
    }
    heads = lambda m: m.reshape(m.shape[0], 8, -1)
    with_bias = lambda m, b: np.concatenate([m, b[None]], axis=0)
    a |= {
        "uq_t": heads(with_bias(w["L1_attn_W_UQ"], w["L1_attn_b_UQ"])).transpose(2, 1, 0),
        "uk_t": heads(with_bias(w["L1_attn_W_UK"], w["L1_attn_b_UK"])).transpose(2, 1, 0),
        "uv_t": heads(w["L1_attn_W_UV"]).transpose(2, 1, 0),
        "wo1": w["L1_attn_W_O"].reshape(8, 128, D).transpose(1, 0, 2),
        "buv": w["L1_attn_b_UV"].reshape(8, 128).T,
        "qr": heads(with_bias(w["L1_attn_W_QR"], w["L1_attn_b_QR"])),
        "w_cat": rows(np.concatenate([w["L1_attn_W_DKV"], w["L1_attn_W_KR"], w["L1_attn_W_DQ"]], axis=1)),
        "b_cat": np.concatenate([w["L1_attn_b_DKV"], w["L1_attn_b_KR"], w["L1_attn_b_DQ"]])[:, None],
        "b_kv4": np.tile(w["L1_attn_b_DKV"], 4)[:, None],
        "zero_rows": np.zeros((DUMMY, D), np.float32),
        "bo1": w["L1_attn_b_O"][None],
    }
    return {k: np.ascontiguousarray(v) for k, v in a.items()}


def kernel(**inputs):
    import numpy as np
    import concourse.bacc as bacc
    from concourse.bass_utils import run_bass_kernel_spmd

    arrays = lay_out(**{k: np.asarray(v) for k, v in inputs.items()})
    nc = bacc.Bacc("TRN2", target_bir_lowering=False, num_devices=1)
    io = {k: nc.dram_tensor(k, v.shape, mybir.dt.from_np(v.dtype), kind="ExternalInput").ap() for k, v in arrays.items()}
    out = nc.dram_tensor("out", (TOKENS, D), F32, kind="ExternalOutput").ap()
    build(nc, io, out)
    result = run_bass_kernel_spmd(nc, [arrays], core_ids=[0])
    return result.results[0]["out"].reshape(IMAGES, SEQ, D)
```

```python
from contextlib import ExitStack

import concourse.bass as bass
from concourse import mybir

F32 = mybir.dt.float32
F16 = mybir.dt.float16
I32 = mybir.dt.int32
ALU = mybir.AluOpType
ACT = mybir.ActivationFunctionType
AX = mybir.AxisListType

IMAGES = 64
GRID = 6
PATCHES = GRID * GRID
SEQ = PATCHES + 1
TOKENS = IMAGES * SEQ
D = 256
DC = D // 128
PATCH_DIM = 768
PC = PATCH_DIM // 128
PAIRS = IMAGES // 2
SLOT = 64
PAIR = 2 * SEQ
TRIO = 3 * SEQ
EPS = 1e-5
WS = 64.0

DUMMY = 128
ROWS = TOKENS + DUMMY
TOK_TILES = -(-TOKENS // 128)
TE = 8


class Sems:

    def __init__(self, nc, prefix):
        self.nc, self.prefix, self.made = nc, prefix, {}

    def __call__(self, name):
        if name not in self.made:
            self.made[name] = self.nc.alloc_semaphore(f"{self.prefix}_{name}")
        return self.made[name]

    def clear(self):
        self.nc.clear_and_free_semaphores(list(self.made.values()))
        self.nc.all_engine_barrier()


def wait(eng, sem, count):
    if isinstance(count, int) and count <= 0:
        return
    eng.wait_ge(sem, count)


def wait_alone(eng, S, name, count):
    wait(eng, S(name), count)
    if not isinstance(count, int):
        eng.sem_inc(S("passed"), 1)


class Resident:

    def __init__(self, nc, ctx, name, inputs):
        self.tensors, self.transfers = {}, []
        for key, shape, dt, start, src in inputs:
            self.tensors[key] = ctx.enter_context(nc.sbuf_tensor(f"{name}_{key}", shape, dt))
            self.transfers.append((self.tensors[key][start:], src))

    def __getitem__(self, key):
        return self.tensors[key]

    def load(self, eng, sem):
        for dst, src in self.transfers:
            eng.dma_start(dst, src).then_inc(sem, 16)
        return 16 * len(self.transfers)


class Step:

    def __init__(self, h, u, unroll, total):
        self.h, self.u, self.unroll, self.total = h, u, unroll, total

    def active(self, skew):
        if not isinstance(self.h, int):
            return True
        return 0 <= self.unroll * self.h + self.u - skew < self.total

    def item(self, skew):
        s = self.u - skew
        return (self.h * self.unroll + s, s % 2, self.h * (self.unroll // 2) + s // 2, s % self.unroll)


def run_steps(eng, total, skews, body, unroll=4):
    first = -(-(skews + 2) // unroll)
    last = total // unroll
    for h in range(first):
        for u in range(unroll):
            body(Step(h, u, unroll, total))
    with eng.Fori(first, last) as h:
        for u in range(unroll):
            body(Step(h, u, unroll, total))
    for t in range(last * unroll, total + skews):
        body(Step(t // unroll, t % unroll, unroll, total))
def build_attention0(nc, io, x1, later):
    HEADS, HD = 16, 16
    HC = 8
    with ExitStack() as ctx:
        def sb(name, shape, dt):
            return ctx.enter_context(nc.sbuf_tensor("a0_" + name, shape, dt))

        def ps(name, shape, dt=F32):
            return ctx.enter_context(nc.psum_tensor("a0_" + name, shape, dt))

        S = Sems(nc, "a0")
        ctx.callback(S.clear)

        w_stage = sb("w_stage", [128, PC, D], F32)
        w_emb = sb("w_emb", [128, 2, PC, D], F16)
        w_stage4 = sb("w_stage4", [128, 4, DC, D], F32)
        w_qkvo = sb("w_qkvo", [128, 2, 4, DC, D], F16)
        eye = sb("eye", [128, 128], F16)
        eye_ws = sb("eye_ws", [128, 128], F16)
        bias_in = sb("bias_in", [128, 4, DC], F32)
        bias_ws = sb("bias_ws", [128, 4, DC], F32)
        pos_t = sb("pos_t", [128, DC, SEQ], F32)
        cls_t = sb("cls_t", [128, DC, 1], F32)
        bo = sb("bo", [1, D], F32)
        bo_hl = sb("bo_hl", [1, 2, D], F16)
        ones = sb("ones", [1, 128], F16)
        head_mask = sb("head_mask", [128, HC], F32)
        odd_mask = sb("odd_mask", [128, 1], F32)
        even_mask = sb("even_mask", [128, 1], F32)
        half_power = sb("half_power", [128, 1], F32)

        x_in = sb("x_in", [128, 4, PC, 2 * PATCHES], F32)
        x_hl = sb("x_hl", [128, 2, 2, PC, 2 * PATCHES], F16)
        h0 = sb("h0", [128, 4, DC, 2, SEQ], F32)
        h0_hl = sb("h0_hl", [128, 4, 2, DC, 2, SLOT], F16)
        q_hl = sb("q_hl", [128, 2, 2, DC, PAIR], F16)
        k_hl = sb("k_hl", [128, 2, 2, DC, PAIR], F16)
        v_hl = sb("v_hl", [128, 4, 2, D], F16)
        LAST = HC - 3
        q_wide = sb("q_wide", [128, 2, 2, DC, 2, LAST * SEQ + 128], F16)
        qbd = q_wide[:, :, :, :, :, 0:HC * SEQ].rearrange("p b a c i (h q) -> p b a c i h q", q=SEQ)
        row_max = sb("row_max", [TRIO, 12], F32)
        row_sum = sb("row_sum", [TRIO, 12], F32)
        row_inv = sb("row_inv", [TRIO, 12], F32)
        prob = sb("prob", [TRIO, 2, 12, SEQ], F32)
        p_hl = sb("p_hl", [TRIO, 2, 2, 6, 2, SLOT], F16)
        pt_hl = sb("pt_hl", [128, 2, DC, 3 * TRIO], F16)
        odd = sb("odd", [128, 2, DC, SEQ], F32)
        ctx_f = sb("ctx_f", [128, DC, 2, SLOT], F32)
        ctx_hl = sb("ctx_hl", [128, 2, DC, 2, SLOT], F16)
        stats = sb("stats", [128, 6], F32)
        moments = sb("moments", [128, 2], F32)
        var_eps = sb("var_eps", [128, 1], F32)
        rstd = sb("rstd", [128, 1], F32)
        h1 = sb("h1", [128, 2, D], F32)

        psEQK = ps("psEQK", [128, DC * 2 * PATCHES + 2 * DC * PAIR])
        psE = psEQK[:, 0:DC * 2 * PATCHES].rearrange("p (c n) -> p c n", c=DC)
        psQK = psEQK[:, DC * 2 * PATCHES:].rearrange("p (z c n) -> p z c n", z=2, c=DC)
        psO = ps("psO", [128, D])
        psV = ps("psV", [128, D])
        psS = ps("psS", [128, 2, 6, SEQ])
        psT0 = ps("psT0", [128, 1024], F16)
        psT1 = ps("psT1", [128, 1024], F16)
        psC = [ps("psC0", [128, DC, PAIR]), ps("psC1", [128, DC, PAIR])]
        psT = [psT0[:, 0:672].rearrange("p (t c) -> p t c", t=6), psT1[:, 0:672].rearrange("p (t c) -> p t c", t=6)]

        N_SETUP = 8
        run = lambda eng, body: run_steps(eng, PAIRS, 6, body)
        block = ctx.enter_context(nc.Block())

        @block.sync
        def _(sp):
            sp.dma_start(w_stage[:], io["emb_w"]).then_inc(S("setup_in"), 16)
            sp.dma_start(w_stage4[:], io["qkvo_w"]).then_inc(S("setup_in"), 16)
            sp.dma_start(bias_in[:], io["bias0"]).then_inc(S("setup_in"), 16)
            sp.dma_start(pos_t[:], io["pos_t"]).then_inc(S("setup_in"), 16)
            sp.dma_start(cls_t[:], io["cls_t"]).then_inc(S("setup_in"), 16)
            sp.dma_start(bo[:], io["bo"]).then_inc(S("setup_in"), 16)
            sp.dma_start(head_mask[:], io["head_mask"]).then_inc(S("setup_in"), 16)
            sp.dma_start(eye[:], io["eye"]).then_inc(S("setup_in"), 16)

            sp.dma_start(x1[TOKENS:ROWS, :], io["zero_rows"]).then_inc(S("dummy_out"), 16)

            def step(st):
                if st.active(0):
                    p, b, hp, b4 = st.item(0)
                    wait(sp, S("x_high"), p - 3)
                    wait(sp, S("x_low"), p - 3)
                    sp.dma_start(x_in[:, b4], io["patches"][bass.ds(p, 1)].rearrange("a k c n -> k (a c) n")).then_inc(S(f"x_in{b4}"), 16)
                if st.active(6):
                    p, b, hp, _ = st.item(6)
                    wait(sp, S("h1"), p + 1)
                    for i in range(2):
                        sp.dma_start(x1[bass.ds(p * PAIR + i * SEQ, SEQ), :],
                                     h1[i * SLOT:i * SLOT + SEQ, b]).then_inc(S(f"h1_out{b}"), 16)

            loaded = later.load(sp, S("later_in"))
            run(sp, step)
            sp.wait_ge(S("later_in"), loaded)
            sp.wait_ge(S("dummy_out"), 16)
            for b in range(2):
                sp.wait_ge(S(f"h1_out{b}"), 32 * (PAIRS // 2))

        @block.tensor
        def _(pe):
            def products(out, left, right, first=True, last=True):
                n = 0
                todo = [(a, b, c) for c in left[1] for a, b in ((0, 0), (0, 1), (1, 0))]
                for a, b, c in todo:
                    ins = nc.tensor.matmul(out, left[0](a, c), right[0](b, c), start=first and n == 0,
                                           stop=last and n == len(todo) - 1)
                    n += 1
                return ins

            def embed(st):
                p, b, _, _ = st.item(1)
                if isinstance(p, int) and p == 0:
                    pe.wait_ge(S("w_ready"), 2)
                pe.wait_ge(S("x_high"), p + 1)
                pe.wait_ge(S("x_low"), p + 1)
                wait(pe, S("h0"), 2 * p)
                wait(pe, S("qk_low"), 2 * p)
                for m in range(DC):
                    ins = products(psE[:, m], (lambda a, c: w_emb[:, a, c, m * 128:(m + 1) * 128], range(PC)),
                                   (lambda a, c: x_hl[:, b, a, c], range(PC)))
                ins.then_inc(S("embedded"), 1)

            def project(st):
                p, b, _, b4 = st.item(2)
                if isinstance(p, int) and p == 0:
                    pe.wait_ge(S("w_ready"), 4)
                pe.wait_ge(S("h0_high"), p + 1)
                pe.wait_ge(S("h0_low"), p + 1)
                wait(pe, S("qk_low"), 2 * p)
                for z in range(2):
                    for m in range(DC):
                        ins = products(psQK[:, z, m].rearrange("p (i q) -> p i q", i=2), (lambda a, c: w_qkvo[:, a, z, c, m * 128:(m + 1) * 128], range(DC)),
                                       (lambda a, c: h0_hl[:, b4, a, c, :, 0:SEQ], range(DC)))
                ins.then_inc(S("qk"), 1)

            def project_values(st):
                p, b, _, b4 = st.item(2)
                wait(pe, S("v_low"), p)
                products(psV[:], (lambda a, c: h0_hl[:, b4, a, c], range(DC)),
                         (lambda a, c: w_qkvo[:, a, 2, c], range(DC))).then_inc(S("v"), 1)

            def transpose_probs(st):
                p, b, _, _ = st.item(4)
                pe.wait_ge(S("p_high"), p + 1)
                pe.wait_ge(S("p_low"), p + 1)
                wait(pe, S("pt_high"), p)
                wait(pe, S("pt_low"), p)
                for a in range(2):
                    for t in range(6):
                        ins = nc.tensor.transpose(psT[a][:, t, 0:TRIO], p_hl[:, b, a, t].rearrange("r i k -> r (i k)"), eye[0:TRIO, 0:TRIO])
                    ins.then_inc(S("pt"), 1)

            def scores(st):
                p, b, _, _ = st.item(3)
                pe.wait_ge(S("qbd_high"), p + 1)
                pe.wait_ge(S("qbd_low"), p + 1)
                wait(pe, S("shifted"), p)
                for i in range(2):
                    for c in range(DC):
                        for t in range(3):
                            at = min(3 * t, LAST) * SEQ
                            for n, (a, z) in enumerate(((0, 0), (0, 1), (1, 0))):
                                ins = nc.tensor.matmul(psS[:, i, 3 * c + t], q_wide[:, b, a, c, i, at:at + 128],
                                                       k_hl[:, b, z, c, i * SEQ:(i + 1) * SEQ], start=n == 0, stop=n == 2)
                ins.then_inc(S("scored"), 1)

            def values(st):
                p, b, _, b4 = st.item(5)
                pe.wait_ge(S("pt_high"), p + 1)
                pe.wait_ge(S("pt_low"), p + 1)
                wait_alone(pe, S, "ctx", 2 * p)
                for i in range(2):
                    rows = slice(i * SLOT, i * SLOT + SEQ)
                    for c in range(DC):
                        for j in range(4):
                            at = PAIR * j + (SEQ if j == 3 else 0)
                            for n, (a, z) in enumerate(((0, 0), (0, 1), (1, 0))):
                                ins = nc.tensor.matmul(psC[i][32 * j:32 * j + 32, c],
                                                       v_hl[rows, b4, z, c * 128 + 32 * j:c * 128 + 32 * j + 32],
                                                       pt_hl[rows, a, c, at:at + PAIR], start=n == 0, stop=n == 2)
                    ins.then_inc(S("mixed"), 1)

            def residual(st):
                p, b, _, b4 = st.item(5)
                wait(pe, S("h1"), p)
                if isinstance(p, int) and p == 0:
                    pe.wait_ge(S("bo_ready"), 3)
                for a in range(2):
                    nc.tensor.matmul(psO[:], ones[:], bo_hl[:, a], start=a == 0, stop=False)
                for m in range(DC):
                    for a in range(2):
                        ins = nc.tensor.matmul(psO[:, m * 128:(m + 1) * 128], h0_hl[:, b4, a, m], eye_ws[:], start=False, stop=False)
                ins.then_inc(S("residual"), 1)

            def output(st):
                p, b, _, b4 = st.item(5)
                pe.wait_ge(S("ctx_high"), p + 1)
                pe.wait_ge(S("ctx_low"), p + 1)
                ins = products(psO[:], (lambda a, c: ctx_hl[:, a, c], range(DC)),
                               (lambda a, c: w_qkvo[:, a, 3, c], range(DC)), first=False)
                ins.then_inc(S("projected"), 1)

            def step(st):
                if st.active(2):
                    project(st)
                if st.active(2):
                    project_values(st)
                if st.active(5):
                    values(st)
                if st.active(3):
                    scores(st)
                if st.active(5):
                    residual(st)
                if st.active(1):
                    embed(st)
                if st.active(4):
                    transpose_probs(st)
                if st.active(5):
                    output(st)

            run(pe, step)

        @block.scalar
        def _(act):
            act.wait_ge(S("setup_in"), 16 * N_SETUP)
            nc.scalar.activation(w_emb[:, 0], w_stage[:], ACT.Copy, scale=WS).then_inc(S("w_high"), 1)
            nc.scalar.activation(w_qkvo[:, 0], w_stage4[:], ACT.Copy, scale=WS).then_inc(S("w_high"), 1)

            def step(st):
                if st.active(2):
                    p, b, _, b4 = st.item(2)
                    act.wait_ge(S("qk"), p + 1)
                    wait(act, S("qbd_low"), p - 1)
                    wait(act, S("qbd_high"), p - 1)
                    wait(act, S("scored"), p - 1)
                    for z, dst in ((0, q_hl), (1, k_hl)):
                        for c in range(DC):
                            ins = nc.scalar.activation(dst[:, b, 0, c], psQK[:, z, c], ACT.Identity, bias=bias_ws[:, 1 + z, c:c + 1])
                    ins.then_inc(S("qk_high"), 1)
                if st.active(4):
                    p, b, _, _ = st.item(4)
                    act.wait_ge(S("prob"), p + 1)
                    wait(act, S("pt"), 2 * (p - 1))
                    for i in range(2):
                        ins = nc.scalar.activation(p_hl[:, b, 0, :, i, 0:SEQ], prob[:, b, 6 * i:6 * i + 6], ACT.Copy)
                    ins.then_inc(S("p_high"), 1)
                if st.active(2):
                    p, b, _, b4 = st.item(2)
                    act.wait_ge(S("v"), p + 1)
                    wait(act, S("mixed"), 2 * (p - 3))
                    nc.scalar.activation(v_hl[:, b4, 0], psV[:], ACT.Copy).then_inc(S("v_high"), 1)
                if st.active(5):
                    p, b, _, _ = st.item(5)
                    for i in range(2):
                        act.wait_ge(S("mixed"), 2 * p + 1 + i)
                        wait(act, S("ctx"), 2 * p)
                        for c in range(DC):
                            ins = nc.scalar.activation(odd[:, i, c], psC[i][:, c, SEQ:PAIR], ACT.Identity, scale=odd_mask[:, 0:1],
                                                       bias=bias_in[:, 3, c:c + 1])
                        ins.then_inc(S("odd"), 1)
                if st.active(0):
                    p, b, hp, b4 = st.item(0)
                    act.wait_ge(S(f"x_in{b4}"), 16 * st.h + 16)
                    wait(act, S("embedded"), p - 1)
                    nc.scalar.activation(x_hl[:, b, 0], x_in[:, b4], ACT.Copy).then_inc(S("x_high"), 1)
                if st.active(5):
                    p, b, _, _ = st.item(5)
                    act.wait_ge(S("ctx"), 2 * p + 2)
                    wait(act, S("projected"), p)
                    nc.scalar.activation(ctx_hl[:, 0, :, :, 0:SEQ], ctx_f[:, :, :, 0:SEQ], ACT.Copy).then_inc(S("ctx_high"), 1)
                if st.active(3):
                    p, b, _, _ = st.item(3)
                    act.wait_ge(S("shifted"), p + 1)
                    nc.scalar.activation(prob[:, b], prob[:, b], ACT.Exp, scale=1.0 / (WS * WS * HD ** 0.5)).then_inc(S("exp"), 1)
                if st.active(1):
                    p, b, _, b4 = st.item(1)
                    act.wait_ge(S("h0"), 2 * p + 2)
                    wait(act, S("residual"), p - 3)
                    nc.scalar.activation(h0_hl[:, b4, 0, :, :, 0:SEQ], h0[:, b4], ACT.Copy).then_inc(S("h0_high"), 1)
                if st.active(4):
                    p, b, _, _ = st.item(4)
                    act.wait_ge(S("pt"), 2 * p + 1)
                    wait(act, S("mixed"), 2 * p)
                    nc.scalar.activation(pt_hl[:, 0].rearrange("k c (t q) -> k (c t) q", t=3), psT[0][:, :, 0:TRIO], ACT.Copy).then_inc(S("pt_high"), 1)
                    act.wait_ge(S("pt"), 2 * p + 2)
                    nc.scalar.activation(pt_hl[:, 1].rearrange("k c (t q) -> k (c t) q", t=3), psT[1][:, :, 0:TRIO], ACT.Copy).then_inc(S("pt_low"), 1)

            run(act, step)

        @block.gpsimd
        def _(pool):
            nc.gpsimd.memset(h0_hl[:], 0.0).then_inc(S("zeroed"), 1)
            nc.gpsimd.memset(p_hl[:], 0.0).then_inc(S("zeroed"), 1)
            nc.gpsimd.memset(ctx_hl[:], 0.0).then_inc(S("zeroed"), 1)
            nc.gpsimd.memset(half_power[:], -0.5).then_inc(S("zeroed"), 1)
            nc.gpsimd.memset(q_wide[:], 0.0).then_inc(S("zeroed"), 1)
            pool.wait_ge(S("zeroed"), 5)

            def step(st):
                if st.active(4):
                    p, b, _, _ = st.item(4)
                    pool.wait_ge(S("p_high"), p + 1)
                    for i in range(2):
                        ins = nc.gpsimd.tensor_tensor(p_hl[:, b, 1, :, i, 0:SEQ], prob[:, b, 6 * i:6 * i + 6], p_hl[:, b, 0, :, i, 0:SEQ], ALU.subtract)
                    ins.then_inc(S("p_low"), 1)
                if st.active(2):
                    p, b, _, _ = st.item(2)
                    pool.wait_ge(S("qk_low"), 2 * p + 1)
                    wait_alone(pool, S, "scored", p - 1)
                    for h in range(HC // 2):
                        nc.gpsimd.tensor_scalar(qbd[:, b, 1, :, :, h], q_hl[:, b, 1].rearrange("p c (i q) -> p c i q", i=2),
                                                head_mask[:, h:h + 1], 1.0, ALU.mult, ALU.mult)
                if st.active(5):
                    p, b, _, _ = st.item(5)
                    pool.wait_ge(S("ctx_high"), p + 1)
                    nc.gpsimd.tensor_tensor(ctx_hl[:, 1, :, :, 0:SEQ], ctx_f[:, :, :, 0:SEQ], ctx_hl[:, 0, :, :, 0:SEQ],
                                            ALU.subtract).then_inc(S("ctx_low"), 1)
                if st.active(1):
                    p, b, _, b4 = st.item(1)
                    pool.wait_ge(S("h0_high"), p + 1)
                    nc.gpsimd.tensor_tensor(h0_hl[:, b4, 1, :, :, 0:SEQ], h0[:, b4], h0_hl[:, b4, 0, :, :, 0:SEQ],
                                            ALU.subtract).then_inc(S("h0_low"), 1)
                if st.active(2):
                    p, b, _, _ = st.item(2)
                    for h in range(HC // 2, HC):
                        ins = nc.gpsimd.tensor_scalar(qbd[:, b, 1, :, :, h], q_hl[:, b, 1].rearrange("p c (i q) -> p c i q", i=2),
                                                      head_mask[:, h:h + 1], 1.0, ALU.mult, ALU.mult)
                    ins.then_inc(S("qbd_low"), 1)
                if st.active(0):
                    p, b, _, b4 = st.item(0)
                    pool.wait_ge(S("x_high"), p + 1)
                    nc.gpsimd.tensor_tensor(x_hl[:, b, 1], x_in[:, b4], x_hl[:, b, 0], ALU.subtract).then_inc(S("x_low"), 1)
                if st.active(5):
                    p, b, _, _ = st.item(5)
                    pool.wait_ge(S("var_eps"), p + 1)
                    nc.gpsimd.tensor_tensor(rstd[:], var_eps[:], half_power[:], ALU.pow).then_inc(S("rstd"), 1)

            run(pool, step)

        @block.vector
        def _(dve):
            dve.wait_ge(S("setup_in"), 16 * N_SETUP)
            dve.wait_ge(S("w_high"), 1)
            nc.vector.scalar_tensor_tensor(w_emb[:, 1].rearrange("p c n -> p (c n)"), w_stage[:].rearrange("p c n -> p (c n)"), WS,
                                           w_emb[:, 0].rearrange("p c n -> p (c n)"), ALU.mult, ALU.subtract).then_inc(S("w_ready"), 1)
            nc.vector.tensor_scalar(eye_ws[:], eye[:], WS, None, ALU.mult).then_inc(S("w_ready"), 1)
            dve.wait_ge(S("w_high"), 2)
            nc.vector.scalar_tensor_tensor(w_qkvo[:, 1].rearrange("p z c n -> p (z c n)"), w_stage4[:].rearrange("p z c n -> p (z c n)"), WS,
                                           w_qkvo[:, 0].rearrange("p z c n -> p (z c n)"), ALU.mult, ALU.subtract).then_inc(S("w_ready"), 1)
            nc.vector.tensor_scalar(bias_ws[:], bias_in[:], WS, None, ALU.mult).then_inc(S("w_ready"), 1)
            nc.vector.memset(ones[:], 1.0).then_inc(S("bo_ready"), 1)
            nc.vector.tensor_scalar(bo_hl[:, 0], bo[:], WS, None, ALU.mult).then_inc(S("bo_ready"), 1)
            dve.wait_ge(S("bo_ready"), 2)
            nc.vector.scalar_tensor_tensor(bo_hl[:, 1], bo[:], WS, bo_hl[:, 0], ALU.mult, ALU.subtract).then_inc(S("bo_ready"), 1)
            nc.vector.tensor_tensor(odd_mask[:], head_mask[:, 1:2], head_mask[:, 3:4], ALU.add).then_inc(S("masks"), 1)
            for n, h in enumerate((5, 7)):
                dve.wait_ge(S("masks"), n + 1)
                nc.vector.tensor_tensor(odd_mask[:], odd_mask[:], head_mask[:, h:h + 1], ALU.add).then_inc(S("masks"), 1)
            dve.wait_ge(S("masks"), 3)
            nc.vector.tensor_scalar(even_mask[:], odd_mask[:], -1.0 / WS, 1.0 / WS, ALU.mult, ALU.add).then_inc(S("masks"), 1)
            dve.wait_ge(S("masks"), 4)
            nc.vector.tensor_scalar(odd_mask[:], odd_mask[:], 1.0 / WS, None, ALU.mult).then_inc(S("masks"), 1)
            nc.vector.tensor_tensor(cls_t[:], cls_t[:], pos_t[:, :, 0:1], ALU.add).then_inc(S("masks"), 1)
            for c in range(DC):
                nc.vector.tensor_scalar(pos_t[:, c, 1:SEQ], pos_t[:, c, 1:SEQ], bias_in[:, 0, c:c + 1], None, ALU.add).then_inc(S("masks"), 1)
            dve.wait_ge(S("masks"), 6 + DC)
            for b4 in range(4):
                for i in range(2):
                    nc.vector.tensor_copy(h0[:, b4, :, i, 0:1], cls_t[:]).then_inc(S("masks"), 1)
            dve.wait_ge(S("masks"), 14 + DC)

            def step(st):
                scored = psS[0:TRIO].rearrange("r i t k -> r (i t) k")
                if st.active(2):
                    p, b, _, b4 = st.item(2)
                    dve.wait_ge(S("qk_high"), p + 1)
                    for z, dst in ((0, q_hl), (1, k_hl)):
                        for c in range(DC):
                            ins = nc.vector.scalar_tensor_tensor(dst[:, b, 1, c], psQK[:, z, c], bias_ws[:, 1 + z, c:c + 1], dst[:, b, 0, c],
                                                                 ALU.add, ALU.subtract)
                        ins.then_inc(S("qk_low"), 1)
                if st.active(2):
                    p, b, _, b4 = st.item(2)
                    dve.wait_ge(S("v_high"), p + 1)
                    nc.vector.tensor_tensor(v_hl[:, b4, 1], psV[:], v_hl[:, b4, 0], ALU.subtract).then_inc(S("v_low"), 1)
                if st.active(6):
                    p, b, hp, b4 = st.item(6)
                    dve.wait_ge(S("rstd"), p + 1)
                    wait(dve, S(f"h1_out{b}"), 32 * hp)
                    nc.vector.tensor_scalar(h1[:, b], psO[:], moments[:, 0:1], rstd[:, 0:1], ALU.subtract, ALU.mult).then_inc(S("h1"), 1)
                if st.active(3):
                    p, b, _, _ = st.item(3)
                    dve.wait_ge(S("scored"), p + 1)
                    nc.vector.tensor_reduce(row_max[:], scored, AX.X, ALU.max).then_inc(S("row_max"), 1)
                if st.active(5):
                    p, b, _, b4 = st.item(5)
                    for i in range(2):
                        dve.wait_ge(S("odd"), 2 * p + 1 + i)
                        if i == 0:
                            wait(dve, S("ctx_low"), p)
                        nc.vector.scalar_tensor_tensor(ctx_f[:, :, i, 0:SEQ], psC[i][:, :, 0:SEQ], even_mask[:, 0:1], odd[:, i],
                                                       ALU.mult, ALU.add).then_inc(S("ctx"), 1)
                if st.active(3):
                    p, b, _, _ = st.item(3)
                    dve.wait_ge(S("row_max"), p + 1)
                    wait(dve, S("p_low"), p - 1)
                    nc.vector.tensor_tensor(prob[:, b], scored, row_max[:].unsqueeze(2).broadcast_to([TRIO, 12, SEQ]), ALU.subtract).then_inc(S("shifted"), 1)
                if st.active(1):
                    p, b, _, b4 = st.item(1)
                    dve.wait_ge(S("embedded"), p + 1)
                    wait(dve, S("h0_low"), p - 3)
                    for c in range(DC):
                        nc.vector.scalar_tensor_tensor(h0[:, b4, c, :, 1:SEQ], psE[:, c].rearrange("p (i n) -> p i n", i=2), 1.0 / WS,
                                                       pos_t[:, c:c + 1, 1:SEQ].broadcast_to([128, 2, PATCHES]), ALU.mult, ALU.add).then_inc(S("h0"), 1)
                if st.active(2):
                    p, b, _, b4 = st.item(2)
                    wait(dve, S("scored"), p - 1)
                    for h in range(HC):
                        ins = nc.vector.tensor_scalar(qbd[:, b, 0, :, :, h], q_hl[:, b, 0].rearrange("p c (i q) -> p c i q", i=2),
                                                      head_mask[:, h:h + 1], None, ALU.mult)
                    ins.then_inc(S("qbd_high"), 1)
                if st.active(3):
                    p, b, _, _ = st.item(3)
                    dve.wait_ge(S("exp"), p + 1)
                    nc.vector.tensor_reduce(row_sum[:], prob[:, b], AX.X, ALU.add).then_inc(S("row_sum"), 1)
                if st.active(3):
                    p, b, _, _ = st.item(3)
                    dve.wait_ge(S("row_sum"), p + 1)
                    nc.vector.reciprocal(row_inv[:], row_sum[:]).then_inc(S("row_inv"), 1)
                if st.active(5):
                    p, b, hp, b4 = st.item(5)
                    dve.wait_ge(S("projected"), p + 1)
                    nc.vector.bn_stats(stats[:], psO[:]).then_inc(S("stats"), 1)
                if st.active(3):
                    p, b, _, _ = st.item(3)
                    dve.wait_ge(S("row_inv"), p + 1)
                    nc.vector.tensor_tensor(prob[:, b], prob[:, b], row_inv[:].unsqueeze(2).broadcast_to([TRIO, 12, SEQ]), ALU.mult).then_inc(S("prob"), 1)
                if st.active(5):
                    p, b, hp, b4 = st.item(5)
                    wait_alone(dve, S, "stats", p + 1)
                    nc.vector.bn_aggr(moments[:], stats[:]).then_inc(S("moments"), 1)
                if st.active(5):
                    p, b, hp, b4 = st.item(5)
                    dve.wait_ge(S("moments"), p + 1)
                    nc.vector.tensor_scalar(var_eps[:], moments[:, 1:2], WS * WS * EPS, None, ALU.add).then_inc(S("var_eps"), 1)

            run(dve, step)
def routing_inputs(nc, ctx, io):
    TT = TOK_TILES
    return Resident(nc, ctx, "routing", [
        ("wr0", [128, DC, TE], F32, 0, io["wr0"]),
        ("wr1", [128, DC, TE], F32, 0, io["wr1"]),
        ("bias0", [128, TE], F32, 0, io["router_bias0"].broadcast_to([128, TE])),
        ("bias1", [128, TE], F32, 0, io["router_bias1"].broadcast_to([128, TE])),
        ("eye", [128, 128], F32, 0, io["eye_f"]),
        ("below", [128, 128], F16, 0, io["below"]),
        ("lane", [128, 128], F16, 0, io["lane"]),
        ("place", [128, TE], F32, 0, io["place"]),
        ("valid", [128, TT], F32, 0, io["valid"]),
        ("tile_number", [128, 1, TT * TE], F16, 0, io["tile_number"]),
        ("lane_number", [128, 1], F32, 0, io["lane_number"]),
        ("dummy_row", [128, 1], F32, 0, io["dummy_row"]),
        ("steps", [1, TT - 1], F32, 0, io["steps"]),
    ])


def build_routing(nc, io, res, x_rows, acc_rows, plan, layer):
    TT = TOK_TILES
    first = plan.first
    with ExitStack() as ctx:
        def sb(name, shape, dt=F32):
            return ctx.enter_context(nc.sbuf_tensor(f"r{layer}_" + name, shape, dt))

        S = Sems(nc, f"r{layer}")
        ctx.callback(S.clear)
        wr, bias = res[f"wr{layer}"], res[f"bias{layer}"]
        eye, below, lane, place, valid = (res[n] for n in ("eye", "below", "lane", "place", "valid"))
        tile_number, lane_number, dummy_row, steps = (res[n] for n in ("tile_number", "lane_number", "dummy_row", "steps"))
        wr_hl = sb("wr_hl", [128, 2, DC, TE], F16)
        ones = sb("ones", [128, 128], F16)

        XB = 4
        x = sb("x", [128, TT, D])
        xt_hl = sb("xt_hl", [128, XB, 2, DC, 128], F16)
        z = sb("z", [128, TT, TE])
        score = sb("score", [128, TT, TE])
        work = sb("work", [128, TT, TE])
        pick = sb("pick", [128, TT, TE])
        top = sb("top", [128, TT])
        top2 = sb("top2", [128, TT])
        total = sb("total", [128, TT])
        mask = sb("mask", [128, 2 * TT + 1, TE], F16)
        rank = sb("rank", [128, TT * TE])
        rank_i = sb("rank_i", [128, TT * TE], I32)
        lane_i = sb("lane_i", [128, TT * TE], I32)
        tile_i = sb("tile_i", [128, TT * TE], I32)
        lane_f = sb("lane_f", [128, TT * TE])
        lane_neg = sb("lane_neg", [128, TT * TE])
        tile_f = sb("tile_f", [128, TT * TE], F16)
        w_hl = sb("w_hl", [128, 2, TT * TE], F16)
        in_tile = sb("in_tile", [128, TT, TT * TE], F16)
        spread = sb("spread", [128, 4, TT, TT * TE], F16)
        makers = [m for m, _ in zip("dadpddadpddaddpdadpdda" * (TT * TE), range(TT * TE))]
        ring = {"d": 6, "p": 16, "a": 6}
        in_lane = {m: sb("in_lane_" + m, [128, ring[m], 128], F16) for m in "dpa"}
        distance = sb("distance", [128, 2, 128], F16)
        counts = sb("counts", [1, TE])
        over = sb("over", [1, TE, TT - 1])
        tiles = sb("tiles", [1, TE])
        starts = sb("starts", [1, first + TE + 1])
        slot_id = sb("slot_id", [128, TE, TT])
        empty = sb("empty", [128, TE, TT])

        psX = [ctx.enter_context(nc.psum_tensor(f"r{layer}_psX{b}", [128, DC, 128], F32)) for b in range(XB)]
        psL = ctx.enter_context(nc.psum_tensor(f"r{layer}_psL", [128, TT, TE], F32))
        psR = ctx.enter_context(nc.psum_tensor(f"r{layer}_psR", [128, TT + 1, TE], F32))
        psT = [ctx.enter_context(nc.psum_tensor(f"r{layer}_psT{b}", [128, TE // 2, 4, TT], F32)) for b in range(2)]
        GROUP = 5

        def lanes_of(m, eng, make):
            mine = [n for n in range(TT * TE) if makers[n] == m]
            for i, n in enumerate(mine):
                if i >= ring[m]:
                    eng.wait_ge(S("placed"), mine[i - ring[m]] + 1)
                make((n % TT) * TE + n // TT, in_lane[m][:, i % ring[m]]).then_inc(S("in_lane_" + m), 1)

        block = ctx.enter_context(nc.Block())

        @block.sync
        def _(sp):
            for g in range(0, TT, GROUP):
                last = min(g + GROUP, TT)
                sp.dma_start(x[:, g:last], x_rows[g * 128:last * 128, :].rearrange("(t p) d -> p t d", p=128)).then_inc(S(f"x_in{g // GROUP}"), 16)
            sp.dma_start(plan.w_stage[:], io[f"experts{layer}"][0]).then_inc(S("w_in"), 16)
            sp.wait_ge(S("w_in"), 16)
            sp.dma_start(acc_rows, x_rows).then_inc(S("acc_out"), 16)
            sp.wait_ge(S("acc_out"), 16)
            if first:
                sp.dma_start(plan.index[:, 0, :], io["all_index"]).then_inc(S("shared_in"), 16)
                sp.dma_start(plan.weight[:, 0, :], io["valid"]).then_inc(S("shared_in"), 16)
                sp.wait_ge(S("shared_in"), 32)

        @block.tensor
        def _(pe):
            pe.wait_ge(S("wr_ready"), 2)

            def logits(t):
                pe.wait_ge(S("xt_low"), t + 1)
                for n, (a, b, c) in enumerate((a, b, c) for c in range(DC) for a, b in ((0, 0), (0, 1), (1, 0))):
                    ins = nc.tensor.matmul(psL[:, t], xt_hl[:, t % XB, a, c], wr_hl[:, b, c], start=n == 0, stop=n == 3 * DC - 1)
                ins.then_inc(S("logits"), 1)

            for t in range(TT):
                pe.wait_ge(S(f"x_in{t // GROUP}"), 16)
                if t >= XB:
                    pe.wait_ge(S("xt_low"), t + 1 - XB)
                for c in range(DC):
                    ins = nc.tensor.transpose(psX[t % XB][:, c], x[:, t, c * 128:(c + 1) * 128], eye[:])
                ins.then_inc(S("turned"), 1)
                if t >= 2:
                    logits(t - 2)
            logits(TT - 2)
            logits(TT - 1)
            pe.wait_ge(S("mask"), 1)
            pe.wait_ge(S("ones"), 1)
            nc.tensor.matmul(psR[:], below[:], mask[:, TT:], start=True, stop=False)
            for d in range(1, TT + 1):
                nc.tensor.matmul(psR[:], ones[:], mask[:, TT - d:2 * TT + 1 - d], start=False, stop=d == TT).then_inc(S("ranked"), 1)
            pe.wait_ge(S("spread"), 1)
            pe.wait_ge(S("spread_lane"), 1)
            for e in range(TE):
                for t in range(TT):
                    n = e * TT + t
                    i = makers[:n].count(makers[n])
                    pe.wait_ge(S("in_lane_" + makers[n]), i + 1)
                    nc.tensor.matmul(psT[e // 4][:, e % 4], in_lane[makers[n]][:, i % ring[makers[n]]], spread[:, :, :, t * TE + e],
                                     start=t == 0, stop=t == TT - 1).then_inc(S("placed"), 1)

        @block.scalar
        def _(act):
            nc.scalar.activation(wr_hl[:, 0], wr[:], ACT.Copy, scale=WS).then_inc(S("wr_high"), 1)
            for t in range(TT):
                act.wait_ge(S("turned"), t + 1)
                if t >= XB:
                    act.wait_ge(S("logits"), t + 1 - XB)
                nc.scalar.activation(xt_hl[:, t % XB, 0], psX[t % XB][:], ACT.Copy).then_inc(S("xt_high"), 1)
            if layer == 0:
                act.wait_ge(S("z"), 1)
                nc.scalar.activation(score[:], z[:], ACT.Exp, scale=-1.0).then_inc(S("exp"), 1)
            else:
                act.wait_ge(S("z_shifted"), 1)
                nc.scalar.activation(score[:], work[:], ACT.Exp).then_inc(S("exp"), 1)
            act.wait_ge(S("in_tile"), TT)
            nc.scalar.activation(spread[:, 1], in_tile[:], ACT.Copy, scale=lane_number[:, 0:1]).then_inc(S("spread_lane"), 1)

            mine = [n for n in range(TT * TE) if makers[n] == "a"]
            for i in range(len(mine) + 1):
                if i < len(mine):
                    n = mine[i]
                    at = (n % TT) * TE + n // TT
                    if i >= 2:
                        act.wait_ge(S("in_lane_a"), i - 1)
                    nc.scalar.activation(distance[:, i % 2], lane[:], ACT.Abs, bias=lane_neg[:, at:at + 1]).then_inc(S("distance"), 1)
                if i >= 1:
                    act.wait_ge(S("distance"), i)
                    if i > ring["a"]:
                        act.wait_ge(S("placed"), mine[i - 1 - ring["a"]] + 1)
                    nc.scalar.activation(in_lane["a"][:, (i - 1) % ring["a"]], distance[:, (i - 1) % 2], ACT.Relu, scale=-1.0,
                                         bias=1.0).then_inc(S("in_lane_a"), 1)

        @block.gpsimd
        def _(pool):
            nc.gpsimd.memset(ones[:], 1.0).then_inc(S("ones"), 1)
            pool.wait_ge(S("lane_ready"), 1)
            lanes_of("p", pool, lambda at, out: nc.gpsimd.tensor_scalar(out, lane[:], lane_f[:, at:at + 1], 1.0, ALU.is_equal, ALU.mult))

        @block.vector
        def _(dve):
            made = [0]

            def then(ins):
                made[0] += 1
                ins.then_inc(S("link"), 1)
                dve.wait_ge(S("link"), made[0])

            over_tiles = lambda v: v.unsqueeze(1).broadcast_to([128, TT, TE])
            over_experts = lambda v: v.unsqueeze(2).broadcast_to([128, TT, TE])
            dve.wait_ge(S("wr_high"), 1)
            dve.wait_ge(S("ones"), 1)
            nc.vector.scalar_tensor_tensor(wr_hl[:, 1], wr[:], WS, wr_hl[:, 0], ALU.mult, ALU.subtract).then_inc(S("wr_ready"), 1)
            nc.vector.memset(mask[:], 0.0).then_inc(S("wr_ready"), 1)
            dve.wait_ge(S("wr_ready"), 2)
            for t in range(TT):
                dve.wait_ge(S("xt_high"), t + 1)
                if t >= XB:
                    dve.wait_ge(S("logits"), t + 1 - XB)
                nc.vector.tensor_tensor(xt_hl[:, t % XB, 1], psX[t % XB][:], xt_hl[:, t % XB, 0], ALU.subtract).then_inc(S("xt_low"), 1)
            dve.wait_ge(S("logits"), TT)
            nc.vector.scalar_tensor_tensor(z[:], psL[:], 1.0 / WS, over_tiles(bias[:]), ALU.mult, ALU.add).then_inc(S("z"), 1)
            dve.wait_ge(S("z"), 1)
            if layer == 0:
                dve.wait_ge(S("exp"), 1)
                then(nc.vector.tensor_scalar(score[:], score[:], 1.0, None, ALU.add))
                then(nc.vector.reciprocal(z[:], score[:]))

            def take_first(src, top, out):
                then(nc.vector.tensor_reduce(top[:], src[:], AX.X, ALU.max))
                then(nc.vector.tensor_tensor(out[:], src[:], over_experts(top[:]), ALU.is_equal))
                then(nc.vector.tensor_tensor(out[:], out[:], over_tiles(place[:]), ALU.mult))
                then(nc.vector.tensor_reduce(total[:], out[:], AX.X, ALU.max))
                then(nc.vector.tensor_tensor(out[:], out[:], over_experts(total[:]), ALU.is_equal))

            take_first(z, top, pick)
            then(nc.vector.scalar_tensor_tensor(work[:], pick[:], -3.0e38, z[:], ALU.mult, ALU.add))
            if layer == 0:
                take_first(work, top2, score)
                then(nc.vector.tensor_tensor(pick[:], pick[:], score[:], ALU.add))
            else:
                then(nc.vector.tensor_reduce(top2[:], work[:], AX.X, ALU.max))
                then(nc.vector.tensor_tensor(pick[:], z[:], over_experts(top2[:]), ALU.is_ge))
            then(nc.vector.tensor_tensor(pick[:], pick[:], over_experts(valid[:]), ALU.mult))
            nc.vector.tensor_copy(mask[:, TT:2 * TT], pick[:]).then_inc(S("mask"), 1)
            dve.wait_ge(S("mask"), 1)
            if layer == 0:
                then(nc.vector.tensor_tensor(work[:], z[:], pick[:], ALU.mult))
            else:
                nc.vector.tensor_tensor(work[:], z[:], over_experts(top[:]), ALU.subtract).then_inc(S("z_shifted"), 1)
                dve.wait_ge(S("exp"), 1)
                then(nc.vector.tensor_tensor(work[:], score[:], pick[:], ALU.mult))
                then(nc.vector.tensor_reduce(total[:], work[:], AX.X, ALU.add))
                then(nc.vector.tensor_scalar(total[:], total[:], 1.0e-30, None, ALU.max))
                then(nc.vector.reciprocal(top2[:], total[:]))
                then(nc.vector.tensor_tensor(work[:], work[:], over_experts(top2[:]), ALU.mult))
            flat = work[:].rearrange("p t e -> p (t e)")
            then(nc.vector.tensor_copy(w_hl[:, 0], flat))
            then(nc.vector.tensor_tensor(w_hl[:, 1], flat, w_hl[:, 0], ALU.subtract))
            dve.wait_ge(S("ranked"), TT)
            then(nc.vector.scalar_tensor_tensor(rank[:].rearrange("p (t e) -> p t e", e=TE), psR[:, 0:TT], 1.0, pick[:], ALU.add, ALU.mult))
            then(nc.vector.tensor_scalar(rank_i[:], rank[:], -1.0, None, ALU.add))
            then(nc.vector.tensor_scalar(lane_i[:], rank_i[:], 127, None, ALU.bitwise_and))
            then(nc.vector.tensor_scalar(tile_i[:], rank_i[:], 7, None, ALU.arith_shift_right))
            then(nc.vector.tensor_copy(lane_f[:], lane_i[:]))
            nc.vector.tensor_scalar(lane_neg[:], lane_f[:], -1.0, None, ALU.mult).then_inc(S("lane_ready"), 1)
            then(nc.vector.tensor_copy(tile_f[:], tile_i[:]))
            for c in range(TT):
                nc.vector.tensor_scalar(in_tile[:, c], tile_f[:], float(c), None, ALU.is_equal).then_inc(S("in_tile"), 1)
            dve.wait_ge(S("in_tile"), TT)
            for v, factor in ((0, tile_number[:]), (2, w_hl[:, 0:1]), (3, w_hl[:, 1:2])):
                ins = nc.vector.tensor_tensor(spread[:, v], in_tile[:], factor.broadcast_to([128, TT, TT * TE]), ALU.mult)
            ins.then_inc(S("spread"), 1)
            lanes_of("d", dve, lambda at, out: nc.vector.tensor_scalar(out, lane[:], lane_f[:, at:at + 1], None, ALU.is_equal))
            then(nc.vector.tensor_copy(counts[:], psR[0:1, TT]))
            then(nc.vector.tensor_tensor(over[:], counts[:].unsqueeze(2).broadcast_to([1, TE, TT - 1]),
                                         steps[:].unsqueeze(1).broadcast_to([1, TE, TT - 1]), ALU.is_gt))
            then(nc.vector.tensor_reduce(tiles[:], over[:], AX.X, ALU.add))
            then(nc.vector.tensor_scalar(tiles[:], tiles[:], 1.0, float(MIN_TILES), ALU.add, ALU.max))
            then(nc.vector.memset(starts[:], 0.0))
            if first:
                then(nc.vector.memset(starts[:, 1:2], float(TT)))
            for e in range(TE):
                then(nc.vector.tensor_tensor(starts[:, first + e + 1:first + e + 2], starts[:, first + e:first + e + 1], tiles[:, e:e + 1], ALU.add))
            then(nc.vector.tensor_scalar(plan.bounds[:], starts[:], -float(MIN_TILES), None, ALU.add))
            dve.wait_ge(S("placed"), TE * TT)
            for g in range(2):
                half = slice(4 * g, 4 * g + 4)
                then(nc.vector.tensor_copy(slot_id[:, half], psT[g][:, :, 1]))
                then(nc.vector.scalar_tensor_tensor(slot_id[:, half], psT[g][:, :, 0], 128.0, slot_id[:, half], ALU.mult, ALU.add))
                out = plan.weight[:, first + 4 * g:first + 4 * g + 4]
                then(nc.vector.tensor_copy(out, psT[g][:, :, 2]))
                then(nc.vector.tensor_tensor(out, psT[g][:, :, 3], out, ALU.add))
            then(nc.vector.tensor_scalar(empty[:], slot_id[:], 0.0, None, ALU.is_equal))
            then(nc.vector.scalar_tensor_tensor(slot_id[:], empty[:], dummy_row[:, 0:1], slot_id[:], ALU.mult, ALU.add))
            then(nc.vector.tensor_scalar(plan.index[:, first:], slot_id[:], -1.0, None, ALU.add))


MIN_TILES = 3


class Plan:

    def __init__(self, nc, ctx, layer, first):
        self.first = first
        self.experts = first + TE
        self.index = ctx.enter_context(nc.sbuf_tensor(f"plan{layer}_index", [128, self.experts, TOK_TILES], I32))
        self.weight = ctx.enter_context(nc.sbuf_tensor(f"plan{layer}_weight", [128, self.experts, TOK_TILES], F32))
        self.bounds = ctx.enter_context(nc.sbuf_tensor(f"plan{layer}_bounds", [1, self.experts + 1], I32))
        width = 3 * 2 * 512 if layer == 0 else 2 * 1024 + 8 * D
        self.w_stage = ctx.enter_context(nc.sbuf_tensor(f"plan{layer}_w_stage", [128, width], F32))


def build_experts(nc, io, res, x_rows, acc_rows, plan, layer, later=None):
    gated = layer == 0
    NE = plan.experts
    HID = 512 if gated else 1024
    HC = HID // 128
    UP = DC * HID
    W = UP * (2 if gated else 1) + HC * D
    PARTS = HC // 2
    NB = 2 if gated else 4
    LAG = 3 if gated else 2
    with ExitStack() as ctx:
        def sb(name, shape, dt=F32):
            return ctx.enter_context(nc.sbuf_tensor(f"e{layer}_" + name, shape, dt))

        S = Sems(nc, f"e{layer}")
        ctx.callback(S.clear)
        eye = res["eye"]
        w_stage = plan.w_stage
        w_hl = sb("w_hl", [128, 2, 2, W], F16)
        x = sb("x", [128, D])
        xt_hl = sb("xt_hl", [128, 2, DC, 128], F16)
        gate = sb("gate", [128, HC, 128])
        hidden = sb("hidden", [128, HC, 128])
        hid_hl = sb("hid_hl", [128, 2, HC, 128], F16)
        y = sb("y", [128, D])
        y_sum = sb("y_sum", [128, D])
        slot_w = sb("slot_w", [128, 1])
        idx = sb("idx", [128, 1], I32)
        slot_row = sb("slot_row", [128, 1], I32)
        y_rows = sb("y_rows", [128, 1], I32)
        if not gated:
            b1 = sb("b1", [128, 2, HC])
            b2 = sb("b2", [128, 2, D])
        psX = ctx.enter_context(nc.psum_tensor(f"e{layer}_psX", [128, DC, 128], F32))
        psH = [ctx.enter_context(nc.psum_tensor(f"e{layer}_psH{n}", [128, 2 if gated else 1, 2, 128], F32)) for n in range(NB)]
        psY = ctx.enter_context(nc.psum_tensor(f"e{layer}_psY", [128, D], F32))

        def up_w(b, a, z, c, m):
            at = z * UP + c * HID + m * 128
            return w_hl[:, b, a, at:at + 128]

        def down_w(b, a, m):
            at = W - HC * D + m * D
            return w_hl[:, b, a, at:at + D]

        def tiles_before(eng, n):
            return eng.value_load(plan.bounds[0:1, bass.ds(n, 1)], min_val=0, max_val=NE * TOK_TILES - MIN_TILES) + MIN_TILES

        def over_experts(eng, tile, finish):
            def expert(n, b):
                lo = 0 if isinstance(n, int) and n == 0 else tiles_before(eng, n)
                hi = tiles_before(eng, n + 1)
                tile(lo, n, lo, b, 1 - b, 0)
                tile(lo + 1, n, lo, b, b, 1)
                with eng.Fori(lo + 2, hi) as T:
                    tile(T, n, lo, b, b, 2)
                return hi

            last = expert(0, 0)
            with eng.Fori(1, 7, 2) as n:
                expert(n, 1)
                expert(n + 1, 0)
            for n in range(7, NE):
                last = expert(n, n % 2)
            if finish:
                finish(last, (NE - 1) % 2)

        def column(T, n, lo):
            if isinstance(T, int):
                return T
            return nc.s_assert_within(n * TOK_TILES + T - lo, 0, NE * TOK_TILES - 1,
                                      skip_runtime_bounds_check_because="an expert has at most TOK_TILES tiles")

        SPLIT = 2 * PARTS
        piece = lambda k: slice(k * W // SPLIT, (k + 1) * W // SPLIT)
        block = ctx.enter_context(nc.Block())

        @block.sync
        def _(sp):
            if not gated:
                for n in range(2):
                    sp.dma_start(b1[:, n], io["b1"][n]).then_inc(S(f"b_in{n}"), 16)
                    sp.dma_start(b2[:, n], io["b2"][n].broadcast_to([128, D])).then_inc(S(f"b_in{n}"), 16)

            def load(n, b):
                for k in range(SPLIT):
                    sp.wait_ge(S("w_low"), (n - 1) * SPLIT + k + 1)
                    sp.wait_ge(S("w_high"), (n - 1) * SPLIT + k + 1)
                    sp.dma_start(w_stage[:, piece(k)], io[f"experts{layer}"][bass.ds(n, 1), :, piece(k)].rearrange("a p w -> (a p) w")).then_inc(S(f"w_in{k}"), 16)
                if not gated and not (isinstance(n, int) and n < 2):
                    lo = tiles_before(sp, n - 1)
                    sp.wait_ge(S("y"), lo + LAG - 1)
                    sp.dma_start(b1[:, b], io["b1"][bass.ds(n, 1)].rearrange("a p c -> (a p) c")).then_inc(S(f"b_in{b}"), 16)
                    sp.dma_start(b2[:, b], io["b2"][bass.ds(n, 1)].rearrange("a o d -> (a o) d").broadcast_to([128, D])).then_inc(S(f"b_in{b}"), 16)

            load(1, 1)
            with sp.Fori(2, NE - 1, 2) as n:
                load(n, 0)
                load(n + 1, 1)
            if NE % 2:
                load(NE - 1, 0)
            if later:
                sp.wait_ge(S("later_in"), later.load(sp, S("later_in")))

        @block.tensor
        def _(pe):
            def second(T, b, parts):
                if 0 in parts:
                    wait(pe, S("y_sum"), T)
                for k in parts:
                    pe.wait_ge(S("hid_low"), T * PARTS + k + 1)
                    for m in (2 * k, 2 * k + 1):
                        for a, z in ((0, 0), (0, 1), (1, 0)):
                            ins = nc.tensor.matmul(psY[:], hid_hl[:, a, m], down_w(b, z, m),
                                                   start=m == 0 and (a, z) == (0, 0), stop=m == HC - 1 and a == 1)
                if PARTS - 1 in parts:
                    ins.then_inc(S("second"), 1)

            def turn(T):
                pe.wait_ge(S("gathered"), T * 16 + 16)
                wait(pe, S("xt_low"), T)
                for c in range(DC):
                    ins = nc.tensor.transpose(psX[:, c], x[:, c * 128:(c + 1) * 128], eye[:])
                ins.then_inc(S("turned"), 1)

            def tile(T, n, lo, b, b_prev, phase):
                start = isinstance(T, int) and T == 0
                if start:
                    turn(0)
                if phase == 0:
                    pe.wait_ge(S("w_low"), n * SPLIT + SPLIT)
                pe.wait_ge(S("xt_low"), T + 1)
                for k in range(PARTS):
                    if k == 1 and not start and not gated:
                        second(T - 1, b_prev, (PARTS - 1,))
                    if not (start and k < NB):
                        pe.wait_ge(S("hid"), T * PARTS + k + 1 - NB)
                    for mm in range(2):
                        for z in range(2 if gated else 1):
                            for i, (a, r, c) in enumerate((a, r, c) for c in range(DC) for a, r in ((0, 0), (0, 1), (1, 0))):
                                ins = nc.tensor.matmul(psH[k % NB][:, z, mm], up_w(b, a, z, c, 2 * k + mm), xt_hl[:, r, c],
                                                       start=i == 0, stop=i == 3 * DC - 1)
                    ins.then_inc(S("first"), 1)
                turn(T + 1)
                if not gated:
                    second(T, b, range(PARTS - 1))
                elif not start:
                    second(T - 1, b_prev, range(PARTS))

            over_experts(pe, tile, lambda last, b: second(last - 1, b, range(PARTS) if gated else (PARTS - 1,)))

        @block.scalar
        def _(act):
            for k in range(SPLIT):
                nc.scalar.activation(w_hl[:, 0, 0, piece(k)], w_stage[:, piece(k)], ACT.Copy, scale=WS).then_inc(S("w_high"), 1)

            def split(n, lo, b, k):
                act.wait_ge(S(f"w_in{k}"), n * 16 + 16)
                if k == 0:
                    wait(act, S("second"), lo)
                nc.scalar.activation(w_hl[:, 1 - b, 0, piece(k)], w_stage[:, piece(k)], ACT.Copy, scale=WS).then_inc(S("w_high"), 1)

            def turned(T):
                act.wait_ge(S("turned"), T + 1)
                wait(act, S("first"), T * PARTS)
                nc.scalar.activation(xt_hl[:, 0], psX[:], ACT.Copy).then_inc(S("xt_high"), 1)

            def tile(T, n, lo, b, b_prev, phase):
                start = isinstance(T, int) and T == 0
                more = phase < 2 and not (isinstance(n, int) and n == NE - 1)
                if start:
                    turned(0)
                if phase == 0 and not gated:
                    if start:
                        act.wait_ge(S("b_in0"), 32)
                    else:
                        act.wait_ge(S(f"b_in{b}"), (n // 2 + 1) * 32 if isinstance(n, int) else (n * 16 + (32 if b == 0 else 16)))
                def high(k):
                    act.wait_ge(S("hid"), T * PARTS + k + 1)
                    wait(act, S("second"), T)
                    nc.scalar.activation(hid_hl[:, 0, 2 * k:2 * k + 2], hidden[:, 2 * k:2 * k + 2], ACT.Copy).then_inc(S("hid_high"), 1)

                for k in range(PARTS):
                    if k == PARTS - 1:
                        turned(T + 1)
                    act.wait_ge(S("first"), T * PARTS + k + 1)
                    if gated:
                        wait(act, S("hid"), (T - 1) * PARTS + k + 1 if not start else 0)
                        nc.scalar.activation(gate[:, 2 * k:2 * k + 2], psH[k % NB][:, 0], ACT.Silu, scale=1.0 / WS).then_inc(S("gate"), 1)
                    else:
                        wait(act, S("hid_low"), (T - 1) * PARTS + k + 1 if not start else 0)
                        for mm in range(2):
                            m = 2 * k + mm
                            ins = nc.scalar.activation(hidden[:, m], psH[k % NB][:, 0, mm], ACT.Gelu, scale=1.0 / WS, bias=b1[:, b, m:m + 1])
                        ins.then_inc(S("hid"), 1)
                        if more:
                            high(k)
                if gated:
                    for k in range(PARTS):
                        high(k)
                if more:
                    for k in range(PARTS):
                        split(n, lo, b, phase * PARTS + k)

            over_experts(act, tile, None)

        @block.gpsimd
        def _(pool):
            nc.gpsimd.iota(y_rows[:], [[0, 1]], base=TOKENS, channel_multiplier=1).then_inc(S("y_set"), 1)
            nc.gpsimd.memset(y[:], 0.0).then_inc(S("y_set"), 1)
            pool.wait_ge(S("y_set"), 2)
            pool.sem_inc(S("y"), LAG - 1)

            def scatter(T):
                wait_alone(pool, S, "scattered", T * 16)
                wait_alone(pool, S, "y", T)
                nc.gpsimd.indirect_dma_start(out=acc_rows, out_offset=bass.IndirectOffsetOnAxis(ap=y_rows[:, 0:1], axis=0), in_=y[:],
                                             in_offset=None, compute_op=ALU.add).then_inc(S("scattered"), 16)

            def tile(T, n, lo, b, b_prev, phase):
                col = column(T, n, lo)
                wait(pool, S("turned"), T)
                nc.gpsimd.tensor_copy(idx[:], plan.index[:].rearrange("p n c -> p (n c)")[:, bass.ds(col, 1)]).then_inc(S("idx"), 1)
                wait_alone(pool, S, "idx", T + 1)
                nc.gpsimd.indirect_dma_start(out=x[:], out_offset=None, in_=x_rows,
                                             in_offset=bass.IndirectOffsetOnAxis(ap=idx[:, 0:1], axis=0)).then_inc(S("gathered"), 16)
                scatter(T)

            def finish(last, b):
                wait_alone(pool, S, "turned", last)
                nc.gpsimd.indirect_dma_start(out=x[:], out_offset=None, in_=x_rows,
                                             in_offset=bass.IndirectOffsetOnAxis(ap=idx[:, 0:1], axis=0)).then_inc(S("gathered"), 16)
                for n in range(LAG):
                    scatter(last + n)
                pool.wait_ge(S("scattered"), (last + LAG) * 16)
                pool.wait_ge(S("gathered"), last * 16 + 16)

            over_experts(pool, tile, finish)

        @block.vector
        def _(dve):
            for k in range(SPLIT):
                dve.wait_ge(S("w_high"), k + 1)
                nc.vector.scalar_tensor_tensor(w_hl[:, 0, 1, piece(k)], w_stage[:, piece(k)], WS, w_hl[:, 0, 0, piece(k)],
                                               ALU.mult, ALU.subtract).then_inc(S("w_low"), 1)

            def split(n, b, k):
                dve.wait_ge(S("w_high"), n * SPLIT + SPLIT + k + 1)
                nc.vector.scalar_tensor_tensor(w_hl[:, 1 - b, 1, piece(k)], w_stage[:, piece(k)], WS, w_hl[:, 1 - b, 0, piece(k)],
                                               ALU.mult, ALU.subtract).then_inc(S("w_low"), 1)

            def sum_rows(T, b):
                dve.wait_ge(S("second"), T + 1)
                if gated:
                    dve.wait_ge(S("slot_w"), T + 1)
                    dve.wait_ge(S("scattered"), (T + LAG) * 16)
                    nc.vector.tensor_scalar(y[:], psY[:], slot_w[:, 0:1], 1.0 / (WS * WS), ALU.mult, ALU.mult).then_inc(S("y_sum"), 1)
                else:
                    nc.vector.scalar_tensor_tensor(y_sum[:], psY[:], 1.0 / WS, b2[:, b], ALU.mult, ALU.add).then_inc(S("y_sum"), 1)

            def weigh_rows(T):
                if not gated:
                    dve.wait_ge(S("slot_w"), T + 1)
                    dve.wait_ge(S("y_sum"), T + 1)
                    dve.wait_ge(S("scattered"), (T + LAG) * 16)
                    nc.vector.tensor_scalar(y[:], y_sum[:], slot_w[:, 0:1], None, ALU.mult).then_inc(S("y_out"), 1)
                nc.vector.tensor_copy(y_rows[:], slot_row[:]).then_inc(S("y"), 1)

            def turned(T):
                dve.wait_ge(S("xt_high"), T + 1)
                nc.vector.tensor_tensor(xt_hl[:, 1], psX[:], xt_hl[:, 0], ALU.subtract).then_inc(S("xt_low"), 1)

            def tile(T, n, lo, b, b_prev, phase):
                start = isinstance(T, int) and T == 0
                more = phase < 2 and not (isinstance(n, int) and n == NE - 1)
                col = column(T, n, lo)
                if start:
                    turned(0)
                def low(k):
                    part = slice(2 * k, 2 * k + 2)
                    dve.wait_ge(S("hid_high"), T * PARTS + k + 1)
                    nc.vector.tensor_tensor(hid_hl[:, 1, part], hidden[:, part], hid_hl[:, 0, part], ALU.subtract).then_inc(S("hid_low"), 1)

                def high(k):
                    part = slice(2 * k, 2 * k + 2)
                    dve.wait_ge(S("hid"), T * PARTS + k + 1)
                    wait(dve, S("second"), T)
                    nc.vector.tensor_copy(hid_hl[:, 0, part], hidden[:, part]).then_inc(S("hid_high"), 1)

                def next_slots():
                    if not start:
                        weigh_rows(T - 1)
                        dve.wait_ge(S("y"), T + LAG - 1)
                    nc.vector.tensor_copy(slot_row[:], plan.index[:].rearrange("p n c -> p (n c)")[:, bass.ds(col, 1)])
                    nc.vector.tensor_copy(slot_w[:], plan.weight[:].rearrange("p n c -> p (n c)")[:, bass.ds(col, 1)]).then_inc(S("slot_w"), 1)

                for k in range(PARTS):
                    part = slice(2 * k, 2 * k + 2)
                    if k == PARTS - 1:
                        turned(T + 1)
                    if gated:
                        dve.wait_ge(S("gate"), T * PARTS + k + 1)
                        wait(dve, S("hid_low"), (T - 1) * PARTS + k + 1 if not start else 0)
                        nc.vector.tensor_tensor(hidden[:, part], psH[k % NB][:, 1], gate[:, part], ALU.mult).then_inc(S("hid"), 1)
                    else:
                        if not more:
                            high(k)
                        low(k)
                        if k == 0 and not start:
                            sum_rows(T - 1, b_prev)
                        if k == 2:
                            next_slots()
                if gated:
                    if not start:
                        sum_rows(T - 1, b_prev)
                    for k in range(PARTS):
                        low(k)
                    next_slots()
                if more:
                    for k in range(PARTS):
                        split(n, b, phase * PARTS + k)

            def finish(last, b):
                sum_rows(last - 1, b)
                weigh_rows(last - 1)

            over_experts(dve, tile, finish)
def attention1_inputs(nc, ctx, io):
    NH, DK, DL, DR, TOP = 8, 128, 32, 32, 64
    CAT = 2 * DL + DR
    return Resident(nc, ctx, "a1", [
        ("uq_t", [DK, NH, DL + 1], F32, 0, io["uq_t"]),
        ("uk_t", [DK, NH, DL + 1], F32, 0, io["uk_t"]),
        ("uv_t", [DK, NH, DL], F32, 0, io["uv_t"]),
        ("wo", [DK, NH, D], F32, 0, io["wo1"]),
        ("buv", [DK, NH], F32, 0, io["buv"]),
        ("qr", [TOP + DL + 1, NH, DR], F32, TOP, io["qr"]),
        ("w_cat", [128, DC, CAT], F32, 0, io["w_cat"]),
        ("b_cat", [CAT, 1], F32, 0, io["b_cat"]),
        ("b_kv4", [128, 1], F32, 0, io["b_kv4"]),
        ("eye", [128, 128], F32, 0, io["eye_f"]),
        ("eye16", [128, 128], F16, 0, io["eye"]),
        ("bo_rows", [128, D], F32, 0, io["bo1"].broadcast_to([128, D])),
    ])


def build_attention1(nc, io, res, acc_rows, x3):
    NH, DK, DL, DR = 8, 128, 32, 32
    QK = DL + DR + 1
    CAT = 2 * DL + DR
    QS = 4.0
    TOP = 64
    with ExitStack() as ctx:
        def sb(name, shape, dt=F32):
            return ctx.enter_context(nc.sbuf_tensor("a1_" + name, shape, dt))

        def ps(name, shape, dt=F32):
            return ctx.enter_context(nc.psum_tensor("a1_" + name, shape, dt))

        S = Sems(nc, "a1")
        ctx.callback(S.clear)
        uq_t, uk_t, uv_t, wo, buv, bo_rows = (res[n] for n in ("uq_t", "uk_t", "uv_t", "wo", "buv", "bo_rows"))
        qr, w_cat, b_cat, b_kv4, eye, eye16 = (res[n] for n in ("qr", "w_cat", "b_cat", "b_kv4", "eye", "eye16"))
        buv_wide = sb("buv_wide", [DK, NH, 128])
        m_f = sb("m_f", [TOP + DL + 1, NH, QK])
        n_f = sb("n_f", [128, DC, D])
        out_bias = sb("out_bias", [128, D])
        half_power = sb("half_power", [128, 1])
        w_cat_hl = sb("w_cat_hl", [128, 2, DC, CAT], F16)
        m_hl = sb("m_hl", [TOP + DL + 1, 2, NH, QK], F16)
        n_hl = sb("n_hl", [128, 2, DC, D], F16)
        b_cat_ws = sb("b_cat_ws", [CAT, 1])
        b_kv_ws = sb("b_kv_ws", [128, 1])

        x = sb("x", [128, 4, D])
        stats = sb("stats", [128, 6])
        moments = sb("moments", [128, 2])
        var_eps = sb("var_eps", [128, 1])
        rstd = sb("rstd", [128, 1])
        shift = sb("shift", [128, 1])
        h2 = sb("h2", [128, 4, D])
        h2_bias = sb("h2_bias", [128, 4, D])
        ht_hl = sb("ht_hl", [128, 2, 2, DC, 128], F16)
        k_hl = sb("k_hl", [QK, 4, 2, PAIR], F16)
        c_hl = sb("c_hl", [TOP + DL + 1, 2, 2, PAIR], F16)
        v_hl = sb("v_hl", [128, 4, 2, DL], F16)
        LAST = NH - 3
        q_wide = sb("q_wide", [QK, 2, 2, 2, LAST * SEQ + 128], F16)
        q_hl = q_wide[:, :, :, :, 0:NH * SEQ].rearrange("r b a i (h q) -> r b a i h q", q=SEQ)
        row_max = sb("row_max", [TRIO, 6])
        row_sum = sb("row_sum", [TRIO, 6])
        row_inv = sb("row_inv", [TRIO, 6])
        prob = sb("prob", [TRIO, 2, 3, 2, SEQ])
        p_hl = sb("p_hl", [TRIO, 2, 2, 3, 2, SLOT], F16)
        pt_hl = sb("pt_hl", [128, 2, NH, SEQ], F16)
        ctx_hl = sb("ctx_hl", [128, 2, DC, 2, SLOT], F16)
        r = sb("r", [128, D])
        stats2 = sb("stats2", [128, 6])
        moments2 = sb("moments2", [128, 2])
        var_eps2 = sb("var_eps2", [128, 1])
        rstd2 = sb("rstd2", [128, 1])
        shift2 = sb("shift2", [128, 1])
        h3 = sb("h3", [128, 2, D])

        psX = ps("psX", [128, DC, 128])
        psCV = ps("psCV", [128, PAIR + DL])
        psC = psCV[0:CAT, 0:PAIR]
        psV = psCV[:, PAIR:]
        psO = ps("psO", [128, 512])
        psQ = [ps("psQ0", [QK, 2, NH // 2, SEQ]), ps("psQ1", [QK, 2, NH // 2, SEQ])]
        psS = ps("psS", [128, 512])
        scored = psS[0:TRIO, 0:6 * SEQ].rearrange("r (n k) -> r n k", n=6)
        psT = ps("psT", [128, 2, 3, 112], F16)
        psM = ps("psM", [128, 512])
        psA = [t[:, 0:DC * SEQ].rearrange("p (c q) -> p c q", c=DC) for t in (psM[:], psX[:].rearrange("p c n -> p (c n)"))]

        run = lambda eng, body: run_steps(eng, PAIRS, 7, body)
        block = ctx.enter_context(nc.Block())

        @block.sync
        def _(sp):
            sp.dma_start(x3[TOKENS:ROWS, :], io["zero_rows"]).then_inc(S("dummy_out"), 16)
            sp.wait_ge(S("zeroed"), 5)

            def step(st):
                if st.active(0):
                    p, b, hp, b4 = st.item(0)
                    wait(sp, S("h2"), p - 3)
                    for i in range(2):
                        sp.dma_start(x[i * SLOT:i * SLOT + SEQ, b4], acc_rows[bass.ds(p * PAIR + i * SEQ, SEQ), :]).then_inc(S(f"x_in{b4}"), 16)
                if st.active(7):
                    p, b, hp, _ = st.item(7)
                    wait(sp, S("h3"), p + 1)
                    for i in range(2):
                        sp.dma_start(x3[bass.ds(p * PAIR + i * SEQ, SEQ), :], h3[i * SLOT:i * SLOT + SEQ, b]).then_inc(S(f"h3_out{b}"), 16)

            run(sp, step)
            sp.wait_ge(S("dummy_out"), 16)
            for b in range(2):
                sp.wait_ge(S(f"h3_out{b}"), 32 * (PAIRS // 2))

        @block.tensor
        def _(pe):
            def products(out, left, right, chunks):
                todo = [(a, b, c) for c in range(chunks) for a, b in ((0, 0), (0, 1), (1, 0))]
                for n, (a, b, c) in enumerate(todo):
                    ins = nc.tensor.matmul(out, left(a, c), right(b, c), start=n == 0, stop=n == len(todo) - 1)
                return ins

            pe.wait_ge(S("buv_wide"), 1)
            for h in range(NH):
                ins = nc.tensor.matmul(psO[TOP:TOP + DL + 1, (DL + 1) * h:(DL + 1) * (h + 1)], uq_t[:, h], uk_t[:, h], start=True, stop=True)
            ins.then_inc(S("joined"), 1)
            for h in range(NH):
                ins = nc.tensor.matmul((psM, psS)[h // 4][32 * (h % 4):32 * (h % 4) + 32, 0:D], uv_t[:, h], wo[:, h], start=True, stop=True)
            ins.then_inc(S("joined"), 1)
            for h in range(NH):
                ins = nc.tensor.matmul(psX[:].rearrange("p c n -> p (c n)"), buv_wide[:, h], wo[:, h], start=h == 0, stop=h == NH - 1)
            ins.then_inc(S("joined"), 1)
            pe.wait_ge(S("w_ready"), 6)
            pe.wait_ge(S("ones"), 4)
            pe.wait_ge(S("zeroed"), 5)

            def turn(st):
                p, b, _, b4 = st.item(2)
                pe.wait_ge(S("h2"), p + 1)
                wait(pe, S("ht_low"), p)
                wait(pe, S("ctx_low"), 2 * (p - 3))
                for c in range(DC):
                    ins = nc.tensor.transpose(psX[:, c], h2[:, b4, c * 128:(c + 1) * 128], eye[:])
                ins.then_inc(S("turned"), 1)

            def latents(st):
                p, b, _, _ = st.item(2)
                pe.wait_ge(S("ht_high"), p + 1)
                pe.wait_ge(S("ht_low"), p + 1)
                wait(pe, S("latent_low"), p)
                by_image = lambda a, c: ht_hl[:, b, a, c].rearrange("p (i q) -> p i q", i=2)[:, :, 0:SEQ]
                products(psC.rearrange("p (i q) -> p i q", i=2), lambda a, c: w_cat_hl[:, a, c], by_image, DC)
                products(psV, lambda a, c: ht_hl[:, b, a, c], lambda a, c: w_cat_hl[:, a, c, 0:DL], DC).then_inc(S("latent"), 1)

            def queries(st):
                p, b, _, _ = st.item(3)
                pe.wait_ge(S("latent_high"), p + 1)
                pe.wait_ge(S("latent_low"), p + 1)
                wait(pe, S("q_low"), 2 * p)
                for h in range(NH):
                    ins = products(psQ[h // 4][:, :, h % 4], lambda a, c: m_hl[TOP:TOP + DL + 1, a, h],
                                   lambda a, c: c_hl[TOP:TOP + DL + 1, b, a].rearrange("r (i q) -> r i q", i=2), 1)
                    if h % 4 == 3:
                        ins.then_inc(S("q"), 1)

            def scores(st):
                p, b, _, b4 = st.item(4)
                pe.wait_ge(S("q_high"), 2 * p + 2)
                pe.wait_ge(S("q_low"), 2 * p + 2)
                wait(pe, S("shifted"), p)
                for t in range(3):
                    at = min(3 * t, LAST) * SEQ
                    for i in range(2):
                        ins = products(psS[:, (2 * t + i) * SEQ:(2 * t + i + 1) * SEQ], lambda a, c: q_wide[:, b, a, i, at:at + 128],
                                       lambda a, c: k_hl[:, b4, a, i * SEQ:(i + 1) * SEQ], 1)
                ins.then_inc(S("scored"), 1)

            def transpose_probs(st):
                p, b, _, _ = st.item(5)
                pe.wait_ge(S("p_high"), p + 1)
                pe.wait_ge(S("p_low"), p + 1)
                wait(pe, S("pt_copied"), 2 * p)
                for a in range(2):
                    for t in range(3):
                        ins = nc.tensor.transpose(psT[:, a, t, 0:TRIO], p_hl[:, b, a, t].rearrange("r i k -> r (i k)"), eye16[0:TRIO, 0:TRIO])
                ins.then_inc(S("pt"), 1)

            def mix(st):
                p, b, _, b4 = st.item(5)
                pe.wait_ge(S("pt_copied"), 2 * p + 2)
                wait(pe, S("ctx_low"), 2 * p)
                wait_alone(pe, S, "ht_low", min(p + 4, PAIRS) if isinstance(p, int) else p + 4)
                for i in range(2):
                    rows = slice(i * SLOT, i * SLOT + SEQ)
                    for h in range(NH):
                        j, c = h % 4, h // 4
                        for n, (a, z) in enumerate(((0, 0), (0, 1), (1, 0))):
                            ins = nc.tensor.matmul(psA[i][32 * j:32 * j + 32, c], v_hl[rows, b4, z], pt_hl[rows, a, h],
                                                   start=n == 0, stop=n == 2)
                    ins.then_inc(S("mixed"), 1)

            def output(st):
                p, b, _, _ = st.item(6)
                pe.wait_ge(S("ctx_high"), 2 * p + 2)
                pe.wait_ge(S("ctx_low"), 2 * p + 2)
                wait(pe, S("r"), p)
                products(psO[:, 0:D], lambda a, c: ctx_hl[:, a, c], lambda a, c: n_hl[:, a, c], DC).then_inc(S("projected"), 1)

            def step(st):
                if st.active(4):
                    scores(st)
                if st.active(6):
                    output(st)
                if st.active(2):
                    turn(st)
                if st.active(5):
                    transpose_probs(st)
                if st.active(3):
                    queries(st)
                if st.active(5):
                    mix(st)
                if st.active(2):
                    latents(st)

            run(pe, step)

        @block.scalar
        def _(act):
            nc.scalar.activation(w_cat_hl[:, 0], w_cat[:], ACT.Copy, scale=WS).then_inc(S("w_high"), 1)
            act.wait_ge(S("m_ready"), 2)
            nc.scalar.activation(m_hl[TOP:TOP + DL + 1, 0], m_f[TOP:TOP + DL + 1], ACT.Copy, scale=16.0).then_inc(S("w_high"), 1)
            act.wait_ge(S("n_ready"), 2)
            nc.scalar.activation(n_hl[:, 0], n_f[:], ACT.Copy, scale=WS).then_inc(S("w_high"), 1)

            def step(st):
                if st.active(6):
                    p, b, _, _ = st.item(6)
                    wait(act, S("projected"), p)
                    for i in range(2):
                        act.wait_ge(S("mixed"), 2 * p + 1 + i)
                        nc.scalar.activation(ctx_hl[:, 0, :, i, 0:SEQ], psA[i], ACT.Identity, bias=b_kv_ws[:, 0:1]).then_inc(S("ctx_high"), 1)
                if st.active(3):
                    p, b, _, b4 = st.item(3)
                    act.wait_ge(S("latent"), p + 1)
                    wait(act, S("scored"), p - 3)
                    wait(act, S("q"), 2 * (p - 1))
                    wait(act, S("mixed"), 2 * (p - 3))
                    nc.scalar.activation(k_hl[0:TOP, b4, 0], psC[0:TOP], ACT.Identity, bias=b_cat_ws[0:TOP, 0:1])
                    nc.scalar.activation(c_hl[TOP:CAT, b, 0], psC[TOP:CAT], ACT.Identity, bias=b_cat_ws[TOP:CAT, 0:1])
                    nc.scalar.activation(v_hl[:, b4, 0], psV, ACT.Copy).then_inc(S("latent_high"), 1)
                if st.active(1):
                    p, b, _, b4 = st.item(1)
                    act.wait_ge(S("shift"), p + 1)
                    wait(act, S("turned"), p - 3)
                    wait(act, S("h2_bias"), p - 3)
                    nc.scalar.activation(h2[:, b4], x[:, b4], ACT.Identity, scale=rstd[:, 0:1], bias=shift[:, 0:1]).then_inc(S("h2"), 1)
                if st.active(7):
                    p, b, hp, _ = st.item(7)
                    act.wait_ge(S("shift2"), p + 1)
                    wait(act, S(f"h3_out{b}"), 32 * hp)
                    nc.scalar.activation(h3[:, b], r[:], ACT.Identity, scale=rstd2[:, 0:1], bias=shift2[:, 0:1]).then_inc(S("h3"), 1)
                if st.active(4):
                    p, b, _, _ = st.item(4)
                    act.wait_ge(S("shifted"), p + 1)
                    nc.scalar.activation(prob[:, b], prob[:, b], ACT.Exp, scale=1.0 / (QS * WS * (DK + DR) ** 0.5)).then_inc(S("exp"), 1)
                if st.active(2):
                    p, b, _, b4 = st.item(2)
                    act.wait_ge(S("turned"), p + 1)
                    wait(act, S("latent"), p - 1)
                    nc.scalar.activation(ht_hl[:, b, 0], psX[:], ACT.Copy).then_inc(S("ht_high"), 1)
                if st.active(5):
                    p, b, _, _ = st.item(5)
                    act.wait_ge(S("pt"), p + 1)
                    wait(act, S("mixed"), 2 * p)
                    nc.scalar.activation(pt_hl[:, :, 0:6].rearrange("k a (t h) q -> k a t (h q)", t=2), psT[:, :, 0:2, 0:TRIO], ACT.Copy).then_inc(S("pt_copied"), 1)
                    nc.scalar.activation(pt_hl[:, :, 6:8].rearrange("k a h q -> k a (h q)"), psT[:, :, 2, SEQ:TRIO], ACT.Copy).then_inc(S("pt_copied"), 1)
                if st.active(3):
                    p, b, _, _ = st.item(3)
                    wait(act, S("scored"), p - 1)
                    for g in range(2):
                        act.wait_ge(S("q"), 2 * p + g + 1)
                        nc.scalar.activation(q_hl[:, b, 0, :, 4 * g:4 * g + 4], psQ[g][:], ACT.Copy, scale=QS / (16.0 * WS)).then_inc(S("q_high"), 1)
                if st.active(4):
                    p, b, _, _ = st.item(4)
                    act.wait_ge(S("prob"), p + 1)
                    wait(act, S("pt"), p - 1)
                    nc.scalar.activation(p_hl[:, b, 0, :, :, 0:SEQ], prob[:, b], ACT.Copy).then_inc(S("p_high"), 1)

            run(act, step)

        @block.gpsimd
        def _(pool):
            for t, v in ((p_hl, 0.0), (ctx_hl, 0.0), (x, 0.0), (half_power, -0.5), (q_wide, 0.0)):
                nc.gpsimd.memset(t[:], v).then_inc(S("zeroed"), 1)
            pool.wait_ge(S("zeroed"), 5)

            def step(st):
                if st.active(4):
                    p, b, _, b4 = st.item(4)
                    wait(pool, S("r"), p - 3)
                    pool.wait_ge(S("h2"), p + 1)
                    if isinstance(p, int) and p == 0:
                        pool.wait_ge(S("w_ready"), 6)
                    nc.gpsimd.tensor_tensor(h2_bias[:, b4], h2[:, b4], out_bias[:], ALU.add).then_inc(S("h2_bias"), 1)
                if st.active(6):
                    p, b, _, _ = st.item(6)
                    pool.wait_ge(S("var_eps2"), p + 1)
                    wait(pool, S("h3"), p)
                    nc.gpsimd.tensor_tensor(rstd2[:], var_eps2[:], half_power[:], ALU.pow).then_inc(S("rstd2"), 1)
                if st.active(0):
                    p, b, _, b4 = st.item(0)
                    pool.wait_ge(S("var_eps"), p + 1)
                    wait(pool, S("h2"), p)
                    nc.gpsimd.tensor_tensor(rstd[:], var_eps[:], half_power[:], ALU.pow).then_inc(S("rstd"), 1)
                if st.active(4):
                    p, b, _, _ = st.item(4)
                    pool.wait_ge(S("p_high"), p + 1)
                    nc.gpsimd.tensor_tensor(p_hl[:, b, 1, :, :, 0:SEQ], prob[:, b], p_hl[:, b, 0, :, :, 0:SEQ], ALU.subtract).then_inc(S("p_low"), 1)

            run(pool, step)

        @block.vector
        def _(dve):
            hl = lambda t, a: t[:, a].rearrange("p c n -> p (c n)")
            rows = slice(TOP, TOP + DL + 1)
            nc.vector.memset(k_hl[TOP:TOP + 1, :, 1], 0.0).then_inc(S("ones"), 1)
            nc.vector.memset(k_hl[TOP:TOP + 1, :, 0], WS).then_inc(S("ones"), 1)
            nc.vector.memset(c_hl[CAT:CAT + 1, :, 1], 0.0).then_inc(S("ones"), 1)
            nc.vector.memset(c_hl[CAT:CAT + 1, :, 0], WS).then_inc(S("ones"), 1)
            nc.vector.tensor_copy(buv_wide[:], buv[:].unsqueeze(2).broadcast_to([DK, NH, 128])).then_inc(S("buv_wide"), 1)
            dve.wait_ge(S("w_high"), 1)
            nc.vector.scalar_tensor_tensor(hl(w_cat_hl, 1), w_cat[:].rearrange("p c n -> p (c n)"), WS, hl(w_cat_hl, 0), ALU.mult, ALU.subtract).then_inc(S("w_ready"), 1)
            nc.vector.tensor_scalar(b_cat_ws[:], b_cat[:], WS, None, ALU.mult).then_inc(S("w_ready"), 1)
            nc.vector.tensor_scalar(b_kv_ws[:], b_kv4[:], WS, None, ALU.mult).then_inc(S("w_ready"), 1)
            dve.wait_ge(S("joined"), 1)
            joined = psO[rows, 0:NH * (DL + 1)].rearrange("r (h n) -> r h n", h=NH)
            nc.vector.tensor_copy(m_f[rows, :, 0:DL], joined[:, :, 0:DL])
            nc.vector.tensor_copy(m_f[rows, :, QK - 1:QK], joined[:, :, DL:DL + 1]).then_inc(S("m_ready"), 1)
            nc.vector.tensor_copy(m_f[rows, :, DL:DL + DR], qr[rows]).then_inc(S("m_ready"), 1)
            dve.wait_ge(S("joined"), 3)
            nc.vector.tensor_copy(n_f[:, 0], psM[:, 0:D]).then_inc(S("n_ready"), 1)
            nc.vector.tensor_copy(n_f[:, 1], psS[:, 0:D]).then_inc(S("n_ready"), 1)
            nc.vector.tensor_tensor(out_bias[:], psX[:].rearrange("p c n -> p (c n)"), bo_rows[:], ALU.add).then_inc(S("w_ready"), 1)
            dve.wait_ge(S("w_high"), 3)
            dve.wait_ge(S("m_ready"), 2)
            dve.wait_ge(S("n_ready"), 2)
            nc.vector.scalar_tensor_tensor(m_hl[rows, 1].rearrange("r h n -> r (h n)"), m_f[rows].rearrange("r h n -> r (h n)"), 16.0,
                                           m_hl[rows, 0].rearrange("r h n -> r (h n)"), ALU.mult, ALU.subtract).then_inc(S("w_ready"), 1)
            nc.vector.scalar_tensor_tensor(hl(n_hl, 1), n_f[:].rearrange("p c n -> p (c n)"), WS, hl(n_hl, 0), ALU.mult, ALU.subtract).then_inc(S("w_ready"), 1)

            def step(st):
                if st.active(6):
                    p, b, _, _ = st.item(6)
                    for i in range(2):
                        dve.wait_ge(S("ctx_high"), 2 * p + 1 + i)
                        nc.vector.scalar_tensor_tensor(ctx_hl[:, 1, :, i, 0:SEQ], psA[i], b_kv_ws[:, 0:1], ctx_hl[:, 0, :, i, 0:SEQ],
                                                       ALU.add, ALU.subtract).then_inc(S("ctx_low"), 1)
                if st.active(3):
                    p, b, _, b4 = st.item(3)
                    dve.wait_ge(S("latent_high"), p + 1)
                    nc.vector.scalar_tensor_tensor(k_hl[0:TOP, b4, 1], psC[0:TOP], b_cat_ws[0:TOP, 0:1], k_hl[0:TOP, b4, 0], ALU.add, ALU.subtract)
                    nc.vector.scalar_tensor_tensor(c_hl[TOP:CAT, b, 1], psC[TOP:CAT], b_cat_ws[TOP:CAT, 0:1], c_hl[TOP:CAT, b, 0], ALU.add, ALU.subtract)
                    nc.vector.tensor_tensor(v_hl[:, b4, 1], psV, v_hl[:, b4, 0], ALU.subtract).then_inc(S("latent_low"), 1)
                if st.active(1):
                    p, _, _, _ = st.item(1)
                    dve.wait_ge(S("rstd"), p + 1)
                    wait(dve, S("h2"), p)
                    nc.vector.scalar_tensor_tensor(shift[:], moments[:, 0:1], -1.0, rstd[:], ALU.mult, ALU.mult).then_inc(S("shift"), 1)
                if st.active(7):
                    p, _, _, _ = st.item(7)
                    dve.wait_ge(S("rstd2"), p + 1)
                    wait(dve, S("h3"), p)
                    nc.vector.scalar_tensor_tensor(shift2[:], moments2[:, 0:1], -1.0, rstd2[:], ALU.mult, ALU.mult).then_inc(S("shift2"), 1)
                if st.active(4):
                    p, b, _, _ = st.item(4)
                    dve.wait_ge(S("scored"), p + 1)
                    nc.vector.tensor_reduce(row_max[:], scored, AX.X, ALU.max).then_inc(S("row_max"), 1)
                    dve.wait_ge(S("row_max"), p + 1)
                    wait(dve, S("p_low"), p - 1)
                    nc.vector.tensor_tensor(prob[:, b].rearrange("r t i k -> r (t i) k"), scored, row_max[:].unsqueeze(2).broadcast_to([TRIO, 6, SEQ]), ALU.subtract).then_inc(S("shifted"), 1)
                if st.active(6):
                    p, b, hp, b4 = st.item(6)
                    dve.wait_ge(S("projected"), p + 1)
                    dve.wait_ge(S("h2_bias"), p + 1)
                    wait(dve, S("h3"), p)
                    nc.vector.scalar_tensor_tensor(r[:], psO[:, 0:D], 1.0 / (WS * WS), h2_bias[:, b4], ALU.mult, ALU.add).then_inc(S("r"), 1)
                if st.active(2):
                    p, b, _, b4 = st.item(2)
                    dve.wait_ge(S("ht_high"), p + 1)
                    nc.vector.tensor_tensor(ht_hl[:, b, 1], psX[:], ht_hl[:, b, 0], ALU.subtract).then_inc(S("ht_low"), 1)
                if st.active(6):
                    p, _, _, _ = st.item(6)
                    dve.wait_ge(S("r"), p + 1)
                    nc.vector.bn_stats(stats2[:], r[:]).then_inc(S("stats2"), 1)
                if st.active(4):
                    p, b, _, _ = st.item(4)
                    dve.wait_ge(S("exp"), p + 1)
                    nc.vector.tensor_reduce(row_sum[:], prob[:, b].rearrange("r t i k -> r (t i) k"), AX.X, ALU.add).then_inc(S("row_sum"), 1)
                if st.active(6):
                    p, _, _, _ = st.item(6)
                    wait_alone(dve, S, "stats2", p + 1)
                    wait_alone(dve, S, "shift2", p)
                    nc.vector.bn_aggr(moments2[:], stats2[:]).then_inc(S("moments2"), 1)
                if st.active(0):
                    p, _, _, b4 = st.item(0)
                    dve.wait_ge(S(f"x_in{b4}"), 32 * st.h + 32)
                    nc.vector.bn_stats(stats[:], x[:, b4]).then_inc(S("stats"), 1)
                if st.active(6):
                    p, _, _, _ = st.item(6)
                    dve.wait_ge(S("moments2"), p + 1)
                    nc.vector.tensor_scalar(var_eps2[:], moments2[:, 1:2], EPS, None, ALU.add).then_inc(S("var_eps2"), 1)
                if st.active(4):
                    p, _, _, _ = st.item(4)
                    dve.wait_ge(S("row_sum"), p + 1)
                    nc.vector.reciprocal(row_inv[:], row_sum[:]).then_inc(S("row_inv"), 1)
                if st.active(0):
                    p, _, _, _ = st.item(0)
                    wait_alone(dve, S, "stats", p + 1)
                    wait_alone(dve, S, "shift", p)
                    nc.vector.bn_aggr(moments[:], stats[:]).then_inc(S("moments"), 1)
                if st.active(4):
                    p, b, _, _ = st.item(4)
                    flat = prob[:, b].rearrange("r t i k -> r (t i) k")
                    dve.wait_ge(S("row_inv"), p + 1)
                    nc.vector.tensor_tensor(flat, flat, row_inv[:].unsqueeze(2).broadcast_to([TRIO, 6, SEQ]), ALU.mult).then_inc(S("prob"), 1)
                if st.active(0):
                    p, _, _, _ = st.item(0)
                    dve.wait_ge(S("moments"), p + 1)
                    nc.vector.tensor_scalar(var_eps[:], moments[:, 1:2], EPS, None, ALU.add).then_inc(S("var_eps"), 1)
                if st.active(3):
                    p, b, _, _ = st.item(3)
                    for g in range(2):
                        dve.wait_ge(S("q_high"), 2 * p + g + 1)
                        part = lambda a: q_hl[:, b, a, :, 4 * g:4 * g + 4].rearrange("r i h q -> r i (h q)")
                        nc.vector.scalar_tensor_tensor(part(1), psQ[g][:].rearrange("r i h q -> r i (h q)"), QS / (16.0 * WS), part(0),
                                                       ALU.mult, ALU.subtract).then_inc(S("q_low"), 1)

            run(dve, step)


def build_final_norm(nc, acc_rows, out_rows):
    NT = -(-TOKENS // 128)
    GROUP = 5
    groups = [range(g, min(g + GROUP, NT)) for g in range(0, NT, GROUP)]
    full = TOKENS // 128
    rest = TOKENS - full * 128
    with ExitStack() as ctx:
        def sb(name, shape):
            return ctx.enter_context(nc.sbuf_tensor("f_" + name, shape, F32))

        S = Sems(nc, "f")
        ctx.callback(S.clear)
        x = sb("x", [128, NT, D])
        y = sb("y", [128, NT, D])
        stats = sb("stats", [128, NT, 6])
        moments = sb("moments", [128, NT, 2])
        var_eps = sb("var_eps", [128, NT])
        rstd = sb("rstd", [128, NT])
        shift = sb("shift", [128, NT])
        half_power = sb("half_power", [128, GROUP])
        size = lambda t: 128 if t < full else rest
        on_act = lambda t: t % GROUP >= 2
        block = ctx.enter_context(nc.Block())

        def move(eng, g, rows, tiles, store, sem):
            parts = []
            whole = [t for t in groups[g] if t < full]
            if whole:
                lo, hi = whole[0], whole[-1] + 1
                parts.append((rows[lo * 128:hi * 128, :].rearrange("(t p) d -> p t d", p=128), tiles[:, lo:hi]))
            if full in groups[g]:
                parts.append((rows[full * 128:TOKENS, :], tiles[0:rest, full]))
            for dram, sbuf in parts:
                eng.dma_start(*((dram, sbuf) if store else (sbuf, dram))).then_inc(sem, 16)
            return len(parts)

        loads = {}

        @block.sync
        def _(sp):
            for g in range(len(groups)):
                loads[g] = move(sp, g, acc_rows, x, False, S(f"x_in{g}"))
            stores = 0
            for g, tiles in enumerate(groups):
                sp.wait_ge(S("y_act"), sum(on_act(t) for t in range(tiles[-1] + 1)))
                sp.wait_ge(S("y_dve"), sum(not on_act(t) for t in range(tiles[-1] + 1)))
                stores += move(sp, g, out_rows, y, True, S("y_out"))
            sp.wait_ge(S("y_out"), 16 * stores)

        @block.scalar
        def _(act):
            for g, tiles in enumerate(groups):
                act.wait_ge(S("shift"), g + 1)
                for t in tiles:
                    if on_act(t):
                        n = size(t)
                        nc.scalar.activation(y[0:n, t], x[0:n, t], ACT.Identity, scale=rstd[0:n, t:t + 1], bias=shift[0:n, t:t + 1]).then_inc(S("y_act"), 1)

        @block.gpsimd
        def _(pool):
            nc.gpsimd.memset(moments[:], 0.0).then_inc(S("moments_set"), 1)
            nc.gpsimd.memset(half_power[:], -0.5).then_inc(S("half_power"), 1)
            pool.wait_ge(S("half_power"), 1)
            for g, tiles in enumerate(groups):
                pool.wait_ge(S("var_eps"), g + 1)
                cols = slice(tiles[0], tiles[-1] + 1)
                nc.gpsimd.tensor_tensor(rstd[:, cols], var_eps[:, cols], half_power[:, 0:len(tiles)], ALU.pow).then_inc(S("rstd"), 1)

        @block.vector
        def _(dve):
            def scale(g):
                tiles = groups[g]
                cols = slice(tiles[0], tiles[-1] + 1)
                dve.wait_ge(S("rstd"), g + 1)
                nc.vector.scalar_tensor_tensor(shift[:, cols], moments[:, cols, 0], -1.0, rstd[:, cols], ALU.mult, ALU.mult).then_inc(S("shift"), 1)
                for t in tiles:
                    if not on_act(t):
                        n = size(t)
                        nc.vector.tensor_scalar(y[0:n, t], x[0:n, t], moments[0:n, t, 0:1], rstd[0:n, t:t + 1], ALU.subtract, ALU.mult).then_inc(S("y_dve"), 1)

            dve.wait_ge(S("moments_set"), 1)
            for g, tiles in enumerate(groups):
                dve.wait_ge(S(f"x_in{g}"), 16 * loads[g])
                for t in tiles:
                    nc.vector.bn_stats(stats[0:size(t), t], x[0:size(t), t]).then_inc(S("stats"), 1)
                if g >= 1:
                    scale(g - 1)
                dve.wait_ge(S("stats"), tiles[-1] + 1)
                for t in tiles:
                    nc.vector.bn_aggr(moments[0:size(t), t], stats[0:size(t), t]).then_inc(S("moments"), 1)
                dve.wait_ge(S("moments"), tiles[-1] + 1)
                cols = slice(tiles[0], tiles[-1] + 1)
                nc.vector.tensor_scalar(var_eps[:, cols], moments[:, cols, 1], EPS, None, ALU.add).then_inc(S("var_eps"), 1)
            scale(len(groups) - 1)


def build(nc, io, out):
    x1, sum0, x3, sum1 = (nc.dram_tensor(n, (ROWS, D), F32).ap() for n in ("x1", "sum0", "x3", "sum1"))
    with ExitStack() as whole:
        routing = routing_inputs(nc, whole, io)
        attention1 = attention1_inputs(nc, whole, io)
        build_attention0(nc, io, x1, routing)
        for layer, x, total in ((0, x1, sum0), (1, x3, sum1)):
            if layer == 1:
                build_attention1(nc, io, attention1, sum0, x3)
            with ExitStack() as ctx:
                plan = Plan(nc, ctx, layer, 1 if layer == 0 else 0)
                build_routing(nc, io, routing, x, total, plan, layer)
                build_experts(nc, io, routing, x, total, plan, layer, attention1 if layer == 0 else None)
    build_final_norm(nc, sum1, out)


def lay_out(x, **w):
    import numpy as np

    def feat(v):
        return np.ascontiguousarray(v.reshape(-1, 128).T)

    def rows(m):
        k, n = m.shape
        return np.ascontiguousarray(m.reshape(k // 128, 128, n).transpose(1, 0, 2))

    p = x.reshape(PAIRS, 2, 3, GRID, 16, GRID, 16).transpose(0, 2, 4, 6, 1, 3, 5)
    p = p.reshape(PAIRS, PC, 128, 2 * PATCHES).transpose(0, 2, 1, 3)
    part = np.arange(128)
    a = {
        "patches": p,
        "emb_w": rows(w["L0_tok_W"].T),
        "qkvo_w": np.stack([rows(w[f"L0_attn_W{z}"].T) for z in "qkvo"], axis=1),
        "bias0": np.stack([feat(w["L0_tok_b"])] + [feat(w[f"L0_attn_b{z}"]) for z in "qkv"], axis=1),
        "pos_t": w["L0_tok_pos_embed"][0].T.reshape(DC, 128, SEQ).transpose(1, 0, 2),
        "cls_t": feat(w["L0_tok_cls_token"][0, 0])[:, :, None],
        "bo": w["L0_attn_bo"][None],
        "head_mask": (part[:, None] // 16 == np.arange(8)[None]).astype(np.float32),
        "eye": np.eye(128, dtype=np.float16),
    }

    experts0 = [(w["L0_ffn_Wg_s"], w["L0_ffn_Wu_s"], w["L0_ffn_Wd_s"])]
    experts0 += [(w["L0_ffn_Wg"][e], w["L0_ffn_Wu"][e], w["L0_ffn_Wd"][e]) for e in range(TE)]
    tok = np.arange(TOK_TILES * 128).reshape(TOK_TILES, 128).T
    te = TOK_TILES * TE
    a |= {
        "experts0": np.stack([np.concatenate([rows(m.T).reshape(128, -1) for m in e], axis=1) for e in experts0]),
        "experts1": np.stack([np.concatenate([rows(w["L1_ffn_W1"][e]).reshape(128, -1), rows(w["L1_ffn_W2"][e]).reshape(128, -1)], axis=1)
                              for e in range(TE)]),
        "b1": np.stack([feat(w["L1_ffn_b1"][e]) for e in range(TE)]),
        "b2": w["L1_ffn_b2"][:, None, :],
        "wr0": rows(w["L0_ffn_Wr"].T),
        "wr1": rows(w["L1_ffn_Wr"]),
        "router_bias0": w["L0_ffn_rb"][None],
        "router_bias1": w["L1_ffn_br"][None],
        "eye_f": np.eye(128, dtype=np.float32),
        "below": np.triu(np.ones((128, 128), np.float16), 1),
        "lane": np.broadcast_to(np.arange(128, dtype=np.float16), (128, 128)),
        "place": np.broadcast_to(np.arange(TE, 0, -1, dtype=np.float32), (128, TE)),
        "valid": (tok < TOKENS).astype(np.float32),
        "all_index": tok.astype(np.int32),
        "tile_number": np.broadcast_to(np.repeat(np.arange(TOK_TILES), TE), (128, 1, te)).astype(np.float16),
        "lane_number": (part[:, None] + 1).astype(np.float32),
        "dummy_row": (TOKENS + 1 + part[:, None]).astype(np.float32),
        "steps": (128.0 * np.arange(1, TOK_TILES))[None].astype(np.float32),
    }
    heads = lambda m: m.reshape(m.shape[0], 8, -1)
    with_bias = lambda m, b: np.concatenate([m, b[None]], axis=0)
    a |= {
        "uq_t": heads(with_bias(w["L1_attn_W_UQ"], w["L1_attn_b_UQ"])).transpose(2, 1, 0),
        "uk_t": heads(with_bias(w["L1_attn_W_UK"], w["L1_attn_b_UK"])).transpose(2, 1, 0),
        "uv_t": heads(w["L1_attn_W_UV"]).transpose(2, 1, 0),
        "wo1": w["L1_attn_W_O"].reshape(8, 128, D).transpose(1, 0, 2),
        "buv": w["L1_attn_b_UV"].reshape(8, 128).T,
        "qr": heads(with_bias(w["L1_attn_W_QR"], w["L1_attn_b_QR"])),
        "w_cat": rows(np.concatenate([w["L1_attn_W_DKV"], w["L1_attn_W_KR"], w["L1_attn_W_DQ"]], axis=1)),
        "b_cat": np.concatenate([w["L1_attn_b_DKV"], w["L1_attn_b_KR"], w["L1_attn_b_DQ"]])[:, None],
        "b_kv4": np.tile(w["L1_attn_b_DKV"], 4)[:, None],
        "zero_rows": np.zeros((DUMMY, D), np.float32),
        "bo1": w["L1_attn_b_O"][None],
    }
    return {k: np.ascontiguousarray(v) for k, v in a.items()}


def kernel(**inputs):
    import numpy as np
    import concourse.bacc as bacc
    from concourse.bass_utils import run_bass_kernel_spmd

    arrays = lay_out(**{k: np.asarray(v) for k, v in inputs.items()})
    nc = bacc.Bacc("TRN2", target_bir_lowering=False, num_devices=1)
    io = {k: nc.dram_tensor(k, v.shape, mybir.dt.from_np(v.dtype), kind="ExternalInput").ap() for k, v in arrays.items()}
    out = nc.dram_tensor("out", (TOKENS, D), F32, kind="ExternalOutput").ap()
    build(nc, io, out)
    result = run_bass_kernel_spmd(nc, [arrays], core_ids=[0])
    return result.results[0]["out"].reshape(IMAGES, SEQ, D)
```
